# Optimizing a Trainium2 kernel written in Bass

```python
import numpy as np
import jax
import jax.numpy as jnp

def _softmax(x, axis=-1):
    return jax.nn.softmax(x, axis=axis)

def _gelu(x):
    return jax.nn.gelu(x, approximate=True)

def _silu(x):
    return jax.nn.silu(x)

def _sigmoid(x):
    return jax.nn.sigmoid(x)

def _layernorm(x, axis=-1, eps=1e-05):
    m = jnp.mean(x, axis=axis, keepdims=True)
    v = jnp.var(x, axis=axis, keepdims=True)
    return (x - m) / jnp.sqrt(v + eps)

def _scatter_add(tgt, idx, src, axis=0):
    return tgt.at[idx].add(src)

def _segment_sum(src, seg, n):
    return jax.ops.segment_sum(src, seg, n)
kernel_name = 'mk_gnn_ffn_d2_gnn_r32_912afb'

def setup_inputs(seed: int=0):
    np.random.seed(seed)
    _w = jnp.asarray

    def _rec_inputs():
        import jax
        import jax.numpy as jnp
        _gk = jax.random.key(seed)
        x = 0.0009128 + 1.001 * jax.random.normal(jax.random.fold_in(_gk, 1), (3125, 256), jnp.float32)
        src = jax.random.randint(jax.random.fold_in(_gk, 2), (50000,), 0, 3125, jnp.int32)
        dst = jnp.minimum((3125 * jax.random.uniform(jax.random.fold_in(_gk, 3), (50000,)) ** 2.0).astype(jnp.int32), 99999)
        _o = jnp.argsort(dst, stable=True)
        src = src[_o]
        dst = dst[_o]
        edge_attr_3 = -0.000563758 + 1.00031 * jax.random.normal(jax.random.fold_in(_gk, 12), (50000, 3), jnp.float32)
        return (x, src, dst, edge_attr_3)
    x, src, dst, edge_attr_3 = _rec_inputs()

    def _L0_gnn_setup():
        import jax, jax.numpy as jnp
        import numpy as np
        MUL = 64
        N_NODES = 10000
        N_EDGES = 10000
        DIM = MUL + 3 * MUL
        SQ3 = float(np.sqrt(3.0))
        INV_MUL = float(1.0 / np.sqrt(MUL))
        INV_TP = float(1.0 / np.sqrt(2 * MUL))

        def _split(f):
            return (f[:, :MUL], f[:, MUL:].reshape(f.shape[0], MUL, 3))

        def _lin(x0, x1, w0, w1):
            return (x0 @ w0 * INV_MUL, jnp.einsum('eum,uv->evm', x1, w1) * INV_MUL)

        def _fctp(x0, x1, sh1, w00, w11, w01, w10):
            dot = jnp.einsum('eum,em->eu', x1, sh1) / SQ3
            out0 = (x0 @ w00 + dot @ w11) * INV_TP
            out1 = (jnp.einsum('eu,uv->ev', x0, w01)[:, :, None] * sh1[:, None, :] + jnp.einsum('eum,uv->evm', x1, w10)) * INV_TP
            return (out0, out1)

        def _forward(atom_feature, edge_vector, weights, edge_index):
            ls0, ls1, ld0, ld1, t1_00, t1_11, t1_01, t1_10, t2_00, t2_11, t2_01, t2_10, lh0, lh1, lsc = weights
            src, dst = (edge_index[0], edge_index[1])
            r = edge_vector / (jnp.linalg.norm(edge_vector, axis=-1, keepdims=True) + 1e-12)
            sh1 = SQ3 * r
            x0, x1 = _split(atom_feature)
            s0, s1 = _lin(x0[src], x1[src], ls0, ls1)
            d0, d1 = _lin(x0[dst], x1[dst], ld0, ld1)
            h0, h1 = _fctp(s0, s1, sh1, t1_00, t1_11, t1_01, t1_10)
            h0, h1 = _lin(h0, h1, lh0, lh1)
            sc = jax.nn.leaky_relu(h0) @ lsc * INV_MUL
            full = jnp.concatenate([sc, jnp.zeros((sc.shape[0], 3 * MUL), sc.dtype)], axis=-1)
            act = jax.nn.softmax(full, axis=-1)
            o0, o1 = _fctp(h0, h1, sh1, t2_00, t2_11, t2_01, t2_10)
            tp2_flat = jnp.concatenate([o0, o1.reshape(o1.shape[0], 3 * MUL)], axis=-1)
            msgs = act * tp2_flat
            agg = jax.ops.segment_sum(msgs, dst, num_segments=atom_feature.shape[0])
            return atom_feature + agg
        _WNAMES = ['lin_src_w0', 'lin_src_w1', 'lin_dst_w0', 'lin_dst_w1', 'tp1_w00', 'tp1_w11', 'tp1_w01', 'tp1_w10', 'tp2_w00', 'tp2_w11', 'tp2_w01', 'tp2_w10', 'lin_hidden_w0', 'lin_hidden_w1', 'lin_scalar_w']
        key = jax.random.key(seed)
        ks = jax.random.split(key, 18)
        inp = {n: jax.random.normal(ks[i], (MUL, MUL), jnp.float32) for i, n in enumerate(_WNAMES)}
        inp['atom_feature'] = jax.random.normal(ks[15], (N_NODES, DIM), jnp.float32)
        inp['edge_vector'] = jax.random.normal(ks[16], (N_EDGES, 3), jnp.float32)
        inp['edge_index'] = jax.random.randint(ks[17], (2, N_EDGES), 0, N_NODES, dtype=jnp.int32)
        return inp
    _L0_gnn_all = _L0_gnn_setup()
    _L0_gnn_in = {k: v for k, v in _L0_gnn_all.items() if k in ('lin_src_w0', 'lin_src_w1', 'lin_dst_w0', 'lin_dst_w1', 'tp1_w00', 'tp1_w11', 'tp1_w01', 'tp1_w10', 'tp2_w00', 'tp2_w11', 'tp2_w01', 'tp2_w10', 'lin_hidden_w0', 'lin_hidden_w1', 'lin_scalar_w')}
    del _L0_gnn_all

    def _L0_ffn_setup():
        import jax, jax.numpy as jnp
        import numpy as np
        EPS = 1e-08
        key = jax.random.key(seed)
        kx, kw, kb = jax.random.split(key, 3)
        B, S, K, N = (64, 128, 256, 256)
        x = jax.random.normal(kx, (B, S, K), dtype=jnp.float32)
        bound_w = np.sqrt(6.0 / K) / np.sqrt(1.0 + 5.0)
        weight = jax.random.uniform(kw, (N, K), dtype=jnp.float32, minval=-bound_w, maxval=bound_w)
        bound_b = 1.0 / np.sqrt(K)
        bias = jax.random.uniform(kb, (N,), dtype=jnp.float32, minval=-bound_b, maxval=bound_b)
        return {'x': x, 'weight': weight, 'bias': bias}
    _L0_ffn_all = _L0_ffn_setup()
    _L0_ffn_in = {k: v for k, v in _L0_ffn_all.items() if k in ('weight', 'bias')}
    del _L0_ffn_all

    def _L1_gnn_setup():
        import jax, jax.numpy as jnp
        import numpy as np
        N_NODES = 50000
        N_EDGES = 25000
        DIM = 256
        HEADS = 8
        DIM_OUT = 32
        key = jax.random.key(seed)
        ks = jax.random.split(key, 9)
        s = 1.0 / np.sqrt(DIM)
        inner = HEADS * DIM_OUT
        return {'x': jax.random.normal(ks[0], (N_NODES, DIM), dtype=jnp.float32), 'Wq': jax.random.uniform(ks[1], (DIM, inner), jnp.float32, -s, s), 'bq': jax.random.uniform(ks[2], (inner,), jnp.float32, -s, s), 'Wk': jax.random.uniform(ks[3], (DIM, inner), jnp.float32, -s, s), 'bk': jax.random.uniform(ks[4], (inner,), jnp.float32, -s, s), 'Wv': jax.random.uniform(ks[5], (DIM, inner), jnp.float32, -s, s), 'bv': jax.random.uniform(ks[6], (inner,), jnp.float32, -s, s), 'src': jax.random.randint(ks[7], (N_EDGES,), 0, N_NODES), 'dst': jax.random.randint(ks[8], (N_EDGES,), 0, N_NODES)}
    _L1_gnn_all = _L1_gnn_setup()
    _L1_gnn_in = {k: v for k, v in _L1_gnn_all.items() if k in ('Wq', 'bq', 'Wk', 'bk', 'Wv', 'bv')}
    del _L1_gnn_all

    def _L1_ffn_setup():
        import jax, jax.numpy as jnp
        import numpy as np
        E = 8
        K = 2
        D = 256
        H = 512
        DOUT = 256
        EPS = 1e-05
        key = jax.random.key(seed)
        ks = jax.random.split(key, 9)
        s = 0.02
        return {'x': jax.random.normal(ks[0], (4, 256, D), jnp.float32), 'gamma': 1.0 + 0.05 * jax.random.normal(ks[1], (D,), jnp.float32), 'beta': 0.05 * jax.random.normal(ks[2], (D,), jnp.float32), 'Wr': 0.01 * jax.random.normal(ks[3], (D, E), jnp.float32), 'br': jnp.zeros((E,), jnp.float32), 'W1': s * jax.random.normal(ks[4], (E, D, H), jnp.float32), 'b1': s * jax.random.normal(ks[5], (E, H), jnp.float32), 'W2': s * jax.random.normal(ks[6], (E, H, DOUT), jnp.float32), 'b2': s * jax.random.normal(ks[7], (E, DOUT), jnp.float32)}
    _L1_ffn_all = _L1_ffn_setup()
    _L1_ffn_in = {k: v for k, v in _L1_ffn_all.items() if k in ('gamma', 'beta', 'Wr', 'br', 'W1', 'b1', 'W2', 'b2')}
    del _L1_ffn_all
    return {'x': x, 'src': src, 'dst': dst, 'edge_attr_3': edge_attr_3, 'L0_gnn_lin_src_w0': _L0_gnn_in['lin_src_w0'], 'L0_gnn_lin_src_w1': _L0_gnn_in['lin_src_w1'], 'L0_gnn_lin_dst_w0': _L0_gnn_in['lin_dst_w0'], 'L0_gnn_lin_dst_w1': _L0_gnn_in['lin_dst_w1'], 'L0_gnn_tp1_w00': _L0_gnn_in['tp1_w00'], 'L0_gnn_tp1_w11': _L0_gnn_in['tp1_w11'], 'L0_gnn_tp1_w01': _L0_gnn_in['tp1_w01'], 'L0_gnn_tp1_w10': _L0_gnn_in['tp1_w10'], 'L0_gnn_tp2_w00': _L0_gnn_in['tp2_w00'], 'L0_gnn_tp2_w11': _L0_gnn_in['tp2_w11'], 'L0_gnn_tp2_w01': _L0_gnn_in['tp2_w01'], 'L0_gnn_tp2_w10': _L0_gnn_in['tp2_w10'], 'L0_gnn_lin_hidden_w0': _L0_gnn_in['lin_hidden_w0'], 'L0_gnn_lin_hidden_w1': _L0_gnn_in['lin_hidden_w1'], 'L0_gnn_lin_scalar_w': _L0_gnn_in['lin_scalar_w'], 'L0_ffn_weight': _L0_ffn_in['weight'], 'L0_ffn_bias': _L0_ffn_in['bias'], 'L1_gnn_Wq': _L1_gnn_in['Wq'], 'L1_gnn_bq': _L1_gnn_in['bq'], 'L1_gnn_Wk': _L1_gnn_in['Wk'], 'L1_gnn_bk': _L1_gnn_in['bk'], 'L1_gnn_Wv': _L1_gnn_in['Wv'], 'L1_gnn_bv': _L1_gnn_in['bv'], 'L1_ffn_gamma': _L1_ffn_in['gamma'], 'L1_ffn_beta': _L1_ffn_in['beta'], 'L1_ffn_Wr': _L1_ffn_in['Wr'], 'L1_ffn_br': _L1_ffn_in['br'], 'L1_ffn_W1': _L1_ffn_in['W1'], 'L1_ffn_b1': _L1_ffn_in['b1'], 'L1_ffn_W2': _L1_ffn_in['W2'], 'L1_ffn_b2': _L1_ffn_in['b2']}

def reference(x, src, dst, edge_attr_3, L0_gnn_lin_src_w0, L0_gnn_lin_src_w1, L0_gnn_lin_dst_w0, L0_gnn_lin_dst_w1, L0_gnn_tp1_w00, L0_gnn_tp1_w11, L0_gnn_tp1_w01, L0_gnn_tp1_w10, L0_gnn_tp2_w00, L0_gnn_tp2_w11, L0_gnn_tp2_w01, L0_gnn_tp2_w10, L0_gnn_lin_hidden_w0, L0_gnn_lin_hidden_w1, L0_gnn_lin_scalar_w, L0_ffn_weight, L0_ffn_bias, L1_gnn_Wq, L1_gnn_bq, L1_gnn_Wk, L1_gnn_bk, L1_gnn_Wv, L1_gnn_bv, L1_ffn_gamma, L1_ffn_beta, L1_ffn_Wr, L1_ffn_br, L1_ffn_W1, L1_ffn_b1, L1_ffn_W2, L1_ffn_b2):
    import jax
    import jax.numpy as jnp

    def _L0_gnn_ref(atom_feature, edge_vector, lin_src_w0, lin_src_w1, lin_dst_w0, lin_dst_w1, tp1_w00, tp1_w11, tp1_w01, tp1_w10, tp2_w00, tp2_w11, tp2_w01, tp2_w10, lin_hidden_w0, lin_hidden_w1, lin_scalar_w, edge_index):
        import jax, jax.numpy as jnp
        import numpy as np
        MUL = 64
        N_NODES = 10000
        N_EDGES = 10000
        DIM = MUL + 3 * MUL
        SQ3 = float(np.sqrt(3.0))
        INV_MUL = float(1.0 / np.sqrt(MUL))
        INV_TP = float(1.0 / np.sqrt(2 * MUL))

        def _split(f):
            return (f[:, :MUL], f[:, MUL:].reshape(f.shape[0], MUL, 3))

        def _lin(x0, x1, w0, w1):
            return (x0 @ w0 * INV_MUL, jnp.einsum('eum,uv->evm', x1, w1) * INV_MUL)

        def _fctp(x0, x1, sh1, w00, w11, w01, w10):
            dot = jnp.einsum('eum,em->eu', x1, sh1) / SQ3
            out0 = (x0 @ w00 + dot @ w11) * INV_TP
            out1 = (jnp.einsum('eu,uv->ev', x0, w01)[:, :, None] * sh1[:, None, :] + jnp.einsum('eum,uv->evm', x1, w10)) * INV_TP
            return (out0, out1)

        def _forward(atom_feature, edge_vector, weights, edge_index):
            ls0, ls1, ld0, ld1, t1_00, t1_11, t1_01, t1_10, t2_00, t2_11, t2_01, t2_10, lh0, lh1, lsc = weights
            src, dst = (edge_index[0], edge_index[1])
            r = edge_vector / (jnp.linalg.norm(edge_vector, axis=-1, keepdims=True) + 1e-12)
            sh1 = SQ3 * r
            x0, x1 = _split(atom_feature)
            s0, s1 = _lin(x0[src], x1[src], ls0, ls1)
            d0, d1 = _lin(x0[dst], x1[dst], ld0, ld1)
            h0, h1 = _fctp(s0, s1, sh1, t1_00, t1_11, t1_01, t1_10)
            h0, h1 = _lin(h0, h1, lh0, lh1)
            sc = jax.nn.leaky_relu(h0) @ lsc * INV_MUL
            full = jnp.concatenate([sc, jnp.zeros((sc.shape[0], 3 * MUL), sc.dtype)], axis=-1)
            act = jax.nn.softmax(full, axis=-1)
            o0, o1 = _fctp(h0, h1, sh1, t2_00, t2_11, t2_01, t2_10)
            tp2_flat = jnp.concatenate([o0, o1.reshape(o1.shape[0], 3 * MUL)], axis=-1)
            msgs = act * tp2_flat
            agg = jax.ops.segment_sum(msgs, dst, num_segments=atom_feature.shape[0])
            return atom_feature + agg
        _WNAMES = ['lin_src_w0', 'lin_src_w1', 'lin_dst_w0', 'lin_dst_w1', 'tp1_w00', 'tp1_w11', 'tp1_w01', 'tp1_w10', 'tp2_w00', 'tp2_w11', 'tp2_w01', 'tp2_w10', 'lin_hidden_w0', 'lin_hidden_w1', 'lin_scalar_w']
        weights = (lin_src_w0, lin_src_w1, lin_dst_w0, lin_dst_w1, tp1_w00, tp1_w11, tp1_w01, tp1_w10, tp2_w00, tp2_w11, tp2_w01, tp2_w10, lin_hidden_w0, lin_hidden_w1, lin_scalar_w)
        return _forward(atom_feature, edge_vector, weights, edge_index)

    def _L0_ffn_ref(x, weight, bias):
        import jax, jax.numpy as jnp
        import numpy as np
        EPS = 1e-08
        'LNS inference path of LNSLinear.\n\n            log_out[m, n] = logsumexp_k(log(|x[m,k]|+eps) + log(|w[n,k]|+eps))\n            out = sign(sign(x) @ sign(w).T) * exp(log_out) + bias\n            Computed stably as log(exp(lx - mx) @ exp(lw - mw).T) + mx + mw.\n            '
        orig_shape = x.shape
        K = weight.shape[1]
        xf = x.reshape(-1, K)
        log_x = jnp.log(jnp.abs(xf) + EPS)
        x_sign = jnp.sign(xf)
        log_w = jnp.log(jnp.abs(weight) + EPS)
        w_sign = jnp.sign(weight)
        mx = jnp.max(log_x, axis=-1, keepdims=True)
        mw = jnp.max(log_w, axis=-1, keepdims=True)
        acc = jnp.einsum('mk,nk->mn', jnp.exp(log_x - mx), jnp.exp(log_w - mw))
        log_out = jnp.log(acc) + mx + mw.T
        out_sign = jnp.sign(jnp.einsum('mk,nk->mn', x_sign, w_sign))
        out = out_sign * jnp.exp(log_out) + bias
        return out.reshape(orig_shape[:-1] + (weight.shape[0],))

    def _L1_gnn_ref(x, Wq, bq, Wk, bk, Wv, bv, src, dst):
        import jax, jax.numpy as jnp
        import numpy as np
        N_NODES = 50000
        N_EDGES = 25000
        DIM = 256
        HEADS = 8
        DIM_OUT = 32
        n = x.shape[0]
        q = (x @ Wq + bq).reshape(n, HEADS, DIM_OUT)
        k = (x @ Wk + bk).reshape(n, HEADS, DIM_OUT)
        v = (x @ Wv + bv).reshape(n, HEADS, DIM_OUT)
        scores = jnp.einsum('ehd,ehd->eh', q[src], k[dst]) / jnp.sqrt(jnp.asarray(DIM_OUT, dtype=x.dtype))
        m = jax.ops.segment_max(scores, dst, num_segments=n)
        m = jnp.where(jnp.isfinite(m), m, 0.0)
        e = jnp.exp(scores - m[dst])
        z = jax.ops.segment_sum(e, dst, num_segments=n)
        p = e / jnp.maximum(z[dst], 1e-16)
        out = jax.ops.segment_sum(v[src] * p[:, :, None], dst, num_segments=n)
        return out.reshape(n, HEADS * DIM_OUT)

    def _L1_ffn_ref(x, gamma, beta, Wr, br, W1, b1, W2, b2):
        import jax, jax.numpy as jnp
        import numpy as np
        E = 8
        K = 2
        D = 256
        H = 512
        DOUT = 256
        EPS = 1e-05
        mu = jnp.mean(x, axis=-1, keepdims=True)
        var = jnp.mean(jnp.square(x - mu), axis=-1, keepdims=True)
        xn = (x - mu) * jax.lax.rsqrt(var + EPS) * gamma + beta
        logits = jnp.einsum('bsd,de->bse', xn, Wr) + br
        top_vals, top_idx = jax.lax.top_k(logits, K)
        w = jax.nn.softmax(top_vals, axis=-1)
        w_full = jnp.einsum('bsk,bske->bse', w, jax.nn.one_hot(top_idx, E, dtype=w.dtype))
        y = jnp.zeros(x.shape[:-1] + (DOUT,), x.dtype)
        for e in range(E):
            h = jax.nn.gelu(jnp.einsum('bsd,dh->bsh', xn, W1[e]) + b1[e], approximate=False)
            y_e = jnp.einsum('bsh,hd->bsd', h, W2[e]) + b2[e]
            y = y + y_e * w_full[..., e, None]
        return y
    edge_index = jnp.stack([src, dst])
    x = x + _L0_gnn_ref(_layernorm(x, axis=-1), edge_attr_3, L0_gnn_lin_src_w0, L0_gnn_lin_src_w1, L0_gnn_lin_dst_w0, L0_gnn_lin_dst_w1, L0_gnn_tp1_w00, L0_gnn_tp1_w11, L0_gnn_tp1_w01, L0_gnn_tp1_w10, L0_gnn_tp2_w00, L0_gnn_tp2_w11, L0_gnn_tp2_w01, L0_gnn_tp2_w10, L0_gnn_lin_hidden_w0, L0_gnn_lin_hidden_w1, L0_gnn_lin_scalar_w, edge_index)
    x = x + _L0_ffn_ref(_layernorm(x, axis=-1)[None], L0_ffn_weight, L0_ffn_bias)[0]
    x = x + _L1_gnn_ref(_layernorm(x, axis=-1), L1_gnn_Wq, L1_gnn_bq, L1_gnn_Wk, L1_gnn_bk, L1_gnn_Wv, L1_gnn_bv, src, dst)
    x = x + _L1_ffn_ref(_layernorm(x, axis=-1)[None], L1_ffn_gamma, L1_ffn_beta, L1_ffn_Wr, L1_ffn_br, L1_ffn_W1, L1_ffn_b1, L1_ffn_W2, L1_ffn_b2)[0]
    return x

_drawn_inputs = setup_inputs


def setup_inputs(seed=0):
    import zlib

    import numpy as np

    out = dict(_drawn_inputs(seed))
    spreads = {'L1_ffn_br': (0.0, 0.8)}
    factors = {'L0_ffn_bias': 8.0,
     'L1_gnn_Wq': 5.858,
     'L1_gnn_bq': 64.0,
     'L1_gnn_Wk': 5.304,
     'L1_gnn_bk': 8.0,
     'L1_gnn_bv': 8.0,
     'L1_ffn_gamma': 8.0,
     'L1_ffn_beta': 8.0,
     'L1_ffn_Wr': 7.856,
     'L1_ffn_W1': 6.876,
     'L1_ffn_b1': 49.732,
     'L1_ffn_W2': 6.697,
     'L1_ffn_b2': 64.0}
    for name, (base, spread) in spreads.items():
        noise = np.random.default_rng([zlib.crc32(name.encode()), seed]).standard_normal(out[name].shape)
        drawn = base * np.exp(spread * noise) if base else spread * noise
        out[name] = jnp.asarray(drawn.astype(out[name].dtype))
    for name, factor in factors.items():
        out[name] = (out[name] * factor).astype(out[name].dtype)
    return out
```

```python
import concourse.bass as bass
from concourse import mybir
from contextlib import ExitStack

F32 = mybir.dt.float32
BF16 = mybir.dt.bfloat16
I32 = mybir.dt.int32
U32 = mybir.dt.uint32
ALU = mybir.AluOpType
ACT = mybir.ActivationFunctionType
AX = mybir.AxisListType

P = 128
NODES = 3125
NT = 25
NPAD = NT * P
D = 256
MUL = 64
EDGES = 50000
ET = 400
EPAD = ET * P
GT = 4
NG = ET // GT
UN = 4
NI = NG // UN
STEPS = ET + NT - 1
SB = -(-STEPS // GT)
RING = 32
T0W = 448
HEADS = 8
HD = 32
C = 1.0 / 8.0
TP = 1.0 / 128.0 ** 0.5
SQ3 = 3.0 ** 0.5
BIG = 3.0e38
NE = 8
HID = 512


def wait(e, sem, count):
    if not isinstance(count, int) or count > 0:
        e.wait_ge(sem, count)


def rolled(e, n, body, first=1, last=1):
    for i in range(first):
        body(i)
    with e.Fori(first, n - last) as i:
        body(i)
    for i in range(n - last, n):
        body(i)


def tile(t, i):
    if isinstance(i, int):
        return t[:, i, :]
    return t[:, bass.ds(i, 1), :].rearrange("p a w -> p (a w)")


def cols(t, i, w):
    return t[:, i:i + w] if isinstance(i, int) else t[:, bass.ds(i, w)]


def tiles(t, i, n):
    return t[:, i:i + n, :] if isinstance(i, int) else t[:, bass.ds(i, n), :]


class Mem:

    def __init__(self, nc, ctx, tag):
        self.nc, self.ctx, self.tag = nc, ctx, tag

    def sb(self, name, shape, dt=F32):
        return self.ctx.enter_context(self.nc.sbuf_tensor(f"{self.tag}_{name}", shape, dt))

    def ps(self, name, shape, dt=F32):
        return self.ctx.enter_context(self.nc.psum_tensor(f"{self.tag}_{name}", shape, dt))

    def sem(self, name):
        return self.ctx.enter_context(self.nc.semaphore(f"{self.tag}_{name}"))


def setup(nc, d, k):
    with ExitStack() as ctx:
        m = Mem(nc, ctx, "setup")
        w = m.sb("w", [64, 13, 64])
        a = m.sb("a", [64, 4, 64])
        wt = m.sb("wt", [64, 7, 64])
        dst_i = k["dst_i"]
        tile_i = m.sb("tile_i", [P, ET], I32)
        tile_f = m.sb("tile_f", [P, ET])
        last_row = m.sb("last_row", [P, P])
        ends = m.sb("ends", [P, ET])
        hit = m.sb("hit", [P, ET])
        step_tile = m.sb("step_tile", [P, 4])
        attr = m.sb("attr", [P, ET, 3])
        sq = m.sb("sq", [P, ET, 3])
        norm = m.sb("norm", [P, ET])
        norm2 = m.sb("norm2", [P, ET])
        inv = m.sb("inv", [P, ET])
        ia = m.sb("ia", [P, 512], I32)
        ps_w = m.ps("ps_w", [P, 512])
        ps_o = m.ps("ps_o", [P, 512])
        ps_e = m.ps("ps_e", [P, 512])
        ps_r = m.ps("ps_r", [P, 512])
        loaded, w_in, x_in = m.sem("loaded"), m.sem("w_in"), m.sem("x_in")
        made, iota_ok = m.sem("made"), m.sem("iota_ok")
        pe1, ev1, pe2, ev2, pe3, ev3 = (m.sem(n) for n in ("pe1", "ev1", "pe2", "ev2", "pe3", "ev3"))
        sq_ok, sqrt_ok, chain, walk, walk_pe = (m.sem(n) for n in ("sq_ok", "sqrt_ok", "chain", "walk", "walk_pe"))
        names = ["ls0T", "ls1T", "t00", "t11", "t01", "t10", "lh0", "lh1", "u00", "u11", "u01", "u10"]
        W = {n: w[:, i, :] for i, n in enumerate(names)}
        with nc.Block() as block:
            @block.sync
            def _(e):
                e.dma_start(dst_i[:, :], d["dst_pt"]).then_inc(loaded, 16)
                e.dma_start(k["src_i"][:, :], d["src_pt"]).then_inc(loaded, 16)
                e.dma_start(attr[:, :, :], d["attr_pt"]).then_inc(loaded, 16)
                e.dma_start(k["X"][:, :, :], d["x"].rearrange("(n p) c -> p n c", p=P)).then_inc(x_in, 16)
                e.wait_ge(loaded, 48)
                e.wait_ge(x_in, 16)

            @block.scalar
            def _(e):
                for i, n in enumerate(names):
                    e.dma_start(w[:, i, :], d[n]).then_inc(w_in, 16)
                e.dma_start(k["LSC2"][0:64, :], d["lsc"]).then_inc(w_in, 16)
                e.dma_start(k["LSC2"][64:128, :], d["lsc"]).then_inc(w_in, 16)
                e.wait_ge(w_in, 14 * 16)
                e.wait_ge(chain, 2)
                e.activation(norm[:, :], norm2[:, :], ACT.Sqrt).then_inc(sqrt_ok, 1)

            @block.gpsimd
            def _(e):
                e.iota(k["iota"][:, :], pattern=[[1, NPAD]], base=0, channel_multiplier=0,
                       allow_small_or_imprecise_dtypes=True).then_inc(iota_ok, 1)
                e.memset(k["ident"][:, :], 0.0).then_inc(made, 1)
                e.memset(last_row[:, :], 0.0).then_inc(made, 1)
                e.memset(wt[:, :, :], 0.0).then_inc(made, 1)
                e.memset(k["blockww"][:, :], 0.0).then_inc(made, 1)
                e.wait_ge(made, 2)
                e.affine_select(out=k["ident"][:, :], in_=k["ident"][:, :], compare_op=ALU.not_equal, fill=1.0,
                                base=0, pattern=[[-1, P]], channel_multiplier=1).then_inc(made, 1)
                e.affine_select(out=last_row[:, :], in_=last_row[:, :], compare_op=ALU.not_equal, fill=1.0,
                                base=-(P - 1), pattern=[[0, P]], channel_multiplier=1).then_inc(made, 1)
                e.iota(step_tile[:, :], pattern=[[P, 4]], base=0, channel_multiplier=1,
                       allow_small_or_imprecise_dtypes=True).then_inc(made, 1)

            @block.vector
            def _(e):
                n = [0]

                def link(ins):
                    ins.then_inc(chain, 1)
                    n[0] += 1
                    e.wait_ge(chain, n[0])
                e.wait_ge(loaded, 48)
                link(e.tensor_tensor(sq[:, :, :], attr[:, :, :], attr[:, :, :], ALU.mult))
                link(e.tensor_reduce(norm2[:, :], sq[:, :, :], AX.X, ALU.add))
                link(e.tensor_copy(k["dst_f"][:, :], dst_i[:, :]))
                link(e.tensor_single_scalar(tile_i[:, :], dst_i[:, :], 7, ALU.arith_shift_right))
                link(e.tensor_copy(tile_f[:, :], tile_i[:, :]))
                e.wait_ge(sqrt_ok, 1)
                link(e.tensor_scalar_add(norm2[:, :], norm[:, :], 1e-12))
                link(e.reciprocal(inv[:, :], norm2[:, :]))
                link(e.tensor_tensor(k["r"][:, :, :], attr[:, :, :],
                                     inv[:, :].unsqueeze(2).to_broadcast([P, ET, 3]), ALU.mult))
                link(e.tensor_tensor(sq[:, :, :], k["r"][:, :, :], k["r"][:, :, :], ALU.mult))
                link(e.tensor_reduce(k["s2"][:, :], sq[:, :, :], AX.X, ALU.add))
                e.wait_ge(walk_pe, 1)
                e.wait_ge(iota_ok, 1)
                e.wait_ge(made, 7)
                link(e.scalar_tensor_tensor(ends[:, :], ps_r[:, 0:ET], 1.0, k["iota"][:, 0:ET], ALU.add, ALU.add))
                for c in range(4):
                    link(e.tensor_scalar(hit[:, :], ends[:, :], step_tile[:, c:c + 1], 0.0, ALU.is_le, ALU.add,
                                         accum_out=k["tcol"][:, c:c + 1]))
                e.engine_nop().then_inc(walk, 1)
                e.wait_ge(walk_pe, 2)
                link(e.tensor_copy(k["walk_t"][:, :], ps_e[0:1, :]))
                link(e.tensor_tensor(k["walk_n"][:, :], k["iota"][0:1, 0:512], ps_e[0:1, :], ALU.subtract))
                link(e.tensor_single_scalar(k["walk_slot"][:, :], k["walk_t"][:, :], RING - 1, ALU.bitwise_and))
                e.wait_ge(pe1, 1)
                e.tensor_copy(a[:, :, :], ps_w[0:64, 0:256].rearrange("p (a b) -> p a b", a=4)).then_inc(ev1, 1)
                e.wait_ge(pe2, 1)
                s = C * TP * C
                e.tensor_scalar_mul(wt[:, 0:2, :], ps_w[0:64, 256:384].rearrange("p (a b) -> p a b", a=2), s)
                e.tensor_scalar_mul(wt[:, 5, :], ps_w[0:64, 384:448], s)
                e.tensor_scalar_mul(wt[:, 3, :], ps_w[0:64, 448:512], s)
                e.tensor_scalar_mul(wt[:, 4, :], ps_w[0:64, 448:512], s).then_inc(ev2, 1)
                e.wait_ge(pe3, 1)
                e.tensor_copy(k["WH"][:, 0:64], ps_o[:, 0:64])
                e.tensor_scalar_mul(k["WH"][:, 64:128], ps_o[:, 0:64], -0.01)
                e.tensor_scalar_mul(k["WO"][:, 0:64], ps_o[:, 64:128], TP)
                e.tensor_scalar_mul(k["WO"][:, 64:128], ps_o[:, 128:192], SQ3 * TP)
                e.tensor_scalar_mul(k["WO"][:, 128:192], ps_o[:, 192:256], SQ3 * TP)
                e.tensor_scalar_mul(k["blockww"][0:64, 0:64], ps_o[0:64, 256:320], TP)
                e.tensor_scalar_mul(k["blockww"][64:128, 64:128], ps_o[64:128, 256:320], TP)
                e.wait_ge(w_in, 14 * 16)
                e.tensor_scalar_mul(k["LSC2"][0:64, :], k["LSC2"][0:64, :], C)
                e.tensor_scalar_mul(k["LSC2"][64:128, :], k["LSC2"][64:128, :], -C).then_inc(ev3, 1)

            @block.tensor
            def _(e):
                e.wait_ge(made, 7)
                e.wait_ge(chain, 5)
                e.matmul(ps_r[:, 0:ET], last_row[:, :], tile_f[:, :], start=True, stop=True).then_inc(walk_pe, 1)
                e.wait_ge(walk, 1)
                for c in range(4):
                    x = e.matmul(ps_e[0:1, c * P:(c + 1) * P], k["tcol"][:, c:c + 1], k["ident"][:, :],
                                 start=True, stop=True)
                x.then_inc(walk_pe, 1)
                e.wait_ge(w_in, 14 * 16)
                for i, (l, r) in enumerate((("t00", "ls0T"), ("t11", "ls1T"), ("t01", "ls0T"), ("t10", "ls1T"))):
                    x = e.matmul(ps_w[0:64, i * 64:i * 64 + 64], W[l], W[r], start=True, stop=True)
                x.then_inc(pe1, 1)
                e.wait_ge(ev1, 1)
                for i, l in enumerate(("lh0", "lh0", "lh1", "lh1")):
                    x = e.matmul(ps_w[0:64, 256 + i * 64:320 + i * 64], W[l], a[:, i, :], start=True, stop=True)
                x.then_inc(pe2, 1)
                e.wait_ge(ev2, 1)
                pair = lambda i: wt[:, i:i + 2, :].rearrange("p a b -> p (a b)")
                e.matmul(ps_o[:, 0:64], pair(0), k["ident"][0:64, 0:64], start=True, stop=True)
                e.matmul(ps_o[:, 64:128], pair(0), W["u00"], start=True, stop=False)
                e.matmul(ps_o[:, 64:128], pair(2), W["u11"], start=False, stop=True)
                e.matmul(ps_o[:, 128:192], pair(0), W["u01"], start=True, stop=False)
                e.matmul(ps_o[:, 128:192], pair(5), W["u10"], start=False, stop=True)
                e.matmul(ps_o[:, 192:256], pair(5), W["u11"], start=True, stop=True)
                e.matmul(ps_o[:, 256:320], pair(3), W["u10"], start=True, stop=True).then_inc(pe3, 1)


def moments(nc, k, tag):
    with ExitStack() as ctx:
        m = Mem(nc, ctx, tag)
        stats = m.sb("stats", [P, NT, 6])
        var = m.sb("var", [P, NT])
        root = m.sb("root", [P, NT])
        st, mv, ve, sq = m.sem("st"), m.sem("mv"), m.sem("ve"), m.sem("sq")
        with nc.Block() as block:
            @block.vector
            def _(e):
                def stat(i):
                    e.bn_stats(tile(stats, i), tile(k["X"], i)).then_inc(st, 1)
                rolled(e, NT, stat)

                def aggr(i):
                    wait(e, st, NT)
                    e.bn_aggr(tile(k["mv"], i), tile(stats, i)).then_inc(mv, 1)
                for i in range(NT):
                    aggr(i)
                e.wait_ge(mv, NT)
                e.tensor_scalar_add(var[:, :], k["mv"][:, :, 1], 1e-5).then_inc(ve, 1)
                e.wait_ge(sq, 1)
                e.reciprocal(k["rstd"][:, :], root[:, :]).then_inc(ve, 1)

            @block.scalar
            def _(e):
                e.wait_ge(ve, 1)
                e.activation(root[:, :], var[:, :], ACT.Sqrt).then_inc(sq, 1)


def nodes0(nc, d, k):
    with ExitStack() as ctx:
        m = Mem(nc, ctx, "nodes0")
        row = m.sb("row", [P, 2, T0W])
        tt = m.sb("tt", [P, 2, 256])
        ps_t = m.ps("ps_t", [P, 2, 512])
        ps_y = m.ps("ps_y", [P, 2, 512])
        normed, added, t_ps, t_sb, y_ps, y_sb = (m.sem(n) for n in ("normed", "added", "t_ps", "t_sb", "y_ps", "y_sb"))
        stored = [m.sem(f"stored{i}") for i in range(2)]
        table = d["tab0"].rearrange("(n p) c -> n p c", p=P)

        def both(e, body):
            for i in range(2):
                body(i, i, 0)
            with e.Fori(1, 11) as it:
                for j in range(2):
                    body(it * 2 + j, j, it)
            for i in range(22, NT):
                body(i, i % 2, i // 2)

        with nc.Block() as block:
            @block.vector
            def _(e):
                def body(i, j, it):
                    wait(e, stored[j], it * 16)
                    X = tile(k["X"], i)
                    mean = cols(k["mvf"], i * 2, 1)
                    rs = cols(k["rstd"], i, 1)
                    e.tensor_scalar(row[:, j, 0:64], X[:, 0:64], mean, rs, ALU.subtract, ALU.mult).then_inc(normed, 1)
                    e.tensor_scalar(row[:, j, 64:256].rearrange("p (m u) -> p u m", m=3),
                                    X[:, 64:256].rearrange("p (u m) -> p u m", m=3),
                                    mean, rs, ALU.subtract, ALU.mult).then_inc(normed, 1)
                    e.wait_ge(normed, i * 2 + 2)
                    e.tensor_tensor(X[:, 0:64], X[:, 0:64], row[:, j, 0:64], ALU.add)
                    e.tensor_tensor(X[:, 64:256].rearrange("p (u m) -> p u m", m=3),
                                    X[:, 64:256].rearrange("p (u m) -> p u m", m=3),
                                    row[:, j, 64:256].rearrange("p (m u) -> p u m", m=3), ALU.add).then_inc(added, 1)
                both(e, body)

            @block.tensor
            def _(e):
                def body(i, j, it):
                    e.wait_ge(normed, i * 2 + 2)
                    wait(e, t_sb, i - 1)
                    e.transpose(ps_t[:, j, 0:128], row[:, j, 64:192], k["ident"][:, :])
                    e.transpose(ps_t[0:64, j, 128:256], row[:, j, 192:256], k["ident"][:, :]).then_inc(t_ps, 1)
                    e.wait_ge(t_sb, i + 1)
                    wait(e, y_sb, i - 1)
                    e.matmul(ps_y[:, j, 0:128], tt[:, j, 0:128], k["blockww"][:, :], start=True, stop=True)
                    e.matmul(ps_y[:, j, 128:192], tt[0:64, j, 128:256], k["blockww"][0:64, 0:64],
                             start=True, stop=True).then_inc(y_ps, 1)
                both(e, body)

            @block.scalar
            def _(e):
                def body(i, j, it):
                    e.wait_ge(t_ps, i + 1)
                    wait(e, y_ps, i - 1)
                    e.activation(tt[:, j, 0:128], ps_t[:, j, 0:128], ACT.Copy)
                    e.activation(tt[0:64, j, 128:256], ps_t[0:64, j, 128:256], ACT.Copy).then_inc(t_sb, 1)
                    e.wait_ge(y_ps, i + 1)
                    e.wait_ge(normed, i * 2 + 2)
                    e.activation(row[:, j, 256:448], ps_y[:, j, 0:192], ACT.Copy).then_inc(y_sb, 1)
                both(e, body)

            @block.sync
            def _(e):
                def body(i, j, it):
                    e.wait_ge(y_sb, i + 1)
                    e.wait_ge(normed, i * 2 + 2)
                    src = row[:, j, :]
                    dst = table[i, :, :] if isinstance(i, int) else table[bass.ds(i, 1), :, :].rearrange("a p c -> (a p) c")
                    e.dma_start(dst, src).then_inc(stored[j], 16)
                both(e, body)
                e.wait_ge(stored[0], 13 * 16)
                e.wait_ge(stored[1], 12 * 16)


def walk_values(nc, e, k, s, *names):
    top = {"walk_t": ET - 1, "walk_n": NT - 1, "walk_slot": RING - 1}
    out = []
    for n in names:
        at = k[n][0:1, s:s + 1] if isinstance(s, int) else k[n][0:1, bass.ds(s, 1)]
        out.append(nc.s_assert_within(e.value_load(at), 0, top[n], skip_runtime_bounds_check_because=WALK))
    return out


WALK = "the walk visits each edge tile and each node tile in order, in as many steps as it has"


def gathers(e, scr, carried, staged, landed, tables, used):
    e.memset(scr[:, :], 0.0).then_inc(carried, 1)
    n = len(tables)

    def carry(count):
        e.wait_ge(carried, count + 1)
        e.tensor_tensor(scr[:, 0:1], scr[:, 1:2], scr[:, 1:2], ALU.add).then_inc(carried, 1)

    def body(it):
        for b in range(UN):
            g = it * UN + b
            for sem, count in used(g):
                wait(e, sem, count)
            wait(e, landed[b], it * 16 * GT * n)
            carry(2 * g)
            for _, index, stage, _ in tables:
                e.tensor_copy(stage[:, b, :], cols(index, g * GT, GT)).then_inc(staged, 1)
            e.wait_ge(staged, (g + 1) * n)
            carry(2 * g + 1)
            for j in range(GT):
                for table, _, stage, buffer in tables:
                    e.indirect_dma_start(out=buffer(b, j), out_offset=None, in_=table,
                                         in_offset=bass.IndirectOffsetOnAxis(ap=stage[:, b, j:j + 1], axis=0)
                                         ).then_inc(landed[b], 16)
    rolled(e, NI, body)


def edges0(nc, d, k):
    with ExitStack() as ctx:
        m = Mem(nc, ctx, "edges0")
        G = m.sb("G", [P, UN, GT, T0W])
        stage = m.sb("stage", [P, UN, GT], I32)
        scr = m.sb("scr", [P, 2])
        ring = m.sb("ring", [P, RING, D])
        xm = m.sb("xm", [P, GT, 3, 64])
        xs = m.sb("xs", [P, GT, 64])
        XT = m.sb("XT", [P, 2, GT * P])
        HT = m.sb("HT", [P, 2, GT * P])
        mx = m.sb("mx", [P, GT])
        mx0 = m.sb("mx0", [P, GT])
        scs = m.sb("scs", [P, GT, 64])
        ex = m.sb("ex", [P, GT, 64])
        en = m.sb("en", [P, GT])
        zs = m.sb("zs", [P, GT])
        z = m.sb("z", [P, GT])
        rr = m.sb("rr", [P, GT, 3])
        o0 = m.sb("o0", [P, GT, 64])
        o0b = m.sb("o0b", [P, GT, 64])
        o1 = m.sb("o1", [P, GT, 3, 64])
        wz = m.sb("wz", [P, ET])
        hot = m.sb("hot", [P, GT, P])
        ps_x = m.ps("ps_x", [P, GT * P])
        ps_h = m.ps("ps_h", [P, GT * P])
        ps_p = m.ps("ps_p", [P, 2, 512])
        ps_s = m.ps("ps_s", [P, 512])
        ps_a = [m.ps(f"ps_a{i}", [P, 512]) for i in range(2)]
        S = m.sem
        landed = [S(f"landed{i}") for i in range(UN)]
        staged, g_free, x_used, xm_ok, xs_ok, xr_ok = (S(n) for n in ("staged", "g_free2", "x_used", "xm_ok", "xs_ok", "xr_ok"))
        xt_ps, xt_sb, h_ps, h_sb, p_ps, sc_ps = (S(n) for n in ("xt_ps", "xt_sb", "h_ps", "h_sb", "p_ps", "sc_ps"))
        mx_ok, mx0_ok, scs_ok, ex_ok, en_ok, z_ok, zz_ok = (S(n) for n in ("mx_ok", "mx0_ok", "scs_ok", "ex_ok", "en_ok", "z_ok", "zz_ok"))
        wz_ok, rr_ok, q_ok, o_ok, m0_ok, o1_ok, m1_ok = (S(n) for n in ("wz_ok", "rr_ok", "q_ok", "o_ok", "m0_ok", "o1_ok", "m1_ok"))
        hot_ok, sum_ps, acc_ok, scr_ok = (S(n) for n in ("hot_ok", "sum_ps", "acc_ok", "scr_ok"))
        acc = k["acc0"]

        with nc.Block() as block:
            @block.gpsimd
            def _(e):
                gathers(e, scr, scr_ok, staged, landed,
                        [(d["tab0"], k["src_i"], stage, lambda b, j: G[:, b, j, :])],
                        lambda g: [(m1_ok, g - UN + 1), (xt_ps, g - UN + 1)])

            @block.vector
            def _(e):
                e.memset(acc[:, :, :], 0.0).then_inc(acc_ok, 1)
                e.wait_ge(acc_ok, 1)

                def direct(g, b, it):
                    e.wait_ge(landed[b], (it + 1) * 16 * GT)
                    x1 = G[:, b, :, 64:256].rearrange("p t (m u) -> p t m u", m=3)
                    r = tiles(k["r"], g * GT, GT).unsqueeze(3).to_broadcast([P, GT, 3, 64])
                    wait(e, xr_ok, g)
                    e.tensor_tensor(xm[:, :, :, :], x1, r, ALU.mult).then_inc(xm_ok, 1)
                    e.wait_ge(xm_ok, g + 1)
                    e.tensor_tensor(xs[:, :, :], xm[:, :, 0, :], xm[:, :, 1, :], ALU.add).then_inc(xs_ok, 1)
                    e.wait_ge(xs_ok, g + 1)
                    e.tensor_tensor(G[:, b, :, 64:128], xs[:, :, :], xm[:, :, 2, :], ALU.add).then_inc(xr_ok, 1)

                def softmax_a(g, b):
                    e.wait_ge(sc_ps, g + 1)
                    sc = ps_s[:, 0:GT * 64].rearrange("p (t c) -> p t c", t=GT)
                    wait(e, mx0_ok, g)
                    e.tensor_reduce(mx[:, :], sc, AX.X, ALU.max).then_inc(mx_ok, 1)
                    e.wait_ge(mx_ok, g + 1)
                    wait(e, en_ok, g)
                    wait(e, scs_ok, g)
                    e.tensor_scalar_max(mx0[:, :], mx[:, :], 0.0).then_inc(mx0_ok, 1)
                    e.wait_ge(mx0_ok, g + 1)
                    wait(e, ex_ok, g)
                    e.tensor_tensor(scs[:, :, :], sc, mx0[:, :].unsqueeze(2).to_broadcast([P, GT, 64]),
                                    ALU.subtract).then_inc(scs_ok, 1)

                def messages(g, b):
                    e.wait_ge(en_ok, g + 1)
                    e.wait_ge(ex_ok, g + 1)
                    e.wait_ge(p_ps, g + 1)
                    wait(e, m1_ok, g)
                    wait(e, m0_ok, g)
                    P4 = ps_p[:, :, 0:384].rearrange("p h (t c) -> p h t c", t=2)
                    four = lambda t: t[:, :, :].rearrange("p (h t) c -> p h t c", h=2)
                    e.tensor_reduce(zs[:, :], ex[:, :, :], AX.X, ALU.add).then_inc(z_ok, 1)
                    e.tensor_tensor(rr[:, :, :], tiles(k["r"], g * GT, GT),
                                    en[:, :].unsqueeze(2).to_broadcast([P, GT, 3]), ALU.mult).then_inc(rr_ok, 1)
                    s2 = cols(k["s2"], g * GT, GT)
                    for h in range(2):
                        e.tensor_tensor(o0[:, 2 * h:2 * h + 2, :], P4[:, h, :, 128:192],
                                        s2[:, 2 * h:2 * h + 2].unsqueeze(2).to_broadcast([P, 2, 64]),
                                        ALU.mult).then_inc(q_ok, 1)
                    e.wait_ge(z_ok, g + 1)
                    wait(e, wz_ok, g)
                    e.scalar_tensor_tensor(z[:, :], en[:, :], 192.0, zs[:, :], ALU.mult, ALU.add).then_inc(zz_ok, 1)
                    e.wait_ge(q_ok, 2 * g + 2)
                    e.tensor_tensor(four(o0b), four(o0), P4[:, :, :, 0:64], ALU.add).then_inc(o_ok, 1)
                    e.wait_ge(rr_ok, g + 1)
                    for h in range(2):
                        for t in range(2):
                            i = 2 * h + t
                            e.tensor_tensor(o1[:, i, :, :], P4[:, h, t, 64:128].unsqueeze(1).to_broadcast([P, 3, 64]),
                                            rr[:, i, :].unsqueeze(2).to_broadcast([P, 3, 64]), ALU.mult).then_inc(o1_ok, 1)
                    e.wait_ge(zz_ok, g + 1)
                    e.reciprocal(cols(wz, g * GT, GT), z[:, :]).then_inc(wz_ok, 1)
                    slot = (g % (RING // GT)) * GT
                    e.wait_ge(o_ok, g + 1)
                    e.tensor_tensor(tiles(ring, slot, GT)[:, :, 0:64], o0b[:, :, :], ex[:, :, :], ALU.mult).then_inc(m0_ok, 1)
                    e.wait_ge(o1_ok, 4 * g + 4)
                    for i in range(GT):
                        out = tile(ring, slot + i)[:, 64:256]
                        x = e.scalar_tensor_tensor(out, G[:, b, i, 256:448], en[:, i:i + 1],
                                                   o1[:, i, :, :].rearrange("p m u -> p (m u)"), ALU.mult, ALU.add)
                        if i == GT - 1:
                            x.then_inc(m1_ok, 1)

                def one_hots(blk):
                    for j in range(GT):
                        t, n = walk_values(nc, e, k, blk * GT + j, "walk_t", "walk_n")
                        if not isinstance(blk, int) or blk < NG:
                            e.wait_ge(wz_ok, blk + 1)
                        e.tensor_scalar(hot[:, j, :], cols(k["iota"], n * P, P), cols(k["dst_f"], t, 1), cols(wz, t, 1),
                                        ALU.is_equal, ALU.mult).then_inc(hot_ok, 1)

                def add(blk, j):
                    n, = walk_values(nc, e, k, blk * GT + j, "walk_n")
                    e.wait_ge(sum_ps, blk * GT + j + 1)
                    e.wait_ge(acc_ok, blk * GT + j + 1)
                    e.tensor_tensor(tile(acc, n), tile(acc, n), ps_a[j % 2][:, 0:D], ALU.add).then_inc(acc_ok, 1)

                def body(it, last=False):
                    for b in range(UN):
                        g = it * UN + b
                        end = last and b == UN - 1
                        first = isinstance(g, int) and g == 0
                        softmax_a(g, b)
                        if not end:
                            direct(g + 1, (b + 1) % UN, it + 1 if b == UN - 1 else it)
                        if not first:
                            add(g - 1, 0)
                            add(g - 1, 1)
                        messages(g, b)
                        if not first:
                            add(g - 1, 2)
                            add(g - 1, 3)
                        one_hots(g)
                direct(0, 0, 0)
                body(0)
                with e.Fori(1, NI - 1) as it:
                    body(it)
                body(NI - 1, last=True)
                for blk in range(NG, SB + 1):
                    for j in range(GT):
                        add(blk - 1, j)
                    if blk < SB:
                        one_hots(blk)
                e.wait_ge(acc_ok, SB * GT + 1)

            @block.tensor
            def _(e):
                def aggregate(blk, j):
                    slot, = walk_values(nc, e, k, blk * GT + j, "walk_slot")
                    e.wait_ge(hot_ok, blk * GT + GT)
                    if j == 0 and (not isinstance(blk, int) or blk < NG):
                        e.wait_ge(m1_ok, blk + 1)
                        e.wait_ge(m0_ok, blk + 1)
                    wait(e, acc_ok, blk * GT + j)
                    e.matmul(ps_a[j % 2][:, 0:D], hot[:, j, :], tile(ring, slot), start=True, stop=True).then_inc(sum_ps, 1)

                def front(g, b, between):
                    e.wait_ge(xr_ok, g + 1)
                    wait(e, xt_sb, g)
                    for t in range(GT):
                        x = e.transpose(ps_x[:, t * P:(t + 1) * P], G[:, b, t, 0:128], k["ident"][:, :])
                    x.then_inc(xt_ps, 1)
                    between(0)
                    e.wait_ge(xt_sb, g + 1)
                    wait(e, h_sb, g)
                    e.matmul(ps_h[:, :], k["WH"][:, :], XT[:, b % 2, :], start=True, stop=True).then_inc(h_ps, 1)
                    between(1)
                    wait(e, o_ok, g)
                    wait(e, o1_ok, 4 * g)
                    for t in range(GT):
                        x = e.matmul(ps_p[:, t // 2, (t % 2) * 192:(t % 2) * 192 + 192],
                                     XT[:, b % 2, t * P:(t + 1) * P], k["WO"][:, :], start=True, stop=True)
                    x.then_inc(p_ps, 1)
                    e.wait_ge(h_sb, g + 1)
                    wait(e, scs_ok, g)
                    for t in range(GT):
                        x = e.matmul(ps_s[:, t * 64:(t + 1) * 64], HT[:, b % 2, t * P:(t + 1) * P],
                                     k["LSC2"][:, :], start=True, stop=True)
                    x.then_inc(sc_ps, 1)

                def body(it, last=False):
                    for b in range(UN):
                        g = it * UN + b
                        first = isinstance(g, int) and g == 0

                        def between(h):
                            if not first:
                                aggregate(g - 1, 2 * h)
                                aggregate(g - 1, 2 * h + 1)
                        if last and b == UN - 1:
                            between(0)
                            between(1)
                        else:
                            front(g + 1, (b + 1) % UN, between)
                front(0, 0, lambda h: None)
                body(0)
                with e.Fori(1, NI - 1) as it:
                    body(it)
                body(NI - 1, last=True)
                for blk in range(NG - 1, SB):
                    for j in range(GT):
                        aggregate(blk, j)

            @block.scalar
            def _(e):
                def front(g, b):
                    e.wait_ge(xt_ps, g + 1)
                    wait(e, p_ps, g - 1)
                    wait(e, h_ps, g - 1)
                    e.activation(XT[:, b % 2, :], ps_x[:, :], ACT.Copy).then_inc(xt_sb, 1)
                    e.wait_ge(h_ps, g + 1)
                    wait(e, sc_ps, g - 1)
                    e.activation(HT[:, b % 2, :], ps_h[:, :], ACT.Relu).then_inc(h_sb, 1)

                def exps(g):
                    e.wait_ge(mx0_ok, g + 1)
                    wait(e, m1_ok, g)
                    e.activation(en[:, :], mx0[:, :], ACT.Exp, scale=-1.0).then_inc(en_ok, 1)
                    e.wait_ge(scs_ok, g + 1)
                    wait(e, m0_ok, g)
                    wait(e, z_ok, g)
                    e.activation(ex[:, :, :], scs[:, :, :], ACT.Exp).then_inc(ex_ok, 1)

                def body(it, last=False):
                    for b in range(UN):
                        g = it * UN + b
                        exps(g)
                        if not (last and b == UN - 1):
                            front(g + 1, (b + 1) % UN)
                front(0, 0)
                body(0)
                with e.Fori(1, NI - 1) as it:
                    body(it)
                body(NI - 1, last=True)


def pairs(body, n=NT):
    def run(e):
        for i in range(2):
            body(i, i, 0)
        with e.Fori(1, n // 2 - 1) as it:
            for j in range(2):
                body(it * 2 + j, j, it)
        for i in range(2 * (n // 2 - 1), n):
            body(i, i % 2, i // 2)
    return run


def lns(nc, d, k):
    EPS = 1e-8
    with ExitStack() as ctx:
        m = Mem(nc, ctx, "lns")
        w = m.sb("w", [P, 2, D])
        wa = m.sb("wa", [P, 2, D])
        ws = m.sb("ws", [P, 2, D], BF16)
        bias = m.sb("bias", [P, D])
        xn = m.sb("xn", [P, 2, D])
        at = m.sb("at", [P, 2, D])
        ab = m.sb("ab", [P, 2, D])
        wabs = m.sb("wabs", [P, 2, D])
        st = m.sb("st", [P, 2, D], BF16)
        sg = m.sb("sg", [P, 2, D])
        o = m.sb("o", [P, 2, D])
        o2 = m.sb("o2", [P, 2, D])
        ps_t = [m.ps(f"ps_t{i}", [P, 512]) for i in range(2)]
        ps_m = [m.ps(f"ps_m{i}", [P, 512]) for i in range(2)]
        ps_g = [m.ps(f"ps_g{i}", [P, 512]) for i in range(2)]
        S = m.sem
        ab_ok, wabs_ok = S("ab_ok"), S("wabs_ok")
        loaded, wa_ok, ws_ok, xn_ok, t_ps, at_ok, st_ok, y_ps, g_ps, sg_ok, o_ok, o2_ok, x_ok = (S(n) for n in (
            "loaded", "wa_ok", "ws_ok", "xn_ok", "t_ps", "at_ok", "st_ok", "y_ps", "g_ps", "sg_ok", "o_ok", "o2_ok", "x_ok"))
        with nc.Block() as block:
            @block.sync
            def _(e):
                e.dma_start(w[:, :, :], d["lnsT"].rearrange("(c p) n -> p c n", p=P)).then_inc(loaded, 16)
                e.dma_start(bias[:, :], d["lns_b"].to_broadcast([P, D])).then_inc(loaded, 16)

            @block.gpsimd
            def _(e):
                e.wait_ge(loaded, 32)
                e.wait_ge(wabs_ok, 1)
                e.tensor_scalar_add(wa[:, :, :], wabs[:, :, :], EPS).then_inc(wa_ok, 1)

            @block.vector
            def _(e):
                e.wait_ge(loaded, 32)

                def norm(i, j):
                    wait(e, t_ps, i - 1)
                    e.tensor_scalar(xn[:, j, :], tile(k["X"], i), cols(k["mvf"], i * 2, 1), cols(k["rstd"], i, 1),
                                    ALU.subtract, ALU.mult).then_inc(xn_ok, 1)

                def body(i, j, it):
                    if not (isinstance(i, int) and i == NT - 1):
                        norm(i + 1, 1 - j)
                    e.wait_ge(ab_ok, i + 1)
                    wait(e, y_ps, i - 1)
                    e.tensor_scalar_add(at[:, j, :], ab[:, j, :], EPS).then_inc(at_ok, 1)
                    e.wait_ge(sg_ok, i + 1)
                    e.wait_ge(y_ps, i + 1)
                    wait(e, o2_ok, i - 1)
                    e.tensor_tensor(o[:, j, :], sg[:, j, :], ps_m[j][:, 0:D], ALU.mult).then_inc(o_ok, 1)
                    e.wait_ge(o_ok, i + 1)
                    wait(e, x_ok, i - 1)
                    e.tensor_tensor(o2[:, j, :], o[:, j, :], bias[:, :], ALU.add).then_inc(o2_ok, 1)
                    e.wait_ge(o2_ok, i + 1)
                    e.tensor_tensor(tile(k["X"], i), tile(k["X"], i), o2[:, j, :], ALU.add).then_inc(x_ok, 1)
                norm(0, 0)
                pairs(body)(e)

            @block.tensor
            def _(e):
                e.wait_ge(wa_ok, 1)
                e.wait_ge(ws_ok, 1)

                def body(i, j, it):
                    e.wait_ge(xn_ok, i + 1)
                    wait(e, ab_ok, i - 1)
                    wait(e, st_ok, i - 1)
                    for c in range(2):
                        x = e.transpose(ps_t[j][:, c * P:(c + 1) * P], xn[:, j, c * P:(c + 1) * P], k["ident"][:, :])
                    x.then_inc(t_ps, 1)
                    e.wait_ge(st_ok, i + 1)
                    wait(e, sg_ok, i - 1)
                    for c in range(2):
                        x = e.matmul(ps_g[j][:, 0:D], st[:, j, c * P:(c + 1) * P], ws[:, c, :], start=c == 0, stop=c == 1)
                    x.then_inc(g_ps, 1)
                    e.wait_ge(at_ok, i + 1)
                    wait(e, o_ok, i - 1)
                    for c in range(2):
                        x = e.matmul(ps_m[j][:, 0:D], at[:, j, c * P:(c + 1) * P], wa[:, c, :], start=c == 0, stop=c == 1)
                    x.then_inc(y_ps, 1)
                pairs(body)(e)

            @block.scalar
            def _(e):
                e.wait_ge(loaded, 32)
                e.activation(wabs[:, :, :], w[:, :, :], ACT.Abs).then_inc(wabs_ok, 1)
                e.activation(ws[:, :, :], w[:, :, :], ACT.Sign).then_inc(ws_ok, 1)

                def body(i, j, it):
                    e.wait_ge(t_ps, i + 1)
                    wait(e, g_ps, i - 1)
                    e.activation(st[:, j, :], ps_t[j][:, 0:D], ACT.Sign).then_inc(st_ok, 1)
                    wait(e, at_ok, i - 1)
                    e.activation(ab[:, j, :], ps_t[j][:, 0:D], ACT.Abs).then_inc(ab_ok, 1)
                    e.wait_ge(g_ps, i + 1)
                    wait(e, o_ok, i - 1)
                    e.activation(sg[:, j, :], ps_g[j][:, 0:D], ACT.Sign).then_inc(sg_ok, 1)
                pairs(body)(e)


def qkv(nc, d, k):
    with ExitStack() as ctx:
        m = Mem(nc, ctx, "qkv")
        w = m.sb("w", [P, 2, 768])
        bias = m.sb("bias", [P, 768])
        xn = m.sb("xn", [P, 2, D])
        xt = m.sb("xt", [P, 2, D])
        row = m.sb("row", [P, 2, 768])
        ps_t = [m.ps(f"ps_t{i}", [P, 512]) for i in range(2)]
        ps_y = [m.ps(f"ps_y{i}", [P, 1024]) for i in range(2)]
        S = m.sem
        loaded, xn_ok, t_ps, xt_ok, y_ps, row_ok = (S(n) for n in ("loaded", "xn_ok", "t_ps", "xt_ok", "y_ps", "row_ok"))
        stored = [S(f"stored{i}") for i in range(2)]
        with nc.Block() as block:
            @block.sync
            def _(e):
                e.dma_start(w[:, :, :], d["wqkv"].rearrange("(c p) n -> p c n", p=P)).then_inc(loaded, 16)
                e.dma_start(bias[:, :], d["bqkv"].to_broadcast([P, 768])).then_inc(loaded, 16)

                def body(i, j, it):
                    e.wait_ge(row_ok, 2 * i + 2)
                    for n, name in enumerate(("qtab", "ktab", "vtab")):
                        t = d[name].rearrange("(n p) c -> n p c", p=P)
                        dst = t[i, :, :] if isinstance(i, int) else t[bass.ds(i, 1), :, :].rearrange("a p c -> (a p) c")
                        e.dma_start(dst, row[:, j, n * D:(n + 1) * D]).then_inc(stored[j], 16)
                pairs(body)(e)
                e.wait_ge(stored[0], 13 * 48)
                e.wait_ge(stored[1], 12 * 48)

            @block.vector
            def _(e):
                def norm(i, j):
                    wait(e, t_ps, i - 1)
                    e.tensor_scalar(xn[:, j, :], tile(k["X"], i), cols(k["mvf"], i * 2, 1), cols(k["rstd"], i, 1),
                                    ALU.subtract, ALU.mult).then_inc(xn_ok, 1)

                def body(i, j, it):
                    if not (isinstance(i, int) and i == NT - 1):
                        norm(i + 1, 1 - j)
                    e.wait_ge(y_ps, i + 1)
                    wait(e, stored[j], it * 48)
                    e.tensor_tensor(row[:, j, 0:512], ps_y[j][:, 0:512], bias[:, 0:512], ALU.add).then_inc(row_ok, 1)
                    e.tensor_tensor(row[:, j, 512:768], ps_y[j][:, 512:768], bias[:, 512:768], ALU.add).then_inc(row_ok, 1)
                e.wait_ge(loaded, 32)
                norm(0, 0)
                pairs(body)(e)

            @block.tensor
            def _(e):
                e.wait_ge(loaded, 32)

                def body(i, j, it):
                    e.wait_ge(xn_ok, i + 1)
                    wait(e, xt_ok, i - 1)
                    for c in range(2):
                        x = e.transpose(ps_t[j][:, c * P:(c + 1) * P], xn[:, j, c * P:(c + 1) * P], k["ident"][:, :])
                    x.then_inc(t_ps, 1)
                    e.wait_ge(xt_ok, i + 1)
                    wait(e, row_ok, 2 * i - 2)
                    for c in range(2):
                        e.matmul(ps_y[j][:, 0:512], xt[:, j, c * P:(c + 1) * P], w[:, c, 0:512], start=c == 0, stop=c == 1)
                    for c in range(2):
                        x = e.matmul(ps_y[j][:, 512:768], xt[:, j, c * P:(c + 1) * P], w[:, c, 512:768], start=c == 0, stop=c == 1)
                    x.then_inc(y_ps, 1)
                pairs(body)(e)

            @block.scalar
            def _(e):
                def body(i, j, it):
                    e.wait_ge(t_ps, i + 1)
                    wait(e, y_ps, i - 1)
                    e.activation(xt[:, j, :], ps_t[j][:, 0:D], ACT.Copy).then_inc(xt_ok, 1)
                pairs(body)(e)


def scores(nc, d, k):
    with ExitStack() as ctx:
        m = Mem(nc, ctx, "scores")
        Q = m.sb("Q", [P, UN, GT, D])
        K = m.sb("K", [P, UN, GT, D])
        sq, sk = m.sb("sq", [P, UN, GT], I32), m.sb("sk", [P, UN, GT], I32)
        scr = m.sb("scr", [P, 2])
        prod = m.sb("prod", [P, 2, GT, D])
        landed = [m.sem(f"landed{i}") for i in range(UN)]
        staged, carried, prod_ok, s_ok = (m.sem(n) for n in ("staged", "carried", "prod_ok", "s_ok"))
        with nc.Block() as block:
            @block.gpsimd
            def _(e):
                gathers(e, scr, carried, staged, landed,
                        [(d["qtab"], k["src_i"], sq, lambda b, j: Q[:, b, j, :]),
                         (d["ktab"], k["dst_i"], sk, lambda b, j: K[:, b, j, :])],
                        lambda g: [(prod_ok, g - UN + 1)])

            @block.vector
            def _(e):
                def body(it):
                    for b in range(UN):
                        g = it * UN + b
                        e.wait_ge(landed[b], (it + 1) * 16 * GT * 2)
                        wait(e, s_ok, g - 1)
                        e.tensor_tensor(prod[:, b % 2, :, :], Q[:, b, :, :], K[:, b, :, :], ALU.mult).then_inc(prod_ok, 1)
                        e.wait_ge(prod_ok, g + 1)
                        e.tensor_reduce(cols(k["S"], g * GT * HEADS, GT * HEADS),
                                        prod[:, b % 2, :, :].rearrange("p t (h c) -> p (t h) c", c=HD), AX.X, ALU.add
                                        ).then_inc(s_ok, 1)
                rolled(e, NI, body)


CH = 16
CT = ET // CH
CE = CT * P


def softmax_shift(nc, d, k):
    B = 1.0e38
    with ExitStack() as ctx:
        m = Mem(nc, ctx, "shift")
        ST = m.sb("ST", [P, CE])
        DT = m.sb("DT", [P, CE + 2])
        pen = m.sb("pen", [P, CE + 1])
        eq = m.sb("eq", [P, CE + 1])
        F = m.sb("F", [P, CE])
        R = m.sb("R", [P, CE])
        down, up = m.sb("down", [P, P]), m.sb("up", [P, P])
        pi = m.sb("pi", [P, 4], I32)
        pf = m.sb("pf", [P, 2])
        hsel, csel = m.sb("hsel", [P, HEADS]), m.sb("csel", [P, CH])
        hselT = m.sb("hselT", [HEADS, P])
        ends = m.sb("ends", [P, 4])
        spread = m.sb("spread", [P, 4, CH])
        small = m.sb("small", [HEADS, 4, CH])
        carry = m.sb("carry", [HEADS, 2, CH + 1])
        pick = m.sb("pick", [P, 2, CH])
        init = m.sb("init", [P, 2])
        ps = [m.ps(f"ps{i}", [P, 512]) for i in range(2)]
        ps_e = m.ps("ps_e", [P, 512])
        tr, ev, sel, chain, side, pe = (m.sem(n) for n in ("tr", "ev", "sel", "chain", "side", "pe"))
        ex_ok, back, back_ev, made = (m.sem(n) for n in ("ex_ok", "back", "back_ev", "made"))
        S4 = k["S"][:, :].rearrange("p (c j h) -> p j c h", c=CH, h=HEADS)
        D4 = k["dst_f"][:, :].rearrange("p (c j) -> p j c", c=CH)
        D2, S2 = m.sb("D2", [P, CT, P]), m.sb("S2", [P, CT, P])
        by4 = lambda t: t[:, :, :].rearrange("p j (c h) -> p j c h", h=HEADS)
        ordered = m.sem("ordered")
        rounds = [(a, j0, min(4, CT - j0)) for a in range(2) for j0 in range(0, CT, 4)]
        half = len(rounds) // 2
        with nc.Block() as block:
            @block.tensor
            def _(e):
                e.wait_ge(ordered, 2)
                for n, (a, j0, w) in enumerate(rounds):
                    wait(e, ev, n - 1)
                    for j in range(w):
                        x = e.transpose(ps[n % 2][:, j * P:(j + 1) * P], (D2, S2)[a][:, j0 + j, :], k["ident"][:, :])
                    x.then_inc(tr, 1)
                e.wait_ge(ev, half)
                e.wait_ge(made, 4)
                e.matmul(ps_e[:, 0:1], down[:, :], DT[:, CE:CE + 1], start=True, stop=True)
                e.matmul(ps_e[:, 1:2], up[:, :], DT[:, 1:2], start=True, stop=True).then_inc(pe, 1)
                e.wait_ge(sel, 2)
                e.wait_ge(side, 1)
                e.transpose(ps_e[0:HEADS, 0:P], hsel[:, :], k["ident"][:, :]).then_inc(pe, 1)
                e.wait_ge(side, 2)
                e.wait_ge(chain, 1)
                e.matmul(ps_e[0:HEADS, 128:192], hsel[:, :], spread[:, :, :].rearrange("p a c -> p (a c)"),
                         start=True, stop=True).then_inc(pe, 1)
                e.wait_ge(side, 3)
                e.matmul(ps_e[:, 256:288], hselT[:, :], small[:, 0:2, :].rearrange("p a c -> p (a c)"), start=True, stop=True).then_inc(pe, 1)
                e.wait_ge(ex_ok, 1)
                for n, (a, j0, w) in enumerate(rounds[half:]):
                    wait(e, back_ev, n - 1)
                    for j in range(w):
                        x = e.transpose(ps[n % 2][:, j * P:(j + 1) * P], F[:, (j0 + j) * P:(j0 + j + 1) * P], k["ident"][:, :])
                    x.then_inc(back, 1)

            @block.gpsimd
            def _(e):
                e.memset(down[:, :], 0.0).then_inc(made, 1)
                e.memset(up[:, :], 0.0).then_inc(made, 1)
                e.wait_ge(made, 2)
                e.tensor_copy(down[:, HEADS:P], k["ident"][:, 0:P - HEADS]).then_inc(made, 1)
                e.tensor_copy(up[:, 0:P - HEADS], k["ident"][:, HEADS:P]).then_inc(made, 1)
                e.iota(pi[:, 0:1], pattern=[[1, 1]], base=0, channel_multiplier=1).then_inc(made, 1)

            @block.scalar
            def _(e):
                e.activation(by4(D2), D4.unsqueeze(3).to_broadcast([P, CT, CH, HEADS]), ACT.Copy).then_inc(ordered, 1)
                for n, (a, j0, w) in enumerate(rounds):
                    to = DT[:, 1 + j0 * P:1 + (j0 + w) * P] if a == 0 else ST[:, j0 * P:(j0 + w) * P]
                    e.wait_ge(tr, n + 1)
                    e.activation(to, ps[n % 2][:, 0:w * P], ACT.Copy).then_inc(ev, 1)
                e.wait_ge(chain, 2)
                e.activation(F[:, :], R[:, :], ACT.Exp, scale=1.0 / HD ** 0.5).then_inc(ex_ok, 1)
                for n, (a, j0, w) in enumerate(rounds[half:]):
                    e.wait_ge(back, n + 1)
                    e.activation(S4[:, j0:j0 + w, :, :],
                                 ps[n % 2][:, 0:w * P].rearrange("p (j c h) -> p j c h", j=w, h=HEADS), ACT.Copy).then_inc(back_ev, 1)

            @block.vector
            def _(e):
                n = [0]
                own = m.sem("own")

                def link(ins):
                    ins.then_inc(own, 1)
                    n[0] += 1
                    e.wait_ge(own, n[0])
                e.tensor_copy(by4(S2), S4).then_inc(ordered, 1)
                e.wait_ge(made, 5)
                link(e.tensor_single_scalar(pi[:, 1:2], pi[:, 0:1], HEADS - 1, ALU.bitwise_and))
                link(e.tensor_single_scalar(pi[:, 2:3], pi[:, 0:1], 3, ALU.arith_shift_right))
                link(e.tensor_copy(pf[:, :], pi[:, 1:3]))
                e.tensor_scalar(hsel[:, :], k["iota"][:, 0:HEADS], pf[:, 0:1], None, ALU.is_equal).then_inc(sel, 1)
                e.tensor_scalar(csel[:, :], k["iota"][:, 0:CH], pf[:, 1:2], None, ALU.is_equal).then_inc(sel, 1)
                e.wait_ge(sel, 2)
                e.wait_ge(pe, 1)
                link(e.tensor_tensor(DT[:, 0:1], ps_e[:, 0:1], csel[:, 0:1], ALU.subtract))
                link(e.tensor_tensor(DT[:, CE + 1:CE + 2], ps_e[:, 1:2], csel[:, CH - 1:CH], ALU.subtract))
                e.engine_nop().then_inc(side, 1)
                link(e.tensor_tensor(eq[:, :], DT[:, 0:CE + 1], DT[:, 1:CE + 2], ALU.is_equal))
                link(e.tensor_scalar(pen[:, :], eq[:, :], -1.0, B, ALU.add, ALU.mult))
                e.wait_ge(ev, len(rounds))
                e.tensor_reduce(ends[:, 1:2], pen[:, 0:CE], AX.X, ALU.min)
                e.tensor_reduce(ends[:, 3:4], pen[:, 1:CE + 1], AX.X, ALU.min)
                e.tensor_tensor_scan(F[:, :], pen[:, 0:CE], ST[:, :], -B, ALU.add, ALU.max)
                link(e.tensor_tensor_scan(R[:, ::-1], pen[:, CE:0:-1], ST[:, ::-1], -B, ALU.add, ALU.max))
                e.tensor_copy(ends[:, 0:1], F[:, CE - 1:CE])
                link(e.tensor_copy(ends[:, 2:3], R[:, 0:1]))
                e.tensor_tensor(spread[:, :, :], ends[:, :].unsqueeze(2).to_broadcast([P, 4, CH]),
                                csel[:, :].unsqueeze(1).to_broadcast([P, 4, CH]), ALU.mult).then_inc(chain, 1)
                e.wait_ge(pe, 2)
                e.tensor_copy(hselT[:, :], ps_e[0:HEADS, 0:P]).then_inc(side, 1)
                e.memset(carry[:, :, :], -B)
                e.wait_ge(pe, 3)
                link(e.tensor_copy(small[:, :, :], ps_e[0:HEADS, 128:192].rearrange("p (a c) -> p a c", a=4)))
                link(e.tensor_tensor_scan(carry[:, 0, 1:CH + 1], small[:, 1, :], small[:, 0, :], -B, ALU.add, ALU.max))
                link(e.tensor_tensor_scan(carry[:, 1, CH - 1::-1], small[:, 3, ::-1], small[:, 2, ::-1], -B, ALU.add, ALU.max))
                e.tensor_copy(small[:, 0, :], carry[:, 0, 0:CH])
                e.tensor_copy(small[:, 1, :], carry[:, 1, 1:CH + 1]).then_inc(side, 1)
                e.wait_ge(pe, 4)
                link(e.tensor_tensor(pick[:, :, :], ps_e[:, 256:288].rearrange("p (a c) -> p a c", a=2),
                                     csel[:, :].unsqueeze(1).to_broadcast([P, 2, CH]), ALU.mult))
                link(e.tensor_reduce(init[:, :], pick[:, :, :], AX.X, ALU.add))
                link(e.tensor_tensor_scan(F[:, :], pen[:, 0:CE], ST[:, :], init[:, 0:1], ALU.add, ALU.max))
                link(e.tensor_tensor_scan(R[:, ::-1], pen[:, CE:0:-1], ST[:, ::-1], init[:, 1:2], ALU.add, ALU.max))
                link(e.tensor_tensor(eq[:, 0:CE], F[:, :], R[:, :], ALU.max))
                e.tensor_tensor(R[:, :], ST[:, :], eq[:, 0:CE], ALU.subtract).then_inc(chain, 1)


def aggregate1(nc, d, k):
    A = D + HEADS
    with ExitStack() as ctx:
        m = Mem(nc, ctx, "agg1")
        V = m.sb("V", [P, UN, GT, D])
        stage = m.sb("stage", [P, UN, GT], I32)
        scr = m.sb("scr", [P, 2])
        ring = m.sb("ring", [P, RING, A])
        hot = m.sb("hot", [P, 2, GT, P])
        ps_a = [m.ps(f"ps_a{i}", [P, 512]) for i in range(4)]
        landed = [m.sem(f"landed{i}") for i in range(UN)]
        staged, carried, msg_ok, p_ok, hot_ok, sum_ps, acc_ok = (
            m.sem(n) for n in ("staged", "carried", "msg_ok", "p_ok", "hot_ok", "sum_ps", "acc_ok"))
        acc = k["acc1"]
        with nc.Block() as block:
            @block.gpsimd
            def _(e):
                gathers(e, scr, carried, staged, landed,
                        [(d["vtab"], k["src_i"], stage, lambda b, j: V[:, b, j, :])], lambda g: [(msg_ok, g - UN + 1)])

            @block.vector
            def _(e):
                e.memset(acc[:, :, :], 0.0).then_inc(acc_ok, 1)

                def one_hots(blk, b):
                    for j in range(GT):
                        t, n = walk_values(nc, e, k, blk * GT + j, "walk_t", "walk_n")
                        wait(e, sum_ps, blk * GT - GT)
                        e.tensor_scalar(hot[:, b % 2, j, :], cols(k["iota"], n * P, P), cols(k["dst_f"], t, 1), None,
                                        ALU.is_equal).then_inc(hot_ok, 1)

                def add(blk, j):
                    n, = walk_values(nc, e, k, blk * GT + j, "walk_n")
                    e.wait_ge(sum_ps, blk * GT + j + 1)
                    e.wait_ge(acc_ok, blk * GT + j + 1)
                    e.tensor_tensor(tile(acc, n), tile(acc, n), ps_a[j][:, 0:A], ALU.add).then_inc(acc_ok, 1)

                def body(it):
                    for b in range(UN):
                        g = it * UN + b
                        one_hots(g, b)
                        e.wait_ge(landed[b], (it + 1) * 16 * GT)
                        slot = (g % (RING // GT)) * GT
                        p = cols(k["S"], g * GT * HEADS, GT * HEADS).rearrange("p (t h) -> p t h", h=HEADS)
                        e.tensor_copy(tiles(ring, slot, GT)[:, :, D:A], p).then_inc(p_ok, 1)
                        e.tensor_tensor(tiles(ring, slot, GT)[:, :, 0:D].rearrange("p t (h c) -> p t h c", c=HD),
                                        V[:, b, :, :].rearrange("p t (h c) -> p t h c", c=HD),
                                        p.unsqueeze(3).to_broadcast([P, GT, HEADS, HD]), ALU.mult).then_inc(msg_ok, 1)
                        if not (isinstance(g, int) and g == 0):
                            for j in range(GT):
                                add(g - 1, j)
                rolled(e, NI, body)
                for blk in range(NG, SB + 1):
                    if blk < SB:
                        one_hots(blk, blk)
                    for j in range(GT):
                        add(blk - 1, j)
                e.wait_ge(acc_ok, SB * GT + 1)

            @block.tensor
            def _(e):
                def block_of(blk, b):
                    for j in range(GT):
                        slot, = walk_values(nc, e, k, blk * GT + j, "walk_slot")
                        e.wait_ge(hot_ok, blk * GT + j + 1)
                        if j == 0 and not (isinstance(blk, int) and blk >= NG):
                            e.wait_ge(msg_ok, blk + 1)
                            e.wait_ge(p_ok, blk + 1)
                        wait(e, acc_ok, blk * GT + j - GT + 2)
                        e.matmul(ps_a[j][:, 0:A], hot[:, b % 2, j, :], tile(ring, slot), start=True, stop=True).then_inc(sum_ps, 1)

                def body(it):
                    for b in range(UN):
                        block_of(it * UN + b, b)
                rolled(e, NI, body)
                for blk in range(NG, SB):
                    block_of(blk, blk)


def add_acc1(nc, k):
    with ExitStack() as ctx:
        m = Mem(nc, ctx, "add1")
        z, rz = m.sb("z", [P, NT, HEADS]), m.sb("rz", [P, NT, HEADS])
        s = m.sem("s")
        acc = k["acc1"]
        with nc.Block() as block:
            @block.vector
            def _(e):
                e.tensor_scalar_max(z[:, :, :], acc[:, :, D:D + HEADS], 1e-16).then_inc(s, 1)
                e.wait_ge(s, 1)
                e.reciprocal(rz[:, :, :], z[:, :, :]).then_inc(s, 1)
                e.wait_ge(s, 2)
                v = acc[:, :, 0:D].rearrange("p n (h c) -> p n h c", c=HD)
                e.tensor_tensor(v, v, rz[:, :, :].unsqueeze(3).to_broadcast([P, NT, HEADS, HD]), ALU.mult).then_inc(s, 1)
                e.wait_ge(s, 3)
                e.tensor_tensor(k["X"][:, :, :], k["X"][:, :, :], acc[:, :, 0:D], ALU.add).then_inc(s, 1)


def route(nc, d, k):
    with ExitStack() as ctx:
        m = Mem(nc, ctx, "route")
        gb = m.sb("gb", [P, 2, 2])
        wr = m.sb("wr", [P, 2, NE])
        br = m.sb("br", [P, NE])
        b2 = m.sb("b2", [NE, D])
        xn = m.sb("xn", [P, 2, D])
        xt = m.sb("xt", [P, 2, D])
        lg = m.sb("lg", [P, NT, NE])
        top = m.sb("top", [P, NT, 8])
        idx = m.sb("idx", [P, NT, 8], U32)
        idf = m.sb("idf", [P, NT, 2])
        df, ed, ep, w0, w1 = (m.sb(n, [P, NT]) for n in ("df", "ed", "ep", "w0", "w1"))
        one = m.sb("one", [P, 2, NT, NE])
        wT = m.sb("wT", [NE, 2, P])
        ps_t = [m.ps(f"ps_t{i}", [P, 512]) for i in range(2)]
        ps_l = [m.ps(f"ps_l{i}", [P, 512]) for i in range(2)]
        S = m.sem
        loaded, xn_ok, t_ps, xt_ok, xc_ok, l_ps, lg_ok, top_ok, idx_ok, own, df_ok, ed_ok, wf_ok = (S(n) for n in (
            "loaded", "xn_ok", "t_ps", "xt_ok", "xc_ok", "l_ps", "lg_ok", "top_ok", "idx_ok", "own", "df_ok", "ed_ok", "wf_ok"))
        wt_ps, wt_ok, b_ps, x_ok = (S(n) for n in ("wt_ps", "wt_ok", "b_ps", "x_ok"))
        with nc.Block() as block:
            @block.sync
            def _(e):
                e.dma_start(gb[:, 0, :], d["gamma"]).then_inc(loaded, 16)
                e.dma_start(gb[:, 1, :], d["beta"]).then_inc(loaded, 16)
                e.dma_start(wr[:, :, :], d["Wr"].rearrange("(c p) n -> p c n", p=P)).then_inc(loaded, 16)
                e.dma_start(br[:, :], d["br"].to_broadcast([P, NE])).then_inc(loaded, 16)
                e.dma_start(b2[:, :], d["b2"]).then_inc(loaded, 16)
                e.dma_start(k["b1"][:, :, :], d["b1"]).then_inc(loaded, 16)
                e.wait_ge(loaded, 96)

            @block.vector
            def _(e):
                def norm(i, j):
                    wait(e, t_ps, i - 1)
                    e.tensor_scalar(xn[:, j, :], tile(k["X"], i), cols(k["mvf"], i * 2, 1), cols(k["rstd"], i, 1),
                                    ALU.subtract, ALU.mult).then_inc(xn_ok, 1)

                def body(i, j, it):
                    if not (isinstance(i, int) and i == NT - 1):
                        norm(i + 1, 1 - j)
                    e.wait_ge(t_ps, i + 1)
                    wait(e, l_ps, i - 1)
                    wait(e, xc_ok, i - 1)
                    for c in range(2):
                        e.tensor_scalar(xt[:, j, c * P:(c + 1) * P], ps_t[j][:, c * P:(c + 1) * P], gb[:, 0, c:c + 1],
                                        gb[:, 1, c:c + 1], ALU.mult, ALU.add).then_inc(xt_ok, 1)
                    e.wait_ge(l_ps, i + 1)
                    e.tensor_tensor(tile(lg, i), ps_l[j][:, 0:NE], br[:, :], ALU.add).then_inc(lg_ok, 1)
                e.wait_ge(loaded, 96)
                norm(0, 0)
                pairs(body)(e)
                n = [0]

                def link(ins):
                    ins.then_inc(own, 1)
                    n[0] += 1
                    e.wait_ge(own, n[0])
                e.wait_ge(lg_ok, NT)
                for i in range(NT):
                    e.max(top[:, i, :], lg[:, i, :]).then_inc(top_ok, 1)
                for i in range(NT):
                    e.wait_ge(top_ok, i + 1)
                    e.max_index(idx[:, i, :], top[:, i, :], lg[:, i, :]).then_inc(idx_ok, 1)
                e.wait_ge(idx_ok, NT)
                link(e.tensor_copy(idf[:, :, :], idx[:, :, 0:2]))
                e.tensor_tensor(df[:, :], top[:, :, 1], top[:, :, 0], ALU.subtract).then_inc(df_ok, 1)
                e.wait_ge(ed_ok, 1)
                link(e.tensor_scalar_add(ep[:, :], ed[:, :], 1.0))
                link(e.reciprocal(w0[:, :], ep[:, :]))
                link(e.tensor_tensor(w1[:, :], ed[:, :], w0[:, :], ALU.mult))
                for r, w in enumerate((w0, w1)):
                    hit = one[:, r, :, :]
                    link(e.tensor_tensor(hit, k["iota"][:, 0:NE].unsqueeze(1).to_broadcast([P, NT, NE]),
                                         idf[:, :, r].unsqueeze(2).to_broadcast([P, NT, NE]), ALU.is_equal))
                    link(e.tensor_tensor(hit, hit, w[:, :].unsqueeze(2).to_broadcast([P, NT, NE]), ALU.mult))
                e.tensor_tensor(k["wfull"][:, :, :], one[:, 0, :, :], one[:, 1, :, :], ALU.add).then_inc(wf_ok, 1)
                for i in range(NT):
                    e.wait_ge(b_ps, i + 1)
                    e.tensor_tensor(k["X"][:, i, :], k["X"][:, i, :], ps_l[i % 2][:, 256:256 + D], ALU.add).then_inc(x_ok, 1)

            @block.tensor
            def _(e):
                e.wait_ge(loaded, 96)

                def body(i, j, it):
                    e.wait_ge(xn_ok, i + 1)
                    wait(e, xt_ok, 2 * i - 2)
                    for c in range(2):
                        x = e.transpose(ps_t[j][:, c * P:(c + 1) * P], xn[:, j, c * P:(c + 1) * P], k["ident"][:, :])
                    x.then_inc(t_ps, 1)
                    e.wait_ge(xt_ok, 2 * i + 2)
                    wait(e, lg_ok, i - 1)
                    for c in range(2):
                        x = e.matmul(ps_l[j][:, 0:NE], xt[:, j, c * P:(c + 1) * P], wr[:, c, :], start=c == 0, stop=c == 1)
                    x.then_inc(l_ps, 1)
                pairs(body)(e)
                e.wait_ge(wf_ok, 1)
                for i in range(NT):
                    wait(e, wt_ok, i - 1)
                    e.transpose(ps_t[i % 2][0:NE, 0:P], k["wfull"][:, i, :], k["ident"][:, :]).then_inc(wt_ps, 1)
                    e.wait_ge(wt_ok, i + 1)
                    wait(e, x_ok, i - 1)
                    e.matmul(ps_l[i % 2][:, 256:256 + D], wT[:, i % 2, :], b2[:, :], start=True, stop=True).then_inc(b_ps, 1)

            @block.scalar
            def _(e):
                def body(i, j, it):
                    e.wait_ge(xt_ok, 2 * i + 2)
                    e.activation(cols(k["XNT"][0], i * P, P), xt[:, j, 0:P], ACT.Copy)
                    e.activation(cols(k["XNT"][1], i * P, P), xt[:, j, P:2 * P], ACT.Copy).then_inc(xc_ok, 1)
                pairs(body)(e)
                e.wait_ge(df_ok, 1)
                e.activation(ed[:, :], df[:, :], ACT.Exp).then_inc(ed_ok, 1)
                for i in range(NT):
                    e.wait_ge(wt_ps, i + 1)
                    wait(e, b_ps, i - 1)
                    e.activation(wT[:, i % 2, :], ps_t[i % 2][0:NE, 0:P], ACT.Copy).then_inc(wt_ok, 1)


BT = 5
NB = NT // BT
HC = HID // P


def experts(nc, d, k):
    with ExitStack() as ctx:
        m = Mem(nc, ctx, "experts")
        H = m.sb("H", [P, 2, HC, BT * P])
        ps_h = [m.ps(f"ps_h{i}", [P, 512]) for i in range(4)]
        ps_y = [m.ps(f"ps_y{i}", [P, 512]) for i in range(4)]
        h_ps, h_ok, y_ps, x_ok = (m.sem(n) for n in ("h_ps", "h_ok", "y_ps", "x_ok"))
        W1, W2 = k["W1"], k["W2"]
        half = BT * P // 2
        NH = 2 * HC
        with nc.Block() as block:
            @block.tensor
            def _(e):
                e.wait_ge(k["w_in"], 32)

                def up(n, q, batch, x):
                    for c in range(HC):
                        for h in range(2):
                            r = (2 * c + h) % 4
                            wait(e, h_ok, n * NH + 2 * c + h - 3)
                            for kc in range(2):
                                i = e.matmul(ps_h[r][:, 0:half], W1[:, x, kc, c * P:(c + 1) * P],
                                             cols(k["XNT"][kc], batch * (BT * P) + h * half, half), start=kc == 0, stop=kc == 1)
                            i.then_inc(h_ps, 1)

                def down(n, x):
                    for t in range(BT):
                        e.wait_ge(h_ok, n * NH + NH)
                        r = (x * BT + t) % 4
                        wait(e, x_ok, n * BT + t - 3)
                        for c in range(HC):
                            i = e.matmul(ps_y[r][:, 0:D], H[:, x % 2, c, t * P:(t + 1) * P], W2[:, x, c, :],
                                         start=c == 0, stop=c == HC - 1)
                        i.then_inc(y_ps, 1)

                rounds(e, lambda b, x: up(b * NE + x, x % 2, b, x), lambda b, x: down(b * NE + x, x))

            @block.scalar
            def _(e):
                def body(b):
                    for x in range(NE):
                        n = b * NE + x
                        for c in range(HC):
                            for h in range(2):
                                e.wait_ge(h_ps, n * NH + 2 * c + h + 1)
                                if c == 0 and h == 0:
                                    wait(e, y_ps, (n - 1) * BT)
                                e.activation(H[:, x % 2, c, h * half:(h + 1) * half], ps_h[(2 * c + h) % 4][:, 0:half],
                                             ACT.Gelu, bias=k["b1"][:, x, c:c + 1]).then_inc(h_ok, 1)
                rolled(e, NB, body)

            @block.vector
            def _(e):
                def body(b):
                    for x in range(NE):
                        n = b * NE + x
                        for t in range(BT):
                            r = (x * BT + t) % 4
                            e.wait_ge(y_ps, n * BT + t + 1)
                            wait(e, x_ok, n * BT + t - BT + 1)
                            X = tile(k["X"], b * BT + t)
                            w = cols(k["wflat"], (b * BT + t) * NE + x, 1)
                            e.scalar_tensor_tensor(X, ps_y[r][:, 0:D], w, X, ALU.mult, ALU.add).then_inc(x_ok, 1)
                rolled(e, NB, body)


def rounds(e, up, down):
    up(0, 0)

    def body(b, last=False):
        for x in range(NE):
            if x < NE - 1:
                up(b, x + 1)
            elif not last:
                up(b + 1, 0)
            down(b, x)
    body(0)
    with e.Fori(1, NB - 1) as b:
        body(b)
    body(NB - 1, last=True)


def write_x(nc, d, k):
    with nc.semaphore("out_done") as done, nc.Block() as block:
        @block.sync
        def _(e):
            full = NODES // P
            e.dma_start(d["out"][0:full * P, :].rearrange("(n p) c -> p n c", p=P), k["X"][:, 0:full, :]).then_inc(done, 16)
            e.dma_start(d["out"][full * P:NODES, :], k["X"][0:NODES - full * P, full, :]).then_inc(done, 16)
            e.wait_ge(done, 32)


def add_acc0(nc, k):
    with nc.semaphore("a0") as s, nc.Block() as block:
        @block.vector
        def _(e):
            X, acc = k["X"], k["acc0"]
            e.tensor_tensor(X[:, :, 0:64], X[:, :, 0:64], acc[:, :, 0:64], ALU.add)
            for m in range(3):
                e.tensor_tensor(X[:, :, 64 + m:256:3], X[:, :, 64 + m:256:3], acc[:, :, 64 + 64 * m:128 + 64 * m], ALU.add)
            e.engine_nop().then_inc(s, 1)


def build(nc, d, stop=99):
    with ExitStack() as ctx:
        m = Mem(nc, ctx, "k")
        k = {}
        for name, shape, dt in (("X", [P, NT, D], F32), ("iota", [P, NPAD], F32), ("ident", [P, P], F32),
                                ("dst_f", [P, ET], F32), ("src_i", [P, ET], I32), ("dst_i", [P, ET], I32),
                                ("walk_t", [1, 512], I32), ("walk_n", [1, 512], I32), ("walk_slot", [1, 512], I32),
                                ("tcol", [P, 4], F32), ("mv", [P, NT, 2], F32), ("rstd", [P, NT], F32)):
            k[name] = m.sb(name, shape, dt)
        k["mvf"] = k["mv"][:, :, :].rearrange("p n a -> p (n a)")
        with ExitStack() as c0:
            m0 = Mem(nc, c0, "l0")
            for name, shape in (("r", [P, ET, 3]), ("s2", [P, ET]), ("WH", [P, 128]), ("WO", [P, 192]),
                                ("LSC2", [P, 64]), ("blockww", [P, P])):
                k[name] = m0.sb(name, shape)
            setup(nc, d, k)
            moments(nc, k, "mom0")
            nodes0(nc, d, k)
            if stop > 0:
                k["acc0"] = m0.sb("acc0", [P, NT, D])
                edges0(nc, d, k)
                add_acc0(nc, k)
        if stop > 1:
            moments(nc, k, "mom1")
            lns(nc, d, k)
        if stop > 2:
            k["w_in"] = m.sem("w_in")
            moments(nc, k, "mom2")
            qkv(nc, d, k)
            with ExitStack() as c1:
                m1 = Mem(nc, c1, "l1")
                k["S"] = m1.sb("S", [P, ET * HEADS])
                scores(nc, d, k)
                softmax_shift(nc, d, k)
                k["acc1"] = m1.sb("acc1", [P, NT, D + HEADS])
                aggregate1(nc, d, k)
                add_acc1(nc, k)
        if stop > 3:
            moments(nc, k, "mom3")
            k["W1"] = m.sb("W1", [P, NE, 2, HID])
            k["W2"] = m.sb("W2", [P, NE, HC, D])
            k["b1"] = m.sb("b1", [P, NE, HC])
            k["XNT"] = [m.sb(f"XNT{c}", [P, NPAD]) for c in range(2)]
            k["wfull"] = m.sb("wfull", [P, NT, NE])
            k["wflat"] = k["wfull"][:, :, :].rearrange("p n x -> p (n x)")
            with nc.Block() as block:
                @block.sync
                def _(e):
                    e.dma_start(k["W1"][:, :, :, :], d["W1"].rearrange("x (c p) h -> p x c h", p=P)).then_inc(k["w_in"], 16)
                    e.dma_start(k["W2"][:, :, :, :], d["W2"].rearrange("x (c p) h -> p x c h", p=P)).then_inc(k["w_in"], 16)
            route(nc, d, k)
            experts(nc, d, k)
        write_x(nc, d, k)


def kernel(**a):
    import numpy as np
    import concourse.bacc as bacc
    from concourse.bass_utils import run_bass_kernel_spmd

    nc = bacc.Bacc("TRN2", target_bir_lowering=False, num_devices=1)
    f = {n: np.ascontiguousarray(v) for n, v in a.items()}
    g = lambda n: f["L0_gnn_" + n]
    pad = EPAD - EDGES
    src = np.pad(f["src"], (0, pad))
    dst = np.pad(f["dst"], (0, pad), constant_values=NPAD - 1)
    attr = np.pad(f["edge_attr_3"], ((0, pad), (0, 0)))
    arrays = {
        "x": np.pad(f["x"], ((0, NPAD - NODES), (0, 0))),
        "src_pt": src.reshape(ET, P).T, "dst_pt": dst.reshape(ET, P).T,
        "attr_pt": attr.reshape(ET, P, 3).transpose(1, 0, 2),
        "ls0T": g("lin_src_w0").T, "ls1T": g("lin_src_w1").T,
        "t00": g("tp1_w00"), "t11": g("tp1_w11"), "t01": g("tp1_w01"), "t10": g("tp1_w10"),
        "lh0": g("lin_hidden_w0"), "lh1": g("lin_hidden_w1"),
        "u00": g("tp2_w00"), "u11": g("tp2_w11"), "u01": g("tp2_w01"), "u10": g("tp2_w10"),
        "lsc": g("lin_scalar_w"),
        "lnsT": f["L0_ffn_weight"].T, "lns_b": f["L0_ffn_bias"].reshape(1, D),
        "wqkv": np.concatenate([f["L1_gnn_Wq"], f["L1_gnn_Wk"], f["L1_gnn_Wv"]], 1),
        "bqkv": np.concatenate([f["L1_gnn_bq"], f["L1_gnn_bk"], f["L1_gnn_bv"]])[None],
        "gamma": f["L1_ffn_gamma"].reshape(2, P).T, "beta": f["L1_ffn_beta"].reshape(2, P).T,
        "Wr": f["L1_ffn_Wr"], "br": f["L1_ffn_br"][None],
        "W1": f["L1_ffn_W1"], "b1": f["L1_ffn_b1"].reshape(NE, HID // P, P).transpose(2, 0, 1),
        "W2": f["L1_ffn_W2"], "b2": f["L1_ffn_b2"],
    }
    arrays = {n: np.ascontiguousarray(v) for n, v in arrays.items()}
    d = {n: nc.dram_tensor("in_" + n, v.shape, mybir.dt.from_np(v.dtype), kind="ExternalInput").ap()
         for n, v in arrays.items()}
    d["tab0"] = nc.dram_tensor("tab0", (NPAD, T0W), F32, kind="Internal").ap()
    for n in ("qtab", "ktab", "vtab"):
        d[n] = nc.dram_tensor(n, (NPAD, D), F32, kind="Internal").ap()
    d["out"] = nc.dram_tensor("out_x", (NODES, D), F32, kind="ExternalOutput").ap()
    build(nc, d, **OPTIONS)
    r = run_bass_kernel_spmd(nc, [{"in_" + n: v for n, v in arrays.items()}], core_ids=[0])
    return r.results[0]["out_x"]


OPTIONS = {}
```

```python
import concourse.bass as bass
from concourse import mybir
from contextlib import ExitStack

F32 = mybir.dt.float32
BF16 = mybir.dt.bfloat16
I32 = mybir.dt.int32
U32 = mybir.dt.uint32
ALU = mybir.AluOpType
ACT = mybir.ActivationFunctionType
AX = mybir.AxisListType

P = 128
NODES = 3125
NT = 25
NPAD = NT * P
D = 256
MUL = 64
EDGES = 50000
ET = 400
EPAD = ET * P
GT = 4
NG = ET // GT
UN = 4
NI = NG // UN
STEPS = ET + NT - 1
SB = -(-STEPS // GT)
RING = 32
T0W = 512
HEADS = 8
HD = 32
C = 1.0 / 8.0
TP = 1.0 / 128.0 ** 0.5
SQ3 = 3.0 ** 0.5
BIG = 3.0e38
NE = 8
HID = 512


def wait(e, sem, count):
    if not isinstance(count, int) or count > 0:
        e.wait_ge(sem, count)


def rolled(e, n, body, first=1, last=1):
    for i in range(first):
        body(i)
    with e.Fori(first, n - last) as i:
        body(i)
    for i in range(n - last, n):
        body(i)


def tile(t, i):
    if isinstance(i, int):
        return t[:, i, :]
    return t[:, bass.ds(i, 1), :].rearrange("p a w -> p (a w)")


def cols(t, i, w):
    return t[:, i:i + w] if isinstance(i, int) else t[:, bass.ds(i, w)]


def tiles(t, i, n):
    return t[:, i:i + n, :] if isinstance(i, int) else t[:, bass.ds(i, n), :]


class Mem:

    def __init__(self, nc, ctx, tag):
        self.nc, self.ctx, self.tag, self.sems = nc, ctx, tag, []
        ctx.callback(self.clear)

    def sb(self, name, shape, dt=F32):
        return self.ctx.enter_context(self.nc.sbuf_tensor(f"{self.tag}_{name}", shape, dt))

    def ps(self, name, shape, dt=F32):
        return self.ctx.enter_context(self.nc.psum_tensor(f"{self.tag}_{name}", shape, dt))

    def sem(self, name):
        self.sems.append(self.nc.alloc_semaphore(name=f"{self.tag}_{name}"))
        return self.sems[-1]

    def clear(self):
        if self.sems:
            self.nc.clear_and_free_semaphores(self.sems)
            self.nc.all_engine_barrier()


FW = EPAD // P
SC = 8
SE = EPAD // SC


def edges_in(nc, d, k):
    with ExitStack() as ctx:
        m = Mem(nc, ctx, "in")
        flat = m.sb("flat", [P, FW + 1], I32)
        drop = m.sb("drop", [P, FW])
        drops = m.sb("drops", [P, 1])
        ones = m.sb("ones", [P, 1])
        flag = m.sb("flag", [1, 1], I32)
        ps = m.ps("ps", [P, 512])
        loaded, cmp_ok, sum_ok, one_ok, tot, flag_ok = (m.sem(n) for n in (
            "loaded", "cmp_ok", "sum_ok", "one_ok", "tot", "flag_ok"))
        with nc.Block() as block:
            @block.sync
            def _(e):
                e.dma_start(flat[:, :], bass.AP(d["dst_flat"].tensor, 0, [[FW, P], [1, FW + 1]])).then_inc(loaded, 16)
                e.dma_start(k["dst_i"][:, :], d["dst_pt"]).then_inc(loaded, 16)
                e.dma_start(k["src_i"][:, :], d["src_pt"]).then_inc(loaded, 16)
                e.dma_start(k["attr"][:, :, :], d["attr_pt"]).then_inc(loaded, 16)
                e.wait_ge(loaded, 64)

            @block.vector
            def _(e):
                e.memset(ones[:, :], 1.0).then_inc(one_ok, 1)
                e.wait_ge(loaded, 64)
                e.tensor_tensor(drop[:, :], flat[:, 0:FW], flat[:, 1:FW + 1], ALU.is_gt).then_inc(cmp_ok, 1)
                e.wait_ge(cmp_ok, 1)
                e.tensor_reduce(drops[:, :], drop[:, :], AX.X, ALU.add).then_inc(sum_ok, 1)
                e.wait_ge(tot, 1)
                e.tensor_copy(flag[:, :], ps[0:1, 0:1]).then_inc(flag_ok, 1)

            @block.tensor
            def _(e):
                e.wait_ge(one_ok, 1)
                e.wait_ge(sum_ok, 1)
                e.matmul(ps[0:1, 0:1], drops[:, :], ones[:, :], start=True, stop=True).then_inc(tot, 1)
        sort_edges(nc, d, k, flag)


def sort_edges(nc, d, k, flag):
    with ExitStack() as ctx:
        m = Mem(nc, ctx, "sort")
        raw = m.sb("raw", [P, SE], I32)
        keys = m.sb("keys", [P, SE])
        tno = m.sb("tno", [P, SE])
        junk = m.sb("junk", [P, SE])
        key = m.sb("key", [P, ET])
        part = m.sb("part", [P, SC + 1, ET])
        rank_f = m.sb("rank_f", [P, ET])
        rank = m.sb("rank", [P, ET], I32)
        tri = m.sb("tri", [P, P])
        junk2 = m.sb("junk2", [P, P])
        tcol = m.sb("tcol", [P, ET])
        rows = m.sb("rows", [P, ET, 8], I32)
        row = m.sb("row", [P, 8], I32)
        at = m.sb("at", [P, 1], I32)
        scr = m.sb("scr", [P, 2])
        S = m.sem
        raw_in, keyed, tied, counted, ranked, made, staged, carried, put, back, own = (S(n) for n in (
            "raw_in", "keyed", "tied", "counted", "ranked", "made", "staged", "carried", "put", "back", "own"))
        with nc.Block() as block:
            @block.gpsimd
            def _(e):
                unsorted = e.value_load(flag[0:1, 0:1], min_val=0, max_val=EPAD)
                with e.If(unsorted > 0):
                    e.memset(scr[:, :], 0.0).then_inc(carried, 1)
                    e.memset(tri[:, :], 1.0).then_inc(made, 1)
                    e.wait_ge(made, 1)
                    e.affine_select(out=tri[:, :], in_=tri[:, :], compare_op=ALU.is_gt, fill=0.0, base=0,
                                    pattern=[[-1, P]], channel_multiplier=1).then_inc(made, 1)
                    e.iota(tcol[:, :], pattern=[[1, ET]], base=0, channel_multiplier=0,
                           allow_small_or_imprecise_dtypes=True).then_inc(made, 1)
                    for c in range(SC):
                        wait(e, counted, c)
                        e.dma_start(raw[:, :], d["dst_flat"][0:1, c * SE:(c + 1) * SE].to_broadcast([P, SE])
                                    ).then_inc(raw_in, 16)
                        e.iota(tno[:, :], pattern=[[1, SE // P], [0, P]], base=c * (SE // P), channel_multiplier=0,
                               allow_small_or_imprecise_dtypes=True).then_inc(made, 1)
                    e.wait_ge(ranked, 1)

                    def scatter(t):
                        wait(e, put, t * 16)
                        e.wait_ge(carried, 2 * t + 1)
                        e.tensor_tensor(scr[:, 0:1], scr[:, 1:2], scr[:, 1:2], ALU.add).then_inc(carried, 1)
                        e.tensor_copy(row[:, :], tile(rows, t)).then_inc(staged, 1)
                        e.tensor_copy(at[:, :], cols(rank, t, 1)).then_inc(staged, 1)
                        e.wait_ge(staged, 2 * t + 2)
                        e.wait_ge(carried, 2 * t + 2)
                        e.tensor_tensor(scr[:, 0:1], scr[:, 1:2], scr[:, 1:2], ALU.add).then_inc(carried, 1)
                        e.indirect_dma_start(out=d["sorted"], out_offset=bass.IndirectOffsetOnAxis(ap=at[:, :], axis=0),
                                             in_=row[:, :], in_offset=None).then_inc(put, 16)
                    rolled(e, ET, scatter)
                    e.wait_ge(put, ET * 16)
                    for c in range(SC):
                        w = ET // SC
                        e.dma_start(rows[:, c * w:(c + 1) * w, :],
                                    d["sorted"][c * SE:(c + 1) * SE, :].rearrange("(t p) c -> p t c", p=P)).then_inc(back, 16)
                        e.wait_ge(back, 16 * (c + 1))

            @block.vector
            def _(e):
                unsorted = e.value_load(flag[0:1, 0:1], min_val=0, max_val=EPAD)
                with e.If(unsorted > 0):
                    n = [0]

                    def link(ins):
                        ins.then_inc(own, 1)
                        n[0] += 1
                        e.wait_ge(own, n[0])
                    e.wait_ge(made, 3)
                    link(e.scalar_tensor_tensor(key[:, :], k["dst_i"][:, :], 512.0, tcol[:, :], ALU.mult, ALU.add))
                    for c in range(SC):
                        e.wait_ge(raw_in, (c + 1) * 16)
                        e.wait_ge(made, c + 4)
                        e.scalar_tensor_tensor(keys[:, :], raw[:, :], 512.0, tno[:, :], ALU.mult, ALU.add).then_inc(keyed, 1)
                        e.wait_ge(keyed, c + 1)

                        def count(t, c=c):
                            e.wait_ge(tied, t + 1 + c * (ET + SE // P))
                            e.tensor_scalar(junk[:, :], keys[:, :], cols(key, t, 1), 0.0, ALU.is_lt, ALU.add,
                                            accum_out=cols(part[:, c, :], t, 1)).then_inc(tied, 1)
                        if c == 0:
                            e.memset(junk2[:, :], 0.0).then_inc(tied, 1)
                        rolled(e, ET, count)

                        def tie(i, c=c):
                            e.wait_ge(tied, i + 1 + ET + c * (ET + SE // P))
                            e.scalar_tensor_tensor(junk2[:, :], cols(keys, i * P, P), cols(key, i + c * (SE // P), 1), tri[:, :],
                                                   ALU.is_equal, ALU.mult,
                                                   accum_out=cols(part[:, SC, :], i + c * (SE // P), 1)).then_inc(tied, 1)
                        rolled(e, SE // P, tie)
                        e.wait_ge(tied, 1 + (c + 1) * (ET + SE // P))
                        e.memset(junk2[:, 0:1], 0.0).then_inc(counted, 1)
                        e.wait_ge(counted, c + 1)
                    link(e.tensor_reduce(rank_f[:, :], part[:, :, :].rearrange("p c t -> p t c"), AX.X, ALU.add))
                    link(e.tensor_copy(rank[:, :], rank_f[:, :]))
                    link(e.memset(rows[:, :, :], 0))
                    link(e.tensor_copy(rows[:, :, 0:1], k["src_i"][:, :].unsqueeze(2)))
                    link(e.tensor_copy(rows[:, :, 1:2], k["dst_i"][:, :].unsqueeze(2)))
                    e.tensor_copy(rows[:, :, 2:5].bitcast(F32), k["attr"][:, :, :]).then_inc(ranked, 1)
                    e.wait_ge(back, 16 * SC)
                    link(e.tensor_copy(k["src_i"][:, :].unsqueeze(2), rows[:, :, 0:1]))
                    link(e.tensor_copy(k["dst_i"][:, :].unsqueeze(2), rows[:, :, 1:2]))
                    link(e.tensor_copy(k["attr"][:, :, :], rows[:, :, 2:5].bitcast(F32)))


def setup(nc, d, k):
    with ExitStack() as ctx:
        m = Mem(nc, ctx, "setup")
        w = m.sb("w", [64, 13, 64])
        a = m.sb("a", [64, 4, 64])
        wt = m.sb("wt", [64, 7, 64])
        dst_i = k["dst_i"]
        tile_i = m.sb("tile_i", [P, ET], I32)
        tile_f = m.sb("tile_f", [P, ET])
        last_row = m.sb("last_row", [P, P])
        ends = m.sb("ends", [P, ET])
        hit = m.sb("hit", [P, ET])
        step_tile = m.sb("step_tile", [P, 4])
        tcol = m.sb("tcol", [P, 4])
        tbc = m.sb("tbc", [P, 4, P])
        nbase = m.sb("nbase", [P, 512])
        walk_i = m.sb("walk_i", [1, 512], I32)
        dT = m.sb("dT", [P, 4, P])
        pick = m.sb("pick", [P, 4, 512])
        attr = k["attr"]
        sq = m.sb("sq", [P, ET, 3])
        norm = m.sb("norm", [P, ET])
        norm2 = m.sb("norm2", [P, ET])
        inv = m.sb("inv", [P, ET])
        ia = m.sb("ia", [P, 512], I32)
        ps_w = m.ps("ps_w", [P, 512])
        ps_o = m.ps("ps_o", [P, 512])
        ps_e = m.ps("ps_e", [P, 512])
        ps_r = m.ps("ps_r", [P, 512])
        ps_d = m.ps("ps_d", [P, 512])
        ps_k = m.ps("ps_k", [P, 512])
        w_in, x_in = m.sem("w_in"), m.sem("x_in")
        made, iota_ok = m.sem("made"), m.sem("iota_ok")
        pe1, ev1, pe2, ev2, pe3, ev3 = (m.sem(n) for n in ("pe1", "ev1", "pe2", "ev2", "pe3", "ev3"))
        sq_ok, sqrt_ok, chain, walk, walk_pe = (m.sem(n) for n in ("sq_ok", "sqrt_ok", "chain", "walk", "walk_pe"))
        names = ["ls0T", "ls1T", "t00", "t11", "t01", "t10", "lh0", "lh1", "u00", "u11", "u01", "u10"]
        W = {n: w[:, i, :] for i, n in enumerate(names)}
        with nc.Block() as block:
            @block.sync
            def _(e):
                e.dma_start(k["X"][:, :, :], d["x"].rearrange("(n p) c -> p n c", p=P)).then_inc(x_in, 16)
                e.wait_ge(x_in, 16)

            @block.scalar
            def _(e):
                for i, n in enumerate(names):
                    e.dma_start(w[:, i, :], d[n]).then_inc(w_in, 16)
                e.dma_start(k["LSC2"][0:64, :], d["lsc"]).then_inc(w_in, 16)
                e.dma_start(k["LSC2"][64:128, :], d["lsc"]).then_inc(w_in, 16)
                e.wait_ge(w_in, 14 * 16)
                e.wait_ge(chain, 2)
                e.activation(norm[:, :], norm2[:, :], ACT.Sqrt).then_inc(sqrt_ok, 1)

            @block.gpsimd
            def _(e):
                e.iota(k["iota"][:, :], pattern=[[1, 512]], base=0, channel_multiplier=0,
                       allow_small_or_imprecise_dtypes=True).then_inc(iota_ok, 1)
                e.memset(k["ident"][:, :], 0.0).then_inc(made, 1)
                e.memset(last_row[:, :], 0.0).then_inc(made, 1)
                e.memset(wt[:, :, :], 0.0).then_inc(made, 1)
                e.memset(k["blockww"][:, :], 0.0).then_inc(made, 1)
                e.wait_ge(made, 2)
                e.affine_select(out=k["ident"][:, :], in_=k["ident"][:, :], compare_op=ALU.not_equal, fill=1.0,
                                base=0, pattern=[[-1, P]], channel_multiplier=1).then_inc(made, 1)
                e.affine_select(out=last_row[:, :], in_=last_row[:, :], compare_op=ALU.not_equal, fill=1.0,
                                base=-(P - 1), pattern=[[0, P]], channel_multiplier=1).then_inc(made, 1)
                e.iota(step_tile[:, :], pattern=[[P, 4]], base=0, channel_multiplier=1,
                       allow_small_or_imprecise_dtypes=True).then_inc(made, 1)

            @block.vector
            def _(e):
                n = [0]

                def link(ins):
                    ins.then_inc(chain, 1)
                    n[0] += 1
                    e.wait_ge(chain, n[0])
                link(e.tensor_tensor(sq[:, :, :], attr[:, :, :], attr[:, :, :], ALU.mult))
                link(e.tensor_reduce(norm2[:, :], sq[:, :, :], AX.X, ALU.add))
                link(e.tensor_copy(k["dst_f"][:, :], dst_i[:, :]))
                link(e.tensor_single_scalar(tile_i[:, :], dst_i[:, :], 7, ALU.arith_shift_right))
                link(e.tensor_copy(tile_f[:, :], tile_i[:, :]))
                e.wait_ge(sqrt_ok, 1)
                link(e.tensor_scalar_add(norm2[:, :], norm[:, :], 1e-12))
                link(e.reciprocal(inv[:, :], norm2[:, :]))
                link(e.tensor_tensor(k["r"][:, :, :], attr[:, :, :],
                                     inv[:, :].unsqueeze(2).to_broadcast([P, ET, 3]), ALU.mult))
                link(e.tensor_tensor(sq[:, :, :], k["r"][:, :, :], k["r"][:, :, :], ALU.mult))
                link(e.tensor_reduce(k["s2"][:, :], sq[:, :, :], AX.X, ALU.add))
                e.wait_ge(walk_pe, 1)
                e.wait_ge(iota_ok, 1)
                e.wait_ge(made, 7)
                link(e.scalar_tensor_tensor(ends[:, :], ps_r[:, 0:ET], 1.0, k["iota"][:, 0:ET], ALU.add, ALU.add))
                for c in range(4):
                    link(e.tensor_scalar(hit[:, :], ends[:, :], step_tile[:, c:c + 1], 0.0, ALU.is_le, ALU.add,
                                         accum_out=tcol[:, c:c + 1]))
                e.tensor_copy(tbc[:, :, :], tcol[:, :].unsqueeze(2).to_broadcast([P, 4, P])).then_inc(walk, 1)
                e.wait_ge(walk_pe, 2)
                link(e.tensor_copy(walk_i[:, :], ps_e[0:1, :]))
                link(e.tensor_tensor(k["walk_n"][:, :], k["iota"][0:1, :], ps_e[0:1, :], ALU.subtract))
                link(e.tensor_single_scalar(k["walk_slot"][:, :], walk_i[:, :], RING - 1, ALU.bitwise_and))
                link(e.tensor_tensor(nbase[:, :], k["iota"][:, :], ps_e[:, :], ALU.subtract))
                for c in range(4):
                    link(e.tensor_scalar(pick[:, c, :], ps_e[:, :], step_tile[:, c:c + 1], None, ALU.is_equal))
                e.wait_ge(walk_pe, 3)
                for c in range(4):
                    w = min(P, ET - c * P)
                    link(e.tensor_copy(dT[0:w, c, :], ps_d[0:w, c * P:(c + 1) * P]))
                e.engine_nop().then_inc(walk, 1)
                e.wait_ge(walk_pe, 4)
                link(e.scalar_tensor_tensor(k["dstep"][:, :], nbase[:, :], -float(P), ps_k[:, :], ALU.mult, ALU.add))
                e.wait_ge(pe1, 1)
                e.tensor_copy(a[:, :, :], ps_w[0:64, 0:256].rearrange("p (a b) -> p a b", a=4)).then_inc(ev1, 1)
                e.wait_ge(pe2, 1)
                s = C * TP * C
                e.tensor_scalar_mul(wt[:, 0:2, :], ps_w[0:64, 256:384].rearrange("p (a b) -> p a b", a=2), s)
                e.tensor_scalar_mul(wt[:, 5, :], ps_w[0:64, 384:448], s)
                e.tensor_scalar_mul(wt[:, 3, :], ps_w[0:64, 448:512], s)
                e.tensor_scalar_mul(wt[:, 4, :], ps_w[0:64, 448:512], s).then_inc(ev2, 1)
                e.wait_ge(pe3, 1)
                e.tensor_copy(k["WH"][:, 0:64], ps_o[:, 0:64])
                e.tensor_scalar_mul(k["WH"][:, 64:128], ps_o[:, 0:64], -0.01)
                e.tensor_scalar_mul(k["WO"][:, 0:64], ps_o[:, 64:128], TP)
                e.tensor_scalar_mul(k["WO"][:, 64:128], ps_o[:, 128:192], SQ3 * TP)
                e.tensor_scalar_mul(k["WQ"][:, :], ps_o[0:64, 192:256], SQ3 * TP)
                e.tensor_scalar_mul(k["blockww"][0:64, 0:64], ps_o[0:64, 256:320], TP)
                e.tensor_scalar_mul(k["blockww"][64:128, 64:128], ps_o[64:128, 256:320], TP)
                e.wait_ge(w_in, 14 * 16)
                e.tensor_scalar_mul(k["LSC2"][0:64, :], k["LSC2"][0:64, :], C)
                e.tensor_scalar_mul(k["LSC2"][64:128, :], k["LSC2"][64:128, :], -C).then_inc(ev3, 1)

            @block.tensor
            def _(e):
                e.wait_ge(made, 7)
                e.wait_ge(chain, 5)
                e.matmul(ps_r[:, 0:ET], last_row[:, :], tile_f[:, :], start=True, stop=True).then_inc(walk_pe, 1)
                e.wait_ge(walk, 1)
                for c in range(4):
                    x = e.matmul(ps_e[:, c * P:(c + 1) * P], tbc[:, c, :], k["ident"][:, :], start=True, stop=True)
                x.then_inc(walk_pe, 1)
                for c in range(4):
                    w = min(P, ET - c * P)
                    x = e.transpose(ps_d[0:w, c * P:(c + 1) * P], k["dst_f"][:, c * P:c * P + w], k["ident"][:, :])
                x.then_inc(walk_pe, 1)
                e.wait_ge(walk, 2)
                for c in range(4):
                    w = min(P, ET - c * P)
                    x = e.matmul(ps_k[:, :], dT[0:w, c, :], pick[0:w, c, :], start=c == 0, stop=c == 3)
                x.then_inc(walk_pe, 1)
                e.wait_ge(w_in, 14 * 16)
                for i, (l, r) in enumerate((("t00", "ls0T"), ("t11", "ls1T"), ("t01", "ls0T"), ("t10", "ls1T"))):
                    x = e.matmul(ps_w[0:64, i * 64:i * 64 + 64], W[l], W[r], start=True, stop=True)
                x.then_inc(pe1, 1)
                e.wait_ge(ev1, 1)
                for i, l in enumerate(("lh0", "lh0", "lh1", "lh1")):
                    x = e.matmul(ps_w[0:64, 256 + i * 64:320 + i * 64], W[l], a[:, i, :], start=True, stop=True)
                x.then_inc(pe2, 1)
                e.wait_ge(ev2, 1)
                pair = lambda i: wt[:, i:i + 2, :].rearrange("p a b -> p (a b)")
                e.matmul(ps_o[:, 0:64], pair(0), k["ident"][0:64, 0:64], start=True, stop=True)
                e.matmul(ps_o[:, 64:128], pair(0), W["u00"], start=True, stop=False)
                e.matmul(ps_o[:, 64:128], pair(2), W["u11"], start=False, stop=True)
                e.matmul(ps_o[:, 128:192], pair(0), W["u01"], start=True, stop=False)
                e.matmul(ps_o[:, 128:192], pair(5), W["u10"], start=False, stop=True)
                e.matmul(ps_o[:, 192:256], pair(5), W["u11"], start=True, stop=True)
                e.matmul(ps_o[:, 256:320], pair(3), W["u10"], start=True, stop=True).then_inc(pe3, 1)


def moments(nc, k, tag):
    with ExitStack() as ctx:
        m = Mem(nc, ctx, tag)
        stats = m.sb("stats", [P, NT, 6])
        var = m.sb("var", [P, NT])
        root = m.sb("root", [P, NT])
        st, mv, ve, sq = m.sem("st"), m.sem("mv"), m.sem("ve"), m.sem("sq")
        with nc.Block() as block:
            @block.vector
            def _(e):
                def stat(i):
                    e.bn_stats(tile(stats, i), tile(k["X"], i)).then_inc(st, 1)
                rolled(e, NT, stat)

                def aggr(i):
                    wait(e, st, NT)
                    e.bn_aggr(tile(k["mv"], i), tile(stats, i)).then_inc(mv, 1)
                for i in range(NT):
                    aggr(i)
                e.wait_ge(mv, NT)
                e.tensor_scalar_add(var[:, :], k["mv"][:, :, 1], 1e-5).then_inc(ve, 1)
                e.wait_ge(sq, 1)
                e.reciprocal(k["rstd"][:, :], root[:, :]).then_inc(ve, 1)

            @block.scalar
            def _(e):
                e.wait_ge(ve, 1)
                e.activation(root[:, :], var[:, :], ACT.Sqrt).then_inc(sq, 1)


def nodes0(nc, d, k):
    with ExitStack() as ctx:
        m = Mem(nc, ctx, "nodes0")
        row = m.sb("row", [P, 2, T0W])
        tt = m.sb("tt", [P, 2, 384])
        ps_t = m.ps("ps_t", [P, 2, 512])
        ps_y = m.ps("ps_y", [P, 2, 512])
        normed, added, t_ps, t_sb, y_ps, y_sb = (m.sem(n) for n in ("normed", "added", "t_ps", "t_sb", "y_ps", "y_sb"))
        stored = [m.sem(f"stored{i}") for i in range(2)]
        table = d["tab0"].rearrange("(n p) c -> n p c", p=P)

        def both(e, body):
            for i in range(2):
                body(i, i, 0)
            with e.Fori(1, 11) as it:
                for j in range(2):
                    body(it * 2 + j, j, it)
            for i in range(22, NT):
                body(i, i % 2, i // 2)

        with nc.Block() as block:
            @block.vector
            def _(e):
                def body(i, j, it):
                    wait(e, stored[j], it * 16)
                    X = tile(k["X"], i)
                    mean = cols(k["mvf"], i * 2, 1)
                    rs = cols(k["rstd"], i, 1)
                    e.tensor_scalar(row[:, j, 0:64], X[:, 0:64], mean, rs, ALU.subtract, ALU.mult).then_inc(normed, 1)
                    e.tensor_scalar(row[:, j, 64:256].rearrange("p (m u) -> p u m", m=3),
                                    X[:, 64:256].rearrange("p (u m) -> p u m", m=3),
                                    mean, rs, ALU.subtract, ALU.mult).then_inc(normed, 1)
                    e.wait_ge(normed, i * 2 + 2)
                    e.tensor_tensor(X[:, 0:64], X[:, 0:64], row[:, j, 0:64], ALU.add)
                    e.tensor_tensor(X[:, 64:256].rearrange("p (u m) -> p u m", m=3),
                                    X[:, 64:256].rearrange("p (u m) -> p u m", m=3),
                                    row[:, j, 64:256].rearrange("p (m u) -> p u m", m=3), ALU.add).then_inc(added, 1)
                both(e, body)

            @block.tensor
            def _(e):
                def body(i, j, it):
                    e.wait_ge(normed, i * 2 + 2)
                    wait(e, t_sb, i - 1)
                    e.transpose(ps_t[:, j, 0:128], row[:, j, 64:192], k["ident"][:, :])
                    e.transpose(ps_t[0:64, j, 128:256], row[:, j, 192:256], k["ident"][:, :])
                    e.transpose(ps_t[0:64, j, 256:384], row[:, j, 0:64], k["ident"][:, :]).then_inc(t_ps, 1)
                    e.wait_ge(t_sb, i + 1)
                    wait(e, y_sb, i - 1)
                    e.matmul(ps_y[:, j, 0:128], tt[:, j, 0:128], k["blockww"][:, :], start=True, stop=True)
                    e.matmul(ps_y[:, j, 128:192], tt[0:64, j, 128:256], k["blockww"][0:64, 0:64], start=True, stop=True)
                    e.matmul(ps_y[:, j, 192:256], tt[0:64, j, 256:384], k["WQ"][:, :], start=True, stop=True).then_inc(y_ps, 1)
                both(e, body)

            @block.scalar
            def _(e):
                def body(i, j, it):
                    e.wait_ge(t_ps, i + 1)
                    wait(e, y_ps, i - 1)
                    e.activation(tt[:, j, 0:128], ps_t[:, j, 0:128], ACT.Copy)
                    e.activation(tt[0:64, j, 128:384], ps_t[0:64, j, 128:384], ACT.Copy).then_inc(t_sb, 1)
                    e.wait_ge(y_ps, i + 1)
                    e.wait_ge(normed, i * 2 + 2)
                    e.activation(row[:, j, 256:512], ps_y[:, j, 0:256], ACT.Copy).then_inc(y_sb, 1)
                both(e, body)

            @block.sync
            def _(e):
                def body(i, j, it):
                    e.wait_ge(y_sb, i + 1)
                    e.wait_ge(normed, i * 2 + 2)
                    src = row[:, j, :]
                    dst = table[i, :, :] if isinstance(i, int) else table[bass.ds(i, 1), :, :].rearrange("a p c -> (a p) c")
                    e.dma_start(dst, src).then_inc(stored[j], 16)
                both(e, body)
                e.wait_ge(stored[0], 13 * 16)
                e.wait_ge(stored[1], 12 * 16)


def walk_values(nc, e, k, name, blk):
    at = k[name][0:1, blk * GT:blk * GT + GT] if isinstance(blk, int) else k[name][0:1, bass.ds(blk * GT, GT)]
    top = {"walk_n": NT - 1, "walk_slot": RING - 1}[name]
    return nc.values_load_multi_w_load_instructions(
        at, engines=(e.engine,), min_val=0, max_val=top, skip_runtime_bounds_check_because=WALK)[1]


WALK = "the walk visits each edge tile and each node tile in order, in as many steps as it has"


def one_hots(e, k, hot, blk):
    return e.tensor_tensor(hot, k["iota"][:, 0:P].unsqueeze(1).to_broadcast([P, GT, P]),
                           cols(k["dstep"], blk * GT, GT).unsqueeze(2).to_broadcast([P, GT, P]), ALU.is_equal)


def gathers(e, scr, carried, staged, landed, tables, used):
    e.memset(scr[:, :], 0.0).then_inc(carried, 1)
    n = len(tables)

    def carry(count):
        e.wait_ge(carried, count + 1)
        e.tensor_tensor(scr[:, 0:1], scr[:, 1:2], scr[:, 1:2], ALU.add).then_inc(carried, 1)

    def body(it):
        for b in range(UN):
            g = it * UN + b
            for sem, count in used(g):
                wait(e, sem, count)
            wait(e, landed[b], it * 16 * GT * n)
            carry(2 * g)
            for _, index, stage, _ in tables:
                e.tensor_copy(stage[:, b, :], cols(index, g * GT, GT)).then_inc(staged, 1)
            e.wait_ge(staged, (g + 1) * n)
            carry(2 * g + 1)
            for j in range(GT):
                for table, _, stage, buffer in tables:
                    e.indirect_dma_start(out=buffer(b, j), out_offset=None, in_=table,
                                         in_offset=bass.IndirectOffsetOnAxis(ap=stage[:, b, j:j + 1], axis=0)
                                         ).then_inc(landed[b], 16)
    rolled(e, NI, body)


def edges0(nc, d, k):
    with ExitStack() as ctx:
        m = Mem(nc, ctx, "edges0")
        G = m.sb("G", [P, UN, GT, T0W])
        stage = m.sb("stage", [P, UN, GT], I32)
        scr = m.sb("scr", [P, 2])
        ring = m.sb("ring", [P, RING, D])
        xm = m.sb("xm", [P, GT, 3, 64])
        xs = m.sb("xs", [P, GT, 64])
        XT = m.sb("XT", [P, 2, GT * P])
        HT = m.sb("HT", [P, 2, GT * P])
        mx = m.sb("mx", [P, GT])
        nm = m.sb("nm", [P, GT])
        ex = m.sb("ex", [P, GT, 64])
        en, zs, z, rz, enr = (m.sb(n, [P, GT]) for n in ("en", "zs", "z", "rz", "enr"))
        rr = m.sb("rr", [P, GT, 3])
        o0 = m.sb("o0", [P, GT, 64])
        o1 = m.sb("o1", [P, GT, 3, 64])
        hot = m.sb("hot", [P, 2, GT, P])
        ps_x = m.ps("ps_x", [P, GT * P])
        ps_h = m.ps("ps_h", [P, GT * P])
        ps_p = m.ps("ps_p", [P, GT * P])
        ps_s = m.ps("ps_s", [P, 512])
        ps_a = [m.ps(f"ps_a{i}", [P, 512]) for i in range(GT)]
        S = m.sem
        landed = [S(f"landed{i}") for i in range(UN)]
        staged, xm_ok, xs_ok, xr_ok, xt_ps, xt_sb, h_ps, h_sb, p_ps, sc_ps = (S(n) for n in (
            "staged", "xm_ok", "xs_ok", "xr_ok", "xt_ps", "xt_sb", "h_ps", "h_sb", "p_ps", "sc_ps"))
        mx_ok, nm_ok, ex_ok, en_ok, z_ok, rz_ok, enr_ok, rr_ok, o0_ok, o1_ok, m0_ok, m1_ok = (S(n) for n in (
            "mx_ok", "nm_ok", "ex_ok", "en_ok", "z_ok", "rz_ok", "enr_ok", "rr_ok", "o0_ok", "o1_ok", "m0_ok", "m1_ok"))
        hot_ok, sum_ps, acc_ok, scr_ok = (S(n) for n in ("hot_ok", "sum_ps", "acc_ok", "scr_ok"))
        acc = k["acc0"]
        four = lambda t: t[:, 0:GT * P].rearrange("p (t c) -> p t c", t=GT)

        with nc.Block() as block:
            @block.gpsimd
            def _(e):
                gathers(e, scr, scr_ok, staged, landed,
                        [(d["tab0"], k["src_i"], stage, lambda b, j: G[:, b, j, :])],
                        lambda g: [(m1_ok, g - UN + 1), (xt_ps, g - UN + 1)])

            @block.vector
            def _(e):
                e.memset(acc[:, :, :], 0.0).then_inc(acc_ok, 1)
                e.wait_ge(acc_ok, 1)

                def direct(g, b, it):
                    e.wait_ge(landed[b], (it + 1) * 16 * GT)
                    x1 = G[:, b, :, 64:256].rearrange("p t (m u) -> p t m u", m=3)
                    r = tiles(k["r"], g * GT, GT).unsqueeze(3).to_broadcast([P, GT, 3, 64])
                    wait(e, xr_ok, g)
                    e.tensor_tensor(xm[:, :, :, :], x1, r, ALU.mult).then_inc(xm_ok, 1)
                    e.wait_ge(xm_ok, g + 1)
                    e.tensor_tensor(xs[:, :, :], xm[:, :, 0, :], xm[:, :, 1, :], ALU.add).then_inc(xs_ok, 1)
                    e.wait_ge(xs_ok, g + 1)
                    e.tensor_tensor(G[:, b, :, 64:128], xs[:, :, :], xm[:, :, 2, :], ALU.add).then_inc(xr_ok, 1)

                def largest(g):
                    e.wait_ge(sc_ps, g + 1)
                    wait(e, nm_ok, g)
                    sc = ps_s[:, 0:GT * 64].rearrange("p (t c) -> p t c", t=GT)
                    e.tensor_reduce(mx[:, :], sc, AX.X, ALU.max).then_inc(mx_ok, 1)
                    e.wait_ge(mx_ok, g + 1)
                    wait(e, en_ok, g)
                    wait(e, ex_ok, g)
                    e.tensor_scalar(nm[:, :], mx[:, :], -1.0, 0.0, ALU.mult, ALU.min).then_inc(nm_ok, 1)

                def messages(g, b):
                    e.wait_ge(p_ps, g + 1)
                    wait(e, m0_ok, g)
                    for i in range(GT):
                        x = e.scalar_tensor_tensor(o0[:, i, :], G[:, b, i, 448:512], cols(k["s2"], g * GT + i, 1),
                                                   four(ps_p)[:, i, 0:64], ALU.mult, ALU.add)
                    x.then_inc(o0_ok, 1)
                    e.wait_ge(en_ok, g + 1)
                    e.wait_ge(ex_ok, g + 1)
                    wait(e, rz_ok, g)
                    e.scalar_tensor_tensor(z[:, :], en[:, :], 192.0, zs[:, :], ALU.mult, ALU.add).then_inc(z_ok, 1)
                    e.wait_ge(z_ok, g + 1)
                    e.reciprocal(rz[:, :], z[:, :]).then_inc(rz_ok, 1)
                    e.wait_ge(rz_ok, g + 1)
                    wait(e, m1_ok, g)
                    e.tensor_tensor(enr[:, :], en[:, :], rz[:, :], ALU.mult).then_inc(enr_ok, 1)
                    slot = (g % (RING // GT)) * GT
                    e.wait_ge(o0_ok, g + 1)
                    for i in range(GT):
                        x = e.scalar_tensor_tensor(tile(ring, slot + i)[:, 0:64], o0[:, i, :], rz[:, i:i + 1], ex[:, i, :],
                                                   ALU.mult, ALU.mult)
                        if i == 0:
                            e.wait_ge(enr_ok, g + 1)
                            e.tensor_tensor(rr[:, :, :], tiles(k["r"], g * GT, GT),
                                            enr[:, :].unsqueeze(2).to_broadcast([P, GT, 3]), ALU.mult).then_inc(rr_ok, 1)
                    x.then_inc(m0_ok, 1)
                    e.wait_ge(rr_ok, g + 1)
                    e.tensor_tensor(o1[:, :, :, :], four(ps_p)[:, :, 64:128].unsqueeze(2).to_broadcast([P, GT, 3, 64]),
                                    rr[:, :, :].unsqueeze(3).to_broadcast([P, GT, 3, 64]), ALU.mult).then_inc(o1_ok, 1)
                    e.wait_ge(o1_ok, g + 1)
                    for i in range(GT):
                        x = e.scalar_tensor_tensor(tile(ring, slot + i)[:, 64:256], G[:, b, i, 256:448], enr[:, i:i + 1],
                                                   o1[:, i, :, :].rearrange("p m u -> p (m u)"), ALU.mult, ALU.add)
                    x.then_inc(m1_ok, 1)

                def hots(blk, b):
                    wait(e, sum_ps, (blk - 1) * GT)
                    one_hots(e, k, hot[:, b % 2, :, :], blk).then_inc(hot_ok, 1)

                def add(blk, j, n):
                    e.wait_ge(sum_ps, blk * GT + j + 1)
                    e.wait_ge(acc_ok, blk * GT + j + 1)
                    e.tensor_tensor(tile(acc, n), tile(acc, n), ps_a[j][:, 0:D], ALU.add).then_inc(acc_ok, 1)

                def body(it, last=False):
                    for b in range(UN):
                        g = it * UN + b
                        end = last and b == UN - 1
                        first = isinstance(g, int) and g == 0
                        if not first:
                            to = walk_values(nc, e, k, "walk_n", g - 1)
                        largest(g)
                        if not end:
                            direct(g + 1, (b + 1) % UN, it + 1 if b == UN - 1 else it)
                        if not first:
                            add(g - 1, 0, to[0])
                            add(g - 1, 1, to[1])
                        messages(g, b)
                        if not first:
                            add(g - 1, 2, to[2])
                            add(g - 1, 3, to[3])
                        hots(g, b)
                direct(0, 0, 0)
                body(0)
                with e.Fori(1, NI - 1) as it:
                    body(it)
                body(NI - 1, last=True)
                for blk in range(NG - 1, SB):
                    to = walk_values(nc, e, k, "walk_n", blk)
                    for j in range(GT):
                        add(blk, j, to[j])
                    if blk + 1 < SB:
                        hots(blk + 1, blk + 1)
                e.wait_ge(acc_ok, SB * GT + 1)

            @block.tensor
            def _(e):
                def aggregate(blk, b, j, slot):
                    if j == 0:
                        e.wait_ge(hot_ok, blk + 1)
                        if not isinstance(blk, int) or blk < NG:
                            e.wait_ge(m1_ok, blk + 1)
                            e.wait_ge(m0_ok, blk + 1)
                    wait(e, acc_ok, (blk - 1) * GT + j + 2)
                    e.matmul(ps_a[j][:, 0:D], hot[:, b % 2, j, :], tile(ring, slot), start=True, stop=True).then_inc(sum_ps, 1)

                def front(g, b, between):
                    between(0)
                    e.wait_ge(xr_ok, g + 1)
                    wait(e, xt_sb, g)
                    for t in range(GT):
                        x = e.transpose(ps_x[:, t * P:(t + 1) * P], G[:, b, t, 0:128], k["ident"][:, :])
                    x.then_inc(xt_ps, 1)
                    e.wait_ge(xt_sb, g + 1)
                    wait(e, h_sb, g)
                    e.matmul(ps_h[:, :], k["WH"][:, :], XT[:, b % 2, :], start=True, stop=True).then_inc(h_ps, 1)
                    between(1)
                    e.wait_ge(h_sb, g + 1)
                    wait(e, mx_ok, g)
                    wait(e, ex_ok, g)
                    for t in range(GT):
                        x = e.matmul(ps_s[:, t * 64:(t + 1) * 64], HT[:, b % 2, t * P:(t + 1) * P],
                                     k["LSC2"][:, :], start=True, stop=True)
                    x.then_inc(sc_ps, 1)
                    wait(e, o0_ok, g)
                    wait(e, o1_ok, g)
                    for t in range(GT):
                        x = e.matmul(ps_p[:, t * P:(t + 1) * P], XT[:, b % 2, t * P:(t + 1) * P], k["WO"][:, :],
                                     start=True, stop=True)
                    x.then_inc(p_ps, 1)

                def body(it, last=False):
                    for b in range(UN):
                        g = it * UN + b
                        first = isinstance(g, int) and g == 0
                        if not first:
                            slots = walk_values(nc, e, k, "walk_slot", g - 1)

                        def between(h):
                            if not first:
                                for j in (2 * h, 2 * h + 1):
                                    aggregate(g - 1, (b - 1) % UN, j, slots[j])
                        if last and b == UN - 1:
                            between(0)
                            between(1)
                        else:
                            front(g + 1, (b + 1) % UN, between)
                front(0, 0, lambda h: None)
                body(0)
                with e.Fori(1, NI - 1) as it:
                    body(it)
                body(NI - 1, last=True)
                for blk in range(NG - 1, SB):
                    slots = walk_values(nc, e, k, "walk_slot", blk)
                    for j in range(GT):
                        aggregate(blk, blk % UN, j, slots[j])

            @block.scalar
            def _(e):
                def front(g, b):
                    e.wait_ge(xt_ps, g + 1)
                    wait(e, p_ps, g - 1)
                    wait(e, h_ps, g - 1)
                    e.activation(XT[:, b % 2, :], ps_x[:, :], ACT.Copy).then_inc(xt_sb, 1)
                    e.wait_ge(h_ps, g + 1)
                    wait(e, sc_ps, g - 1)
                    e.activation(HT[:, b % 2, :], ps_h[:, :], ACT.Relu).then_inc(h_sb, 1)

                def exps(g):
                    e.wait_ge(nm_ok, g + 1)
                    wait(e, m1_ok, g)
                    wait(e, m0_ok, g)
                    for t in range(GT):
                        x = e.activation(ex[:, t, :], ps_s[:, t * 64:(t + 1) * 64], ACT.Exp, bias=nm[:, t:t + 1],
                                         accum_out=zs[:, t:t + 1])
                    x.then_inc(ex_ok, 1)
                    e.activation(en[:, :], nm[:, :], ACT.Exp).then_inc(en_ok, 1)

                def body(it, last=False):
                    for b in range(UN):
                        g = it * UN + b
                        exps(g)
                        if not (last and b == UN - 1):
                            front(g + 1, (b + 1) % UN)
                front(0, 0)
                body(0)
                with e.Fori(1, NI - 1) as it:
                    body(it)
                body(NI - 1, last=True)


def pairs(body, n=NT):
    def run(e):
        for i in range(2):
            body(i, i, 0)
        with e.Fori(1, n // 2 - 1) as it:
            for j in range(2):
                body(it * 2 + j, j, it)
        for i in range(2 * (n // 2 - 1), n):
            body(i, i % 2, i // 2)
    return run


def lns(nc, d, k):
    EPS = 1e-8
    with ExitStack() as ctx:
        m = Mem(nc, ctx, "lns")
        w = m.sb("w", [P, 2, D])
        wa = m.sb("wa", [P, 2, D])
        ws = m.sb("ws", [P, 2, D], BF16)
        bias = m.sb("bias", [P, D])
        xn = m.sb("xn", [P, 2, D])
        at = m.sb("at", [P, 2, D])
        ab = m.sb("ab", [P, 2, D])
        wabs = m.sb("wabs", [P, 2, D])
        st = m.sb("st", [P, 2, D], BF16)
        sg = m.sb("sg", [P, 2, D])
        o = m.sb("o", [P, 2, D])
        o2 = m.sb("o2", [P, 2, D])
        ps_t = [m.ps(f"ps_t{i}", [P, 512]) for i in range(2)]
        ps_m = [m.ps(f"ps_m{i}", [P, 512]) for i in range(2)]
        ps_g = [m.ps(f"ps_g{i}", [P, 512]) for i in range(2)]
        S = m.sem
        ab_ok, wabs_ok = S("ab_ok"), S("wabs_ok")
        loaded, wa_ok, ws_ok, xn_ok, t_ps, at_ok, st_ok, y_ps, g_ps, sg_ok, o_ok, o2_ok, x_ok = (S(n) for n in (
            "loaded", "wa_ok", "ws_ok", "xn_ok", "t_ps", "at_ok", "st_ok", "y_ps", "g_ps", "sg_ok", "o_ok", "o2_ok", "x_ok"))
        with nc.Block() as block:
            @block.sync
            def _(e):
                e.dma_start(w[:, :, :], d["lnsT"].rearrange("(c p) n -> p c n", p=P)).then_inc(loaded, 16)
                e.dma_start(bias[:, :], d["lns_b"].to_broadcast([P, D])).then_inc(loaded, 16)

            @block.gpsimd
            def _(e):
                e.wait_ge(loaded, 32)
                e.wait_ge(wabs_ok, 1)
                e.tensor_scalar_add(wa[:, :, :], wabs[:, :, :], EPS).then_inc(wa_ok, 1)

            @block.vector
            def _(e):
                e.wait_ge(loaded, 32)

                def norm(i, j):
                    wait(e, t_ps, i - 1)
                    e.tensor_scalar(xn[:, j, :], tile(k["X"], i), cols(k["mvf"], i * 2, 1), cols(k["rstd"], i, 1),
                                    ALU.subtract, ALU.mult).then_inc(xn_ok, 1)

                def body(i, j, it):
                    if not (isinstance(i, int) and i == NT - 1):
                        norm(i + 1, 1 - j)
                    e.wait_ge(ab_ok, i + 1)
                    wait(e, y_ps, i - 1)
                    e.tensor_scalar_add(at[:, j, :], ab[:, j, :], EPS).then_inc(at_ok, 1)
                    e.wait_ge(sg_ok, i + 1)
                    e.wait_ge(y_ps, i + 1)
                    wait(e, o2_ok, i - 1)
                    e.tensor_tensor(o[:, j, :], sg[:, j, :], ps_m[j][:, 0:D], ALU.mult).then_inc(o_ok, 1)
                    e.wait_ge(o_ok, i + 1)
                    wait(e, x_ok, i - 1)
                    e.tensor_tensor(o2[:, j, :], o[:, j, :], bias[:, :], ALU.add).then_inc(o2_ok, 1)
                    e.wait_ge(o2_ok, i + 1)
                    e.tensor_tensor(tile(k["X"], i), tile(k["X"], i), o2[:, j, :], ALU.add).then_inc(x_ok, 1)
                norm(0, 0)
                pairs(body)(e)

            @block.tensor
            def _(e):
                e.wait_ge(wa_ok, 1)
                e.wait_ge(ws_ok, 1)

                def body(i, j, it):
                    e.wait_ge(xn_ok, i + 1)
                    wait(e, ab_ok, i - 1)
                    wait(e, st_ok, i - 1)
                    for c in range(2):
                        x = e.transpose(ps_t[j][:, c * P:(c + 1) * P], xn[:, j, c * P:(c + 1) * P], k["ident"][:, :])
                    x.then_inc(t_ps, 1)
                    e.wait_ge(st_ok, i + 1)
                    wait(e, sg_ok, i - 1)
                    for c in range(2):
                        x = e.matmul(ps_g[j][:, 0:D], st[:, j, c * P:(c + 1) * P], ws[:, c, :], start=c == 0, stop=c == 1)
                    x.then_inc(g_ps, 1)
                    e.wait_ge(at_ok, i + 1)
                    wait(e, o_ok, i - 1)
                    for c in range(2):
                        x = e.matmul(ps_m[j][:, 0:D], at[:, j, c * P:(c + 1) * P], wa[:, c, :], start=c == 0, stop=c == 1)
                    x.then_inc(y_ps, 1)
                pairs(body)(e)

            @block.scalar
            def _(e):
                e.wait_ge(loaded, 32)
                e.activation(wabs[:, :, :], w[:, :, :], ACT.Abs).then_inc(wabs_ok, 1)
                e.activation(ws[:, :, :], w[:, :, :], ACT.Sign).then_inc(ws_ok, 1)

                def body(i, j, it):
                    e.wait_ge(t_ps, i + 1)
                    wait(e, g_ps, i - 1)
                    e.activation(st[:, j, :], ps_t[j][:, 0:D], ACT.Sign).then_inc(st_ok, 1)
                    wait(e, at_ok, i - 1)
                    e.activation(ab[:, j, :], ps_t[j][:, 0:D], ACT.Abs).then_inc(ab_ok, 1)
                    e.wait_ge(g_ps, i + 1)
                    wait(e, o_ok, i - 1)
                    e.activation(sg[:, j, :], ps_g[j][:, 0:D], ACT.Sign).then_inc(sg_ok, 1)
                pairs(body)(e)


def qkv(nc, d, k):
    with ExitStack() as ctx:
        m = Mem(nc, ctx, "qkv")
        w = m.sb("w", [P, 2, 768])
        bias = m.sb("bias", [P, 768])
        xn = m.sb("xn", [P, 2, D])
        xt = m.sb("xt", [P, 2, D])
        row = m.sb("row", [P, 2, 768])
        ps_t = [m.ps(f"ps_t{i}", [P, 512]) for i in range(2)]
        ps_y = [m.ps(f"ps_y{i}", [P, 1024]) for i in range(2)]
        S = m.sem
        loaded, xn_ok, t_ps, xt_ok, y_ps, row_ok = (S(n) for n in ("loaded", "xn_ok", "t_ps", "xt_ok", "y_ps", "row_ok"))
        stored = [S(f"stored{i}") for i in range(2)]
        with nc.Block() as block:
            @block.sync
            def _(e):
                e.dma_start(w[:, :, :], d["wqkv"].rearrange("(c p) n -> p c n", p=P)).then_inc(loaded, 16)
                e.dma_start(bias[:, :], d["bqkv"].to_broadcast([P, 768])).then_inc(loaded, 16)

                def body(i, j, it):
                    e.wait_ge(row_ok, 2 * i + 2)
                    for n, name in enumerate(("qtab", "ktab", "vtab")):
                        t = d[name].rearrange("(n p) c -> n p c", p=P)
                        dst = t[i, :, :] if isinstance(i, int) else t[bass.ds(i, 1), :, :].rearrange("a p c -> (a p) c")
                        e.dma_start(dst, row[:, j, n * D:(n + 1) * D]).then_inc(stored[j], 16)
                pairs(body)(e)
                e.wait_ge(stored[0], 13 * 48)
                e.wait_ge(stored[1], 12 * 48)

            @block.vector
            def _(e):
                def norm(i, j):
                    wait(e, t_ps, i - 1)
                    e.tensor_scalar(xn[:, j, :], tile(k["X"], i), cols(k["mvf"], i * 2, 1), cols(k["rstd"], i, 1),
                                    ALU.subtract, ALU.mult).then_inc(xn_ok, 1)

                def body(i, j, it):
                    if not (isinstance(i, int) and i == NT - 1):
                        norm(i + 1, 1 - j)
                    e.wait_ge(y_ps, i + 1)
                    wait(e, stored[j], it * 48)
                    e.tensor_tensor(row[:, j, 0:512], ps_y[j][:, 0:512], bias[:, 0:512], ALU.add).then_inc(row_ok, 1)
                    e.tensor_tensor(row[:, j, 512:768], ps_y[j][:, 512:768], bias[:, 512:768], ALU.add).then_inc(row_ok, 1)
                e.wait_ge(loaded, 32)
                norm(0, 0)
                pairs(body)(e)

            @block.tensor
            def _(e):
                e.wait_ge(loaded, 32)

                def body(i, j, it):
                    e.wait_ge(xn_ok, i + 1)
                    wait(e, xt_ok, i - 1)
                    for c in range(2):
                        x = e.transpose(ps_t[j][:, c * P:(c + 1) * P], xn[:, j, c * P:(c + 1) * P], k["ident"][:, :])
                    x.then_inc(t_ps, 1)
                    e.wait_ge(xt_ok, i + 1)
                    wait(e, row_ok, 2 * i - 2)
                    for c in range(2):
                        e.matmul(ps_y[j][:, 0:512], xt[:, j, c * P:(c + 1) * P], w[:, c, 0:512], start=c == 0, stop=c == 1)
                    for c in range(2):
                        x = e.matmul(ps_y[j][:, 512:768], xt[:, j, c * P:(c + 1) * P], w[:, c, 512:768], start=c == 0, stop=c == 1)
                    x.then_inc(y_ps, 1)
                pairs(body)(e)

            @block.scalar
            def _(e):
                def body(i, j, it):
                    e.wait_ge(t_ps, i + 1)
                    wait(e, y_ps, i - 1)
                    e.activation(xt[:, j, :], ps_t[j][:, 0:D], ACT.Copy).then_inc(xt_ok, 1)
                pairs(body)(e)


def scores(nc, d, k):
    with ExitStack() as ctx:
        m = Mem(nc, ctx, "scores")
        Q = m.sb("Q", [P, UN, GT, D])
        K = m.sb("K", [P, UN, GT, D])
        sq, sk = m.sb("sq", [P, UN, GT], I32), m.sb("sk", [P, UN, GT], I32)
        scr = m.sb("scr", [P, 2])
        prod = m.sb("prod", [P, 2, GT, D])
        landed = [m.sem(f"landed{i}") for i in range(UN)]
        staged, carried, prod_ok, s_ok = (m.sem(n) for n in ("staged", "carried", "prod_ok", "s_ok"))
        with nc.Block() as block:
            @block.gpsimd
            def _(e):
                gathers(e, scr, carried, staged, landed,
                        [(d["qtab"], k["src_i"], sq, lambda b, j: Q[:, b, j, :]),
                         (d["ktab"], k["dst_i"], sk, lambda b, j: K[:, b, j, :])],
                        lambda g: [(prod_ok, g - UN + 1)])

            @block.vector
            def _(e):
                def body(it):
                    for b in range(UN):
                        g = it * UN + b
                        e.wait_ge(landed[b], (it + 1) * 16 * GT * 2)
                        wait(e, s_ok, g - 1)
                        e.tensor_tensor(prod[:, b % 2, :, :], Q[:, b, :, :], K[:, b, :, :], ALU.mult).then_inc(prod_ok, 1)
                        e.wait_ge(prod_ok, g + 1)
                        e.tensor_reduce(cols(k["S"], g * GT * HEADS, GT * HEADS),
                                        prod[:, b % 2, :, :].rearrange("p t (h c) -> p (t h) c", c=HD), AX.X, ALU.add
                                        ).then_inc(s_ok, 1)
                rolled(e, NI, body)


CH = 16
CT = ET // CH
CE = CT * P


def softmax_shift(nc, d, k):
    B = 1.0e38
    with ExitStack() as ctx:
        m = Mem(nc, ctx, "shift")
        ST = m.sb("ST", [P, CE])
        DT = m.sb("DT", [P, CE + 2])
        pen = m.sb("pen", [P, CE + 1])
        eq = m.sb("eq", [P, CE + 1])
        F = m.sb("F", [P, CE])
        R = m.sb("R", [P, CE])
        down, up = m.sb("down", [P, P]), m.sb("up", [P, P])
        pi = m.sb("pi", [P, 4], I32)
        pf = m.sb("pf", [P, 2])
        hsel, csel = m.sb("hsel", [P, HEADS]), m.sb("csel", [P, CH])
        hselT = m.sb("hselT", [HEADS, P])
        ends = m.sb("ends", [P, 4])
        spread = m.sb("spread", [P, 4, CH])
        small = m.sb("small", [HEADS, 4, CH])
        carry = m.sb("carry", [HEADS, 2, CH + 1])
        pick = m.sb("pick", [P, 2, CH])
        init = m.sb("init", [P, 2])
        ps = [m.ps(f"ps{i}", [P, 512]) for i in range(2)]
        ps_e = m.ps("ps_e", [P, 512])
        tr, ev, sel, chain, side, pe = (m.sem(n) for n in ("tr", "ev", "sel", "chain", "side", "pe"))
        ex_ok, back, back_ev, made = (m.sem(n) for n in ("ex_ok", "back", "back_ev", "made"))
        S4 = k["S"][:, :].rearrange("p (c j h) -> p j c h", c=CH, h=HEADS)
        D4 = k["dst_f"][:, :].rearrange("p (c j) -> p j c", c=CH)
        D2, S2 = m.sb("D2", [P, CT, P]), m.sb("S2", [P, CT, P])
        by4 = lambda t: t[:, :, :].rearrange("p j (c h) -> p j c h", h=HEADS)
        ordered = m.sem("ordered")
        rounds = [(a, j0, min(4, CT - j0)) for a in range(2) for j0 in range(0, CT, 4)]
        half = len(rounds) // 2
        with nc.Block() as block:
            @block.tensor
            def _(e):
                e.wait_ge(ordered, 2)
                for n, (a, j0, w) in enumerate(rounds):
                    wait(e, ev, n - 1)
                    for j in range(w):
                        x = e.transpose(ps[n % 2][:, j * P:(j + 1) * P], (D2, S2)[a][:, j0 + j, :], k["ident"][:, :])
                    x.then_inc(tr, 1)
                e.wait_ge(ev, half)
                e.wait_ge(made, 4)
                e.matmul(ps_e[:, 0:1], down[:, :], DT[:, CE:CE + 1], start=True, stop=True)
                e.matmul(ps_e[:, 1:2], up[:, :], DT[:, 1:2], start=True, stop=True).then_inc(pe, 1)
                e.wait_ge(sel, 2)
                e.wait_ge(side, 1)
                e.transpose(ps_e[0:HEADS, 0:P], hsel[:, :], k["ident"][:, :]).then_inc(pe, 1)
                e.wait_ge(side, 2)
                e.wait_ge(chain, 1)
                e.matmul(ps_e[0:HEADS, 128:192], hsel[:, :], spread[:, :, :].rearrange("p a c -> p (a c)"),
                         start=True, stop=True).then_inc(pe, 1)
                e.wait_ge(side, 3)
                e.matmul(ps_e[:, 256:288], hselT[:, :], small[:, 0:2, :].rearrange("p a c -> p (a c)"), start=True, stop=True).then_inc(pe, 1)
                e.wait_ge(ex_ok, 1)
                for n, (a, j0, w) in enumerate(rounds[half:]):
                    wait(e, back_ev, n - 1)
                    for j in range(w):
                        x = e.transpose(ps[n % 2][:, j * P:(j + 1) * P], F[:, (j0 + j) * P:(j0 + j + 1) * P], k["ident"][:, :])
                    x.then_inc(back, 1)

            @block.gpsimd
            def _(e):
                e.memset(down[:, :], 0.0).then_inc(made, 1)
                e.memset(up[:, :], 0.0).then_inc(made, 1)
                e.wait_ge(made, 2)
                e.tensor_copy(down[:, HEADS:P], k["ident"][:, 0:P - HEADS]).then_inc(made, 1)
                e.tensor_copy(up[:, 0:P - HEADS], k["ident"][:, HEADS:P]).then_inc(made, 1)
                e.iota(pi[:, 0:1], pattern=[[1, 1]], base=0, channel_multiplier=1).then_inc(made, 1)

            @block.scalar
            def _(e):
                e.activation(by4(D2), D4.unsqueeze(3).to_broadcast([P, CT, CH, HEADS]), ACT.Copy).then_inc(ordered, 1)
                for n, (a, j0, w) in enumerate(rounds):
                    to = DT[:, 1 + j0 * P:1 + (j0 + w) * P] if a == 0 else ST[:, j0 * P:(j0 + w) * P]
                    e.wait_ge(tr, n + 1)
                    e.activation(to, ps[n % 2][:, 0:w * P], ACT.Copy).then_inc(ev, 1)
                e.wait_ge(chain, 2)
                e.activation(F[:, :], R[:, :], ACT.Exp, scale=1.0 / HD ** 0.5).then_inc(ex_ok, 1)
                for n, (a, j0, w) in enumerate(rounds[half:]):
                    e.wait_ge(back, n + 1)
                    e.activation(S4[:, j0:j0 + w, :, :],
                                 ps[n % 2][:, 0:w * P].rearrange("p (j c h) -> p j c h", j=w, h=HEADS), ACT.Copy).then_inc(back_ev, 1)

            @block.vector
            def _(e):
                n = [0]
                own = m.sem("own")

                def link(ins):
                    ins.then_inc(own, 1)
                    n[0] += 1
                    e.wait_ge(own, n[0])
                e.tensor_copy(by4(S2), S4).then_inc(ordered, 1)
                e.wait_ge(made, 5)
                link(e.tensor_single_scalar(pi[:, 1:2], pi[:, 0:1], HEADS - 1, ALU.bitwise_and))
                link(e.tensor_single_scalar(pi[:, 2:3], pi[:, 0:1], 3, ALU.arith_shift_right))
                link(e.tensor_copy(pf[:, :], pi[:, 1:3]))
                e.tensor_scalar(hsel[:, :], k["iota"][:, 0:HEADS], pf[:, 0:1], None, ALU.is_equal).then_inc(sel, 1)
                e.tensor_scalar(csel[:, :], k["iota"][:, 0:CH], pf[:, 1:2], None, ALU.is_equal).then_inc(sel, 1)
                e.wait_ge(sel, 2)
                e.wait_ge(pe, 1)
                link(e.tensor_tensor(DT[:, 0:1], ps_e[:, 0:1], csel[:, 0:1], ALU.subtract))
                link(e.tensor_tensor(DT[:, CE + 1:CE + 2], ps_e[:, 1:2], csel[:, CH - 1:CH], ALU.subtract))
                e.engine_nop().then_inc(side, 1)
                link(e.tensor_tensor(eq[:, :], DT[:, 0:CE + 1], DT[:, 1:CE + 2], ALU.is_equal))
                link(e.tensor_scalar(pen[:, :], eq[:, :], -1.0, B, ALU.add, ALU.mult))
                e.wait_ge(ev, len(rounds))
                e.tensor_reduce(ends[:, 1:2], pen[:, 0:CE], AX.X, ALU.min)
                e.tensor_reduce(ends[:, 3:4], pen[:, 1:CE + 1], AX.X, ALU.min)
                e.tensor_tensor_scan(F[:, :], pen[:, 0:CE], ST[:, :], -B, ALU.add, ALU.max)
                link(e.tensor_tensor_scan(R[:, ::-1], pen[:, CE:0:-1], ST[:, ::-1], -B, ALU.add, ALU.max))
                e.tensor_copy(ends[:, 0:1], F[:, CE - 1:CE])
                link(e.tensor_copy(ends[:, 2:3], R[:, 0:1]))
                e.tensor_tensor(spread[:, :, :], ends[:, :].unsqueeze(2).to_broadcast([P, 4, CH]),
                                csel[:, :].unsqueeze(1).to_broadcast([P, 4, CH]), ALU.mult).then_inc(chain, 1)
                e.wait_ge(pe, 2)
                e.tensor_copy(hselT[:, :], ps_e[0:HEADS, 0:P]).then_inc(side, 1)
                e.memset(carry[:, :, :], -B)
                e.wait_ge(pe, 3)
                link(e.tensor_copy(small[:, :, :], ps_e[0:HEADS, 128:192].rearrange("p (a c) -> p a c", a=4)))
                link(e.tensor_tensor_scan(carry[:, 0, 1:CH + 1], small[:, 1, :], small[:, 0, :], -B, ALU.add, ALU.max))
                link(e.tensor_tensor_scan(carry[:, 1, CH - 1::-1], small[:, 3, ::-1], small[:, 2, ::-1], -B, ALU.add, ALU.max))
                e.tensor_copy(small[:, 0, :], carry[:, 0, 0:CH])
                e.tensor_copy(small[:, 1, :], carry[:, 1, 1:CH + 1]).then_inc(side, 1)
                e.wait_ge(pe, 4)
                link(e.tensor_tensor(pick[:, :, :], ps_e[:, 256:288].rearrange("p (a c) -> p a c", a=2),
                                     csel[:, :].unsqueeze(1).to_broadcast([P, 2, CH]), ALU.mult))
                link(e.tensor_reduce(init[:, :], pick[:, :, :], AX.X, ALU.add))
                link(e.tensor_tensor_scan(F[:, :], pen[:, 0:CE], ST[:, :], init[:, 0:1], ALU.add, ALU.max))
                link(e.tensor_tensor_scan(R[:, ::-1], pen[:, CE:0:-1], ST[:, ::-1], init[:, 1:2], ALU.add, ALU.max))
                link(e.tensor_tensor(eq[:, 0:CE], F[:, :], R[:, :], ALU.max))
                e.tensor_tensor(R[:, :], ST[:, :], eq[:, 0:CE], ALU.subtract).then_inc(chain, 1)


def aggregate1(nc, d, k):
    A = D + HEADS
    with ExitStack() as ctx:
        m = Mem(nc, ctx, "agg1")
        V = m.sb("V", [P, UN, GT, D])
        stage = m.sb("stage", [P, UN, GT], I32)
        scr = m.sb("scr", [P, 2])
        ring = m.sb("ring", [P, RING, A])
        hot = m.sb("hot", [P, 2, GT, P])
        ps_a = [m.ps(f"ps_a{i}", [P, 512]) for i in range(4)]
        landed = [m.sem(f"landed{i}") for i in range(UN)]
        staged, carried, msg_ok, p_ok, hot_ok, sum_ps, acc_ok = (
            m.sem(n) for n in ("staged", "carried", "msg_ok", "p_ok", "hot_ok", "sum_ps", "acc_ok"))
        acc = k["acc1"]
        with nc.Block() as block:
            @block.gpsimd
            def _(e):
                gathers(e, scr, carried, staged, landed,
                        [(d["vtab"], k["src_i"], stage, lambda b, j: V[:, b, j, :])], lambda g: [(msg_ok, g - UN + 1)])

            @block.vector
            def _(e):
                e.memset(acc[:, :, :], 0.0).then_inc(acc_ok, 1)

                def hots(blk, b):
                    wait(e, sum_ps, blk * GT - GT)
                    one_hots(e, k, hot[:, b % 2, :, :], blk).then_inc(hot_ok, 1)

                def add(blk, j, n):
                    e.wait_ge(sum_ps, blk * GT + j + 1)
                    e.wait_ge(acc_ok, blk * GT + j + 1)
                    e.tensor_tensor(tile(acc, n), tile(acc, n), ps_a[j][:, 0:A], ALU.add).then_inc(acc_ok, 1)

                def body(it):
                    for b in range(UN):
                        g = it * UN + b
                        first = isinstance(g, int) and g == 0
                        if not first:
                            to = walk_values(nc, e, k, "walk_n", g - 1)
                        hots(g, b)
                        e.wait_ge(landed[b], (it + 1) * 16 * GT)
                        slot = (g % (RING // GT)) * GT
                        p = cols(k["S"], g * GT * HEADS, GT * HEADS).rearrange("p (t h) -> p t h", h=HEADS)
                        e.tensor_copy(tiles(ring, slot, GT)[:, :, D:A], p).then_inc(p_ok, 1)
                        e.tensor_tensor(tiles(ring, slot, GT)[:, :, 0:D].rearrange("p t (h c) -> p t h c", c=HD),
                                        V[:, b, :, :].rearrange("p t (h c) -> p t h c", c=HD),
                                        p.unsqueeze(3).to_broadcast([P, GT, HEADS, HD]), ALU.mult).then_inc(msg_ok, 1)
                        if not first:
                            for j in range(GT):
                                add(g - 1, j, to[j])
                rolled(e, NI, body)
                for blk in range(NG, SB + 1):
                    to = walk_values(nc, e, k, "walk_n", blk - 1)
                    if blk < SB:
                        hots(blk, blk)
                    for j in range(GT):
                        add(blk - 1, j, to[j])
                e.wait_ge(acc_ok, SB * GT + 1)

            @block.tensor
            def _(e):
                def block_of(blk, b):
                    slots = walk_values(nc, e, k, "walk_slot", blk)
                    for j in range(GT):
                        e.wait_ge(hot_ok, blk + 1)
                        if j == 0 and not (isinstance(blk, int) and blk >= NG):
                            e.wait_ge(msg_ok, blk + 1)
                            e.wait_ge(p_ok, blk + 1)
                        wait(e, acc_ok, blk * GT + j - GT + 2)
                        e.matmul(ps_a[j][:, 0:A], hot[:, b % 2, j, :], tile(ring, slots[j]), start=True, stop=True).then_inc(sum_ps, 1)

                def body(it):
                    for b in range(UN):
                        block_of(it * UN + b, b)
                rolled(e, NI, body)
                for blk in range(NG, SB):
                    block_of(blk, blk)


def add_acc1(nc, k):
    with ExitStack() as ctx:
        m = Mem(nc, ctx, "add1")
        z, rz = m.sb("z", [P, NT, HEADS]), m.sb("rz", [P, NT, HEADS])
        s = m.sem("s")
        acc = k["acc1"]
        with nc.Block() as block:
            @block.vector
            def _(e):
                e.tensor_scalar_max(z[:, :, :], acc[:, :, D:D + HEADS], 1e-16).then_inc(s, 1)
                e.wait_ge(s, 1)
                e.reciprocal(rz[:, :, :], z[:, :, :]).then_inc(s, 1)
                e.wait_ge(s, 2)
                v = acc[:, :, 0:D].rearrange("p n (h c) -> p n h c", c=HD)
                e.tensor_tensor(v, v, rz[:, :, :].unsqueeze(3).to_broadcast([P, NT, HEADS, HD]), ALU.mult).then_inc(s, 1)
                e.wait_ge(s, 3)
                e.tensor_tensor(k["X"][:, :, :], k["X"][:, :, :], acc[:, :, 0:D], ALU.add).then_inc(s, 1)


def route(nc, d, k):
    with ExitStack() as ctx:
        m = Mem(nc, ctx, "route")
        gb = m.sb("gb", [P, 2, 2])
        wr = m.sb("wr", [P, 2, NE])
        br = m.sb("br", [P, NE])
        b2 = m.sb("b2", [NE, D])
        xn = m.sb("xn", [P, 2, D])
        xt = m.sb("xt", [P, 2, D])
        lg = m.sb("lg", [P, NT, NE])
        top = m.sb("top", [P, NT, 8])
        idx = m.sb("idx", [P, NT, 8], U32)
        idf = m.sb("idf", [P, NT, 2])
        df, ed, ep, w0, w1 = (m.sb(n, [P, NT]) for n in ("df", "ed", "ep", "w0", "w1"))
        one = m.sb("one", [P, 2, NT, NE])
        wT = m.sb("wT", [NE, 2, P])
        ps_t = [m.ps(f"ps_t{i}", [P, 512]) for i in range(2)]
        ps_l = [m.ps(f"ps_l{i}", [P, 512]) for i in range(2)]
        S = m.sem
        loaded, xn_ok, t_ps, xt_ok, xc_ok, l_ps, lg_ok, top_ok, idx_ok, own, df_ok, ed_ok, wf_ok = (S(n) for n in (
            "loaded", "xn_ok", "t_ps", "xt_ok", "xc_ok", "l_ps", "lg_ok", "top_ok", "idx_ok", "own", "df_ok", "ed_ok", "wf_ok"))
        wt_ps, wt_ok, b_ps, x_ok = (S(n) for n in ("wt_ps", "wt_ok", "b_ps", "x_ok"))
        with nc.Block() as block:
            @block.sync
            def _(e):
                e.dma_start(gb[:, 0, :], d["gamma"]).then_inc(loaded, 16)
                e.dma_start(gb[:, 1, :], d["beta"]).then_inc(loaded, 16)
                e.dma_start(wr[:, :, :], d["Wr"].rearrange("(c p) n -> p c n", p=P)).then_inc(loaded, 16)
                e.dma_start(br[:, :], d["br"].to_broadcast([P, NE])).then_inc(loaded, 16)
                e.dma_start(b2[:, :], d["b2"]).then_inc(loaded, 16)
                e.dma_start(k["b1"][:, :, :], d["b1"]).then_inc(loaded, 16)
                e.wait_ge(loaded, 96)

            @block.vector
            def _(e):
                def norm(i, j):
                    wait(e, t_ps, i - 1)
                    e.tensor_scalar(xn[:, j, :], tile(k["X"], i), cols(k["mvf"], i * 2, 1), cols(k["rstd"], i, 1),
                                    ALU.subtract, ALU.mult).then_inc(xn_ok, 1)

                def body(i, j, it):
                    if not (isinstance(i, int) and i == NT - 1):
                        norm(i + 1, 1 - j)
                    e.wait_ge(t_ps, i + 1)
                    wait(e, l_ps, i - 1)
                    wait(e, xc_ok, i - 1)
                    for c in range(2):
                        e.tensor_scalar(xt[:, j, c * P:(c + 1) * P], ps_t[j][:, c * P:(c + 1) * P], gb[:, 0, c:c + 1],
                                        gb[:, 1, c:c + 1], ALU.mult, ALU.add).then_inc(xt_ok, 1)
                    e.wait_ge(l_ps, i + 1)
                    e.tensor_tensor(tile(lg, i), ps_l[j][:, 0:NE], br[:, :], ALU.add).then_inc(lg_ok, 1)
                e.wait_ge(loaded, 96)
                norm(0, 0)
                pairs(body)(e)
                n = [0]

                def link(ins):
                    ins.then_inc(own, 1)
                    n[0] += 1
                    e.wait_ge(own, n[0])
                e.wait_ge(lg_ok, NT)
                for i in range(NT):
                    e.max(top[:, i, :], lg[:, i, :]).then_inc(top_ok, 1)
                for i in range(NT):
                    e.wait_ge(top_ok, i + 1)
                    e.max_index(idx[:, i, :], top[:, i, :], lg[:, i, :]).then_inc(idx_ok, 1)
                e.wait_ge(idx_ok, NT)
                link(e.tensor_copy(idf[:, :, :], idx[:, :, 0:2]))
                e.tensor_tensor(df[:, :], top[:, :, 1], top[:, :, 0], ALU.subtract).then_inc(df_ok, 1)
                e.wait_ge(ed_ok, 1)
                link(e.tensor_scalar_add(ep[:, :], ed[:, :], 1.0))
                link(e.reciprocal(w0[:, :], ep[:, :]))
                link(e.tensor_tensor(w1[:, :], ed[:, :], w0[:, :], ALU.mult))
                for r, w in enumerate((w0, w1)):
                    hit = one[:, r, :, :]
                    link(e.tensor_tensor(hit, k["iota"][:, 0:NE].unsqueeze(1).to_broadcast([P, NT, NE]),
                                         idf[:, :, r].unsqueeze(2).to_broadcast([P, NT, NE]), ALU.is_equal))
                    link(e.tensor_tensor(hit, hit, w[:, :].unsqueeze(2).to_broadcast([P, NT, NE]), ALU.mult))
                e.tensor_tensor(k["wfull"][:, :, :], one[:, 0, :, :], one[:, 1, :, :], ALU.add).then_inc(wf_ok, 1)
                for i in range(NT):
                    e.wait_ge(b_ps, i + 1)
                    e.tensor_tensor(k["X"][:, i, :], k["X"][:, i, :], ps_l[i % 2][:, 256:256 + D], ALU.add).then_inc(x_ok, 1)

            @block.tensor
            def _(e):
                e.wait_ge(loaded, 96)

                def body(i, j, it):
                    e.wait_ge(xn_ok, i + 1)
                    wait(e, xt_ok, 2 * i - 2)
                    for c in range(2):
                        x = e.transpose(ps_t[j][:, c * P:(c + 1) * P], xn[:, j, c * P:(c + 1) * P], k["ident"][:, :])
                    x.then_inc(t_ps, 1)
                    e.wait_ge(xt_ok, 2 * i + 2)
                    wait(e, lg_ok, i - 1)
                    for c in range(2):
                        x = e.matmul(ps_l[j][:, 0:NE], xt[:, j, c * P:(c + 1) * P], wr[:, c, :], start=c == 0, stop=c == 1)
                    x.then_inc(l_ps, 1)
                pairs(body)(e)
                e.wait_ge(wf_ok, 1)
                for i in range(NT):
                    wait(e, wt_ok, i - 1)
                    e.transpose(ps_t[i % 2][0:NE, 0:P], k["wfull"][:, i, :], k["ident"][:, :]).then_inc(wt_ps, 1)
                    e.wait_ge(wt_ok, i + 1)
                    wait(e, x_ok, i - 1)
                    e.matmul(ps_l[i % 2][:, 256:256 + D], wT[:, i % 2, :], b2[:, :], start=True, stop=True).then_inc(b_ps, 1)

            @block.scalar
            def _(e):
                def body(i, j, it):
                    e.wait_ge(xt_ok, 2 * i + 2)
                    e.activation(cols(k["XNT"][0], i * P, P), xt[:, j, 0:P], ACT.Copy)
                    e.activation(cols(k["XNT"][1], i * P, P), xt[:, j, P:2 * P], ACT.Copy).then_inc(xc_ok, 1)
                pairs(body)(e)
                e.wait_ge(df_ok, 1)
                e.activation(ed[:, :], df[:, :], ACT.Exp).then_inc(ed_ok, 1)
                for i in range(NT):
                    e.wait_ge(wt_ps, i + 1)
                    wait(e, b_ps, i - 1)
                    e.activation(wT[:, i % 2, :], ps_t[i % 2][0:NE, 0:P], ACT.Copy).then_inc(wt_ok, 1)


BT = 5
NB = NT // BT
HC = HID // P


def experts(nc, d, k):
    with ExitStack() as ctx:
        m = Mem(nc, ctx, "experts")
        H = m.sb("H", [P, 2, HC, BT * P])
        ps_h = [m.ps(f"ps_h{i}", [P, 512]) for i in range(4)]
        ps_y = [m.ps(f"ps_y{i}", [P, 512]) for i in range(4)]
        h_ps, h_ok, y_ps, x_ok = (m.sem(n) for n in ("h_ps", "h_ok", "y_ps", "x_ok"))
        W1, W2 = k["W1"], k["W2"]
        half = BT * P // 2
        NH = 2 * HC
        with nc.Block() as block:
            @block.tensor
            def _(e):
                e.wait_ge(k["w_in"], 32)

                def up(n, q, batch, x):
                    for c in range(HC):
                        for h in range(2):
                            r = (2 * c + h) % 4
                            wait(e, h_ok, n * NH + 2 * c + h - 3)
                            for kc in range(2):
                                i = e.matmul(ps_h[r][:, 0:half], W1[:, x, kc, c * P:(c + 1) * P],
                                             cols(k["XNT"][kc], batch * (BT * P) + h * half, half), start=kc == 0, stop=kc == 1)
                            i.then_inc(h_ps, 1)

                def down(n, x):
                    for t in range(BT):
                        e.wait_ge(h_ok, n * NH + NH)
                        r = (x * BT + t) % 4
                        wait(e, x_ok, n * BT + t - 3)
                        for c in range(HC):
                            i = e.matmul(ps_y[r][:, 0:D], H[:, x % 2, c, t * P:(t + 1) * P], W2[:, x, c, :],
                                         start=c == 0, stop=c == HC - 1)
                        i.then_inc(y_ps, 1)

                rounds(e, lambda b, x: up(b * NE + x, x % 2, b, x), lambda b, x: down(b * NE + x, x))

            @block.scalar
            def _(e):
                def body(b):
                    for x in range(NE):
                        n = b * NE + x
                        for c in range(HC):
                            for h in range(2):
                                e.wait_ge(h_ps, n * NH + 2 * c + h + 1)
                                if c == 0 and h == 0:
                                    wait(e, y_ps, (n - 1) * BT)
                                e.activation(H[:, x % 2, c, h * half:(h + 1) * half], ps_h[(2 * c + h) % 4][:, 0:half],
                                             ACT.Gelu, bias=k["b1"][:, x, c:c + 1]).then_inc(h_ok, 1)
                rolled(e, NB, body)

            @block.vector
            def _(e):
                def body(b):
                    for x in range(NE):
                        n = b * NE + x
                        for t in range(BT):
                            r = (x * BT + t) % 4
                            e.wait_ge(y_ps, n * BT + t + 1)
                            wait(e, x_ok, n * BT + t - BT + 1)
                            X = tile(k["X"], b * BT + t)
                            w = cols(k["wflat"], (b * BT + t) * NE + x, 1)
                            e.scalar_tensor_tensor(X, ps_y[r][:, 0:D], w, X, ALU.mult, ALU.add).then_inc(x_ok, 1)
                rolled(e, NB, body)


def rounds(e, up, down):
    up(0, 0)

    def body(b, last=False):
        for x in range(NE):
            if x < NE - 1:
                up(b, x + 1)
            elif not last:
                up(b + 1, 0)
            down(b, x)
    body(0)
    with e.Fori(1, NB - 1) as b:
        body(b)
    body(NB - 1, last=True)


def write_x(nc, d, k):
    with ExitStack() as ctx:
        done = Mem(nc, ctx, "out").sem("done")
        block = ctx.enter_context(nc.Block())

        @block.sync
        def _(e):
            full = NODES // P
            e.dma_start(d["out"][0:full * P, :].rearrange("(n p) c -> p n c", p=P), k["X"][:, 0:full, :]).then_inc(done, 16)
            e.dma_start(d["out"][full * P:NODES, :], k["X"][0:NODES - full * P, full, :]).then_inc(done, 16)
            e.wait_ge(done, 32)


def add_acc0(nc, k):
    with ExitStack() as ctx:
        s = Mem(nc, ctx, "add0").sem("s")
        block = ctx.enter_context(nc.Block())

        @block.vector
        def _(e):
            X, acc = k["X"], k["acc0"]
            e.tensor_tensor(X[:, :, 0:64], X[:, :, 0:64], acc[:, :, 0:64], ALU.add)
            for m in range(3):
                e.tensor_tensor(X[:, :, 64 + m:256:3], X[:, :, 64 + m:256:3], acc[:, :, 64 + 64 * m:128 + 64 * m], ALU.add)
            e.engine_nop().then_inc(s, 1)


def build(nc, d, stop=99):
    with ExitStack() as ctx:
        m = Mem(nc, ctx, "k")
        k = {}
        for name, shape, dt in (("X", [P, NT, D], F32), ("iota", [P, 512], F32), ("ident", [P, P], F32),
                                ("dst_f", [P, ET], F32), ("src_i", [P, ET], I32), ("dst_i", [P, ET], I32),
                                ("walk_n", [1, 512], I32), ("walk_slot", [1, 512], I32), ("dstep", [P, 512], F32),
                                 ("mv", [P, NT, 2], F32), ("rstd", [P, NT], F32)):
            k[name] = m.sb(name, shape, dt)
        k["mvf"] = k["mv"][:, :, :].rearrange("p n a -> p (n a)")
        with ExitStack() as c0:
            m0 = Mem(nc, c0, "l0")
            for name, shape in (("r", [P, ET, 3]), ("s2", [P, ET]), ("WH", [P, 128]), ("WO", [P, 128]), ("WQ", [64, 64]),
                                ("LSC2", [P, 64]), ("blockww", [P, P]), ("attr", [P, ET, 3])):
                k[name] = m0.sb(name, shape)
            edges_in(nc, d, k)
            setup(nc, d, k)
            moments(nc, k, "mom0")
            nodes0(nc, d, k)
            if stop > 0:
                k["acc0"] = m0.sb("acc0", [P, NT, D])
                edges0(nc, d, k)
                add_acc0(nc, k)
        if stop > 1:
            moments(nc, k, "mom1")
            lns(nc, d, k)
        if stop > 2:
            k["w_in"] = m.sem("w_in")
            moments(nc, k, "mom2")
            qkv(nc, d, k)
            with ExitStack() as c1:
                m1 = Mem(nc, c1, "l1")
                k["S"] = m1.sb("S", [P, ET * HEADS])
                scores(nc, d, k)
                softmax_shift(nc, d, k)
                k["acc1"] = m1.sb("acc1", [P, NT, D + HEADS])
                aggregate1(nc, d, k)
                add_acc1(nc, k)
        if stop > 3:
            moments(nc, k, "mom3")
            k["W1"] = m.sb("W1", [P, NE, 2, HID])
            k["W2"] = m.sb("W2", [P, NE, HC, D])
            k["b1"] = m.sb("b1", [P, NE, HC])
            k["XNT"] = [m.sb(f"XNT{c}", [P, NPAD]) for c in range(2)]
            k["wfull"] = m.sb("wfull", [P, NT, NE])
            k["wflat"] = k["wfull"][:, :, :].rearrange("p n x -> p (n x)")
            with nc.Block() as block:
                @block.sync
                def _(e):
                    e.dma_start(k["W1"][:, :, :, :], d["W1"].rearrange("x (c p) h -> p x c h", p=P)).then_inc(k["w_in"], 16)
                    e.dma_start(k["W2"][:, :, :, :], d["W2"].rearrange("x (c p) h -> p x c h", p=P)).then_inc(k["w_in"], 16)
            route(nc, d, k)
            experts(nc, d, k)
        write_x(nc, d, k)


def kernel(**a):
    import numpy as np
    import concourse.bacc as bacc
    from concourse.bass_utils import run_bass_kernel_spmd

    nc = bacc.Bacc("TRN2", target_bir_lowering=False, num_devices=1)
    f = {n: np.ascontiguousarray(v) for n, v in a.items()}
    g = lambda n: f["L0_gnn_" + n]
    pad = EPAD - EDGES
    src = np.pad(f["src"], (0, pad))
    dst = np.pad(f["dst"], (0, pad), constant_values=NPAD - 1)
    attr = np.pad(f["edge_attr_3"], ((0, pad), (0, 0)))
    arrays = {
        "x": np.pad(f["x"], ((0, NPAD - NODES), (0, 0))),
        "src_pt": src.reshape(ET, P).T, "dst_pt": dst.reshape(ET, P).T,
        "dst_flat": np.pad(dst, (0, P), constant_values=NPAD - 1)[None],
        "attr_pt": attr.reshape(ET, P, 3).transpose(1, 0, 2),
        "ls0T": g("lin_src_w0").T, "ls1T": g("lin_src_w1").T,
        "t00": g("tp1_w00"), "t11": g("tp1_w11"), "t01": g("tp1_w01"), "t10": g("tp1_w10"),
        "lh0": g("lin_hidden_w0"), "lh1": g("lin_hidden_w1"),
        "u00": g("tp2_w00"), "u11": g("tp2_w11"), "u01": g("tp2_w01"), "u10": g("tp2_w10"),
        "lsc": g("lin_scalar_w"),
        "lnsT": f["L0_ffn_weight"].T, "lns_b": f["L0_ffn_bias"].reshape(1, D),
        "wqkv": np.concatenate([f["L1_gnn_Wq"], f["L1_gnn_Wk"], f["L1_gnn_Wv"]], 1),
        "bqkv": np.concatenate([f["L1_gnn_bq"], f["L1_gnn_bk"], f["L1_gnn_bv"]])[None],
        "gamma": f["L1_ffn_gamma"].reshape(2, P).T, "beta": f["L1_ffn_beta"].reshape(2, P).T,
        "Wr": f["L1_ffn_Wr"], "br": f["L1_ffn_br"][None],
        "W1": f["L1_ffn_W1"], "b1": f["L1_ffn_b1"].reshape(NE, HID // P, P).transpose(2, 0, 1),
        "W2": f["L1_ffn_W2"], "b2": f["L1_ffn_b2"],
    }
    arrays = {n: np.ascontiguousarray(v) for n, v in arrays.items()}
    d = {n: nc.dram_tensor("in_" + n, v.shape, mybir.dt.from_np(v.dtype), kind="ExternalInput").ap()
         for n, v in arrays.items()}
    d["sorted"] = nc.dram_tensor("sorted", (EPAD, 8), I32, kind="Internal").ap()
    d["tab0"] = nc.dram_tensor("tab0", (NPAD, T0W), F32, kind="Internal").ap()
    for n in ("qtab", "ktab", "vtab"):
        d[n] = nc.dram_tensor(n, (NPAD, D), F32, kind="Internal").ap()
    d["out"] = nc.dram_tensor("out_x", (NODES, D), F32, kind="ExternalOutput").ap()
    build(nc, d, **OPTIONS)
    r = run_bass_kernel_spmd(nc, [{"in_" + n: v for n, v in arrays.items()}], core_ids=[0])
    return r.results[0]["out_x"]


OPTIONS = {}
```

```python
import concourse.bass as bass
from concourse import mybir
from contextlib import ExitStack

F32 = mybir.dt.float32
BF16 = mybir.dt.bfloat16
I32 = mybir.dt.int32
U32 = mybir.dt.uint32
ALU = mybir.AluOpType
ACT = mybir.ActivationFunctionType
AX = mybir.AxisListType

P = 128
NODES = 3125
NT = 25
NPAD = NT * P
D = 256
MUL = 64
EDGES = 50000
ET = 400
EPAD = ET * P
GT = 4
NG = ET // GT
UN = 4
NI = NG // UN
STEPS = ET + NT - 1
SB = -(-STEPS // GT)
UA = 3
QUN = 10
RING = QUN * GT
T0W = 512
HEADS = 8
HD = 32
A = D + HEADS
C = 1.0 / 8.0
TP = 1.0 / 128.0 ** 0.5
SQ3 = 3.0 ** 0.5
BIG = 3.0e38
NE = 8
HID = 512


def wait(e, sem, count):
    if not isinstance(count, int) or count > 0:
        e.wait_ge(sem, count)


def rolled(e, n, body, first=1, last=1):
    for i in range(first):
        body(i)
    with e.Fori(first, n - last) as i:
        body(i)
    for i in range(n - last, n):
        body(i)


def turns(body, n=NT, bufs=2, first=1):
    def run(e):
        for i in range(bufs * first):
            body(i, i % bufs, i // bufs)
        with e.Fori(first, n // bufs - 1) as it:
            for j in range(bufs):
                body(it * bufs + j, j, it)
        for i in range(bufs * (n // bufs - 1), n):
            body(i, i % bufs, i // bufs)
    return run


def is_last(i, n=NT):
    return isinstance(i, int) and i == n - 1


def tile(t, i):
    if isinstance(i, int):
        return t[:, i, :]
    return t[:, bass.ds(i, 1), :].rearrange("p a w -> p (a w)")


def cols(t, i, w):
    return t[:, i:i + w] if isinstance(i, int) else t[:, bass.ds(i, w)]


def place(t, at, w):
    return cols(t[:, :, :].rearrange("p n w -> p (n w)"), at, w)


def tiles(t, i, n):
    return t[:, i:i + n, :] if isinstance(i, int) else t[:, bass.ds(i, n), :]


class Mem:

    def __init__(self, nc, ctx, tag):
        self.nc, self.ctx, self.tag, self.sems = nc, ctx, tag, []
        ctx.callback(self.clear)

    def sb(self, name, shape, dt=F32):
        return self.ctx.enter_context(self.nc.sbuf_tensor(f"{self.tag}_{name}", shape, dt))

    def ps(self, name, shape, dt=F32):
        return self.ctx.enter_context(self.nc.psum_tensor(f"{self.tag}_{name}", shape, dt))

    def sem(self, name):
        self.sems.append(self.nc.alloc_semaphore(name=f"{self.tag}_{name}"))
        return self.sems[-1]

    def clear(self):
        if self.sems:
            self.nc.clear_and_free_semaphores(self.sems)
            self.nc.all_engine_barrier()


FW = EPAD // P
SC = 8
SE = EPAD // SC


def edges_in(nc, d, k):
    with ExitStack() as ctx:
        m = Mem(nc, ctx, "in")
        flat = m.sb("flat", [P, FW + 1], I32)
        drop = m.sb("drop", [P, FW])
        drops = m.sb("drops", [P, 1])
        ones = m.sb("ones", [P, 1])
        flag = m.sb("flag", [1, 1], I32)
        ps = m.ps("ps", [P, 512])
        loaded, cmp_ok, sum_ok, one_ok, tot, flag_ok = (m.sem(n) for n in (
            "loaded", "cmp_ok", "sum_ok", "one_ok", "tot", "flag_ok"))
        with nc.Block() as block:
            @block.sync
            def _(e):
                e.dma_start(flat[:, :], bass.AP(d["dst_flat"].tensor, 0, [[FW, P], [1, FW + 1]])).then_inc(loaded, 16)
                e.dma_start(k["dst_i"][:, :], d["dst_pt"]).then_inc(loaded, 16)
                e.dma_start(k["src_i"][:, :], d["src_pt"]).then_inc(loaded, 16)
                e.dma_start(k["attr"][:, :, :], d["attr_pt"]).then_inc(loaded, 16)
                e.wait_ge(loaded, 64)

            @block.vector
            def _(e):
                e.memset(ones[:, :], 1.0).then_inc(one_ok, 1)
                e.wait_ge(loaded, 64)
                e.tensor_tensor(drop[:, :], flat[:, 0:FW], flat[:, 1:FW + 1], ALU.is_gt).then_inc(cmp_ok, 1)
                e.wait_ge(cmp_ok, 1)
                e.tensor_reduce(drops[:, :], drop[:, :], AX.X, ALU.add).then_inc(sum_ok, 1)
                e.wait_ge(tot, 1)
                e.tensor_copy(flag[:, :], ps[0:1, 0:1]).then_inc(flag_ok, 1)

            @block.tensor
            def _(e):
                e.wait_ge(one_ok, 1)
                e.wait_ge(sum_ok, 1)
                e.matmul(ps[0:1, 0:1], drops[:, :], ones[:, :], start=True, stop=True).then_inc(tot, 1)
        sort_edges(nc, d, k, flag)


def sort_edges(nc, d, k, flag):
    with ExitStack() as ctx:
        m = Mem(nc, ctx, "sort")
        raw = m.sb("raw", [P, SE], I32)
        keys = m.sb("keys", [P, SE])
        tno = m.sb("tno", [P, SE])
        junk = m.sb("junk", [P, SE])
        key = m.sb("key", [P, ET])
        part = m.sb("part", [P, SC + 1, ET])
        rank_f = m.sb("rank_f", [P, ET])
        rank = m.sb("rank", [P, ET], I32)
        tri = m.sb("tri", [P, P])
        junk2 = m.sb("junk2", [P, P])
        tcol = m.sb("tcol", [P, ET])
        rows = m.sb("rows", [P, ET, 8], I32)
        row = m.sb("row", [P, 8], I32)
        at = m.sb("at", [P, 1], I32)
        scr = m.sb("scr", [P, 2])
        S = m.sem
        raw_in, keyed, tied, counted, ranked, made, staged, carried, put, back, own = (S(n) for n in (
            "raw_in", "keyed", "tied", "counted", "ranked", "made", "staged", "carried", "put", "back", "own"))
        with nc.Block() as block:
            @block.gpsimd
            def _(e):
                unsorted = e.value_load(flag[0:1, 0:1], min_val=0, max_val=EPAD)
                with e.If(unsorted > 0):
                    e.memset(scr[:, :], 0.0).then_inc(carried, 1)
                    e.memset(tri[:, :], 1.0).then_inc(made, 1)
                    e.wait_ge(made, 1)
                    e.affine_select(out=tri[:, :], in_=tri[:, :], compare_op=ALU.is_gt, fill=0.0, base=0,
                                    pattern=[[-1, P]], channel_multiplier=1).then_inc(made, 1)
                    e.iota(tcol[:, :], pattern=[[1, ET]], base=0, channel_multiplier=0,
                           allow_small_or_imprecise_dtypes=True).then_inc(made, 1)
                    for c in range(SC):
                        wait(e, counted, c)
                        e.dma_start(raw[:, :], d["dst_flat"][0:1, c * SE:(c + 1) * SE].to_broadcast([P, SE])
                                    ).then_inc(raw_in, 16)
                        e.iota(tno[:, :], pattern=[[1, SE // P], [0, P]], base=c * (SE // P), channel_multiplier=0,
                               allow_small_or_imprecise_dtypes=True).then_inc(made, 1)
                    e.wait_ge(ranked, 1)

                    def scatter(t):
                        wait(e, put, t * 16)
                        e.wait_ge(carried, 2 * t + 1)
                        e.tensor_tensor(scr[:, 0:1], scr[:, 1:2], scr[:, 1:2], ALU.add).then_inc(carried, 1)
                        e.tensor_copy(row[:, :], tile(rows, t)).then_inc(staged, 1)
                        e.tensor_copy(at[:, :], cols(rank, t, 1)).then_inc(staged, 1)
                        e.wait_ge(staged, 2 * t + 2)
                        e.wait_ge(carried, 2 * t + 2)
                        e.tensor_tensor(scr[:, 0:1], scr[:, 1:2], scr[:, 1:2], ALU.add).then_inc(carried, 1)
                        e.indirect_dma_start(out=d["sorted"], out_offset=bass.IndirectOffsetOnAxis(ap=at[:, :], axis=0),
                                             in_=row[:, :], in_offset=None).then_inc(put, 16)
                    rolled(e, ET, scatter)
                    e.wait_ge(put, ET * 16)
                    for c in range(SC):
                        w = ET // SC
                        e.dma_start(rows[:, c * w:(c + 1) * w, :],
                                    d["sorted"][c * SE:(c + 1) * SE, :].rearrange("(t p) c -> p t c", p=P)).then_inc(back, 16)
                        e.wait_ge(back, 16 * (c + 1))

            @block.vector
            def _(e):
                unsorted = e.value_load(flag[0:1, 0:1], min_val=0, max_val=EPAD)
                with e.If(unsorted > 0):
                    n = [0]

                    def link(ins):
                        ins.then_inc(own, 1)
                        n[0] += 1
                        e.wait_ge(own, n[0])
                    e.wait_ge(made, 3)
                    link(e.scalar_tensor_tensor(key[:, :], k["dst_i"][:, :], 512.0, tcol[:, :], ALU.mult, ALU.add))
                    for c in range(SC):
                        e.wait_ge(raw_in, (c + 1) * 16)
                        e.wait_ge(made, c + 4)
                        e.scalar_tensor_tensor(keys[:, :], raw[:, :], 512.0, tno[:, :], ALU.mult, ALU.add).then_inc(keyed, 1)
                        e.wait_ge(keyed, c + 1)

                        def count(t, c=c):
                            e.wait_ge(tied, t + 1 + c * (ET + SE // P))
                            e.tensor_scalar(junk[:, :], keys[:, :], cols(key, t, 1), 0.0, ALU.is_lt, ALU.add,
                                            accum_out=cols(part[:, c, :], t, 1)).then_inc(tied, 1)
                        if c == 0:
                            e.memset(junk2[:, :], 0.0).then_inc(tied, 1)
                        rolled(e, ET, count)

                        def tie(i, c=c):
                            e.wait_ge(tied, i + 1 + ET + c * (ET + SE // P))
                            e.scalar_tensor_tensor(junk2[:, :], cols(keys, i * P, P), cols(key, i + c * (SE // P), 1), tri[:, :],
                                                   ALU.is_equal, ALU.mult,
                                                   accum_out=cols(part[:, SC, :], i + c * (SE // P), 1)).then_inc(tied, 1)
                        rolled(e, SE // P, tie)
                        e.wait_ge(tied, 1 + (c + 1) * (ET + SE // P))
                        e.memset(junk2[:, 0:1], 0.0).then_inc(counted, 1)
                        e.wait_ge(counted, c + 1)
                    link(e.tensor_reduce(rank_f[:, :], part[:, :, :].rearrange("p c t -> p t c"), AX.X, ALU.add))
                    link(e.tensor_copy(rank[:, :], rank_f[:, :]))
                    link(e.memset(rows[:, :, :], 0))
                    link(e.tensor_copy(rows[:, :, 0:1], k["src_i"][:, :].unsqueeze(2)))
                    link(e.tensor_copy(rows[:, :, 1:2], k["dst_i"][:, :].unsqueeze(2)))
                    e.tensor_copy(rows[:, :, 2:5].bitcast(F32), k["attr"][:, :, :]).then_inc(ranked, 1)
                    e.wait_ge(back, 16 * SC)
                    link(e.tensor_copy(k["src_i"][:, :].unsqueeze(2), rows[:, :, 0:1]))
                    link(e.tensor_copy(k["dst_i"][:, :].unsqueeze(2), rows[:, :, 1:2]))
                    link(e.tensor_copy(k["attr"][:, :, :], rows[:, :, 2:5].bitcast(F32)))


def setup(nc, d, k):
    with ExitStack() as ctx:
        m = Mem(nc, ctx, "setup")
        w = m.sb("w", [64, 13, 64])
        a = m.sb("a", [64, 4, 64])
        wt = m.sb("wt", [64, 7, 64])
        dst_i = k["dst_i"]
        tile_i = m.sb("tile_i", [P, ET], I32)
        tile_f = m.sb("tile_f", [P, ET])
        last_row = m.sb("last_row", [P, P])
        ends = m.sb("ends", [P, ET])
        hit = m.sb("hit", [P, ET])
        step_tile = m.sb("step_tile", [P, 4])
        tcol = m.sb("tcol", [P, 4])
        tbc = m.sb("tbc", [P, 4, P])
        nbase = m.sb("nbase", [P, 512])
        walk_i, walk_m, walk_d = (m.sb(n, [1, 512], I32) for n in ("walk_i", "walk_m", "walk_d"))
        dT = m.sb("dT", [P, 4, P])
        pick = m.sb("pick", [P, 4, 512])
        attr = k["attr"]
        sq = m.sb("sq", [P, ET, 3])
        norm = m.sb("norm", [P, ET])
        norm2 = m.sb("norm2", [P, ET])
        inv = m.sb("inv", [P, ET])
        ia = m.sb("ia", [P, 512], I32)
        ps_w = m.ps("ps_w", [P, 512])
        ps_o = m.ps("ps_o", [P, 512])
        ps_e = m.ps("ps_e", [P, 512])
        ps_r = m.ps("ps_r", [P, 512])
        ps_d = m.ps("ps_d", [P, 512])
        ps_k = m.ps("ps_k", [P, 512])
        w_in, x_in = m.sem("w_in"), m.sem("x_in")
        made, iota_ok = m.sem("made"), m.sem("iota_ok")
        pe1, ev1, pe2, ev2, pe3, ev3 = (m.sem(n) for n in ("pe1", "ev1", "pe2", "ev2", "pe3", "ev3"))
        sq_ok, sqrt_ok, chain, walk, walk_pe = (m.sem(n) for n in ("sq_ok", "sqrt_ok", "chain", "walk", "walk_pe"))
        names = ["ls0T", "ls1T", "t00", "t11", "t01", "t10", "lh0", "lh1", "u00", "u11", "u01", "u10"]
        W = {n: w[:, i, :] for i, n in enumerate(names)}
        with nc.Block() as block:
            @block.sync
            def _(e):
                e.dma_start(k["X"][:, :, :], d["x"].rearrange("(n p) c -> p n c", p=P)).then_inc(x_in, 16)
                e.wait_ge(x_in, 16)

            @block.scalar
            def _(e):
                for i, n in enumerate(names):
                    e.dma_start(w[:, i, :], d[n]).then_inc(w_in, 16)
                e.dma_start(k["LSC2"][0:64, :], d["lsc"]).then_inc(w_in, 16)
                e.dma_start(k["LSC2"][64:128, :], d["lsc"]).then_inc(w_in, 16)
                e.wait_ge(w_in, 14 * 16)
                e.wait_ge(chain, 2)
                e.activation(norm[:, :], norm2[:, :], ACT.Sqrt).then_inc(sqrt_ok, 1)

            @block.gpsimd
            def _(e):
                e.iota(k["iota"][:, :], pattern=[[1, 512]], base=0, channel_multiplier=0,
                       allow_small_or_imprecise_dtypes=True).then_inc(iota_ok, 1)
                e.memset(k["ident"][:, :], 0.0).then_inc(made, 1)
                e.memset(last_row[:, :], 0.0).then_inc(made, 1)
                e.memset(wt[:, :, :], 0.0).then_inc(made, 1)
                e.memset(k["blockww"][:, :], 0.0).then_inc(made, 1)
                e.wait_ge(made, 2)
                e.affine_select(out=k["ident"][:, :], in_=k["ident"][:, :], compare_op=ALU.not_equal, fill=1.0,
                                base=0, pattern=[[-1, P]], channel_multiplier=1).then_inc(made, 1)
                e.affine_select(out=last_row[:, :], in_=last_row[:, :], compare_op=ALU.not_equal, fill=1.0,
                                base=-(P - 1), pattern=[[0, P]], channel_multiplier=1).then_inc(made, 1)
                e.iota(step_tile[:, :], pattern=[[P, 4]], base=0, channel_multiplier=1,
                       allow_small_or_imprecise_dtypes=True).then_inc(made, 1)

            @block.vector
            def _(e):
                n = [0]

                def link(ins):
                    ins.then_inc(chain, 1)
                    n[0] += 1
                    e.wait_ge(chain, n[0])
                link(e.tensor_tensor(sq[:, :, :], attr[:, :, :], attr[:, :, :], ALU.mult))
                link(e.tensor_reduce(norm2[:, :], sq[:, :, :], AX.X, ALU.add))
                link(e.tensor_copy(k["dst_f"][:, :], dst_i[:, :]))
                link(e.tensor_single_scalar(tile_i[:, :], dst_i[:, :], 7, ALU.arith_shift_right))
                link(e.tensor_copy(tile_f[:, :], tile_i[:, :]))
                e.wait_ge(sqrt_ok, 1)
                link(e.tensor_scalar_add(norm2[:, :], norm[:, :], 1e-12))
                link(e.reciprocal(inv[:, :], norm2[:, :]))
                link(e.tensor_tensor(k["r"][:, :, :], attr[:, :, :],
                                     inv[:, :].unsqueeze(2).to_broadcast([P, ET, 3]), ALU.mult))
                link(e.tensor_tensor(sq[:, :, :], k["r"][:, :, :], k["r"][:, :, :], ALU.mult))
                link(e.tensor_reduce(k["s2"][:, :], sq[:, :, :], AX.X, ALU.add))
                e.wait_ge(walk_pe, 1)
                e.wait_ge(iota_ok, 1)
                e.wait_ge(made, 7)
                link(e.scalar_tensor_tensor(ends[:, :], ps_r[:, 0:ET], 1.0, k["iota"][:, 0:ET], ALU.add, ALU.add))
                for c in range(4):
                    link(e.tensor_scalar(hit[:, :], ends[:, :], step_tile[:, c:c + 1], 0.0, ALU.is_le, ALU.add,
                                         accum_out=tcol[:, c:c + 1]))
                e.tensor_copy(tbc[:, :, :], tcol[:, :].unsqueeze(2).to_broadcast([P, 4, P])).then_inc(walk, 1)
                e.wait_ge(walk_pe, 2)
                link(e.tensor_copy(walk_i[:, :], ps_e[0:1, :]))
                link(e.tensor_tensor(nbase[:, :], k["iota"][:, :], ps_e[:, :], ALU.subtract))
                link(e.tensor_single_scalar(k["walk_n"][:, :], nbase[0:1, :], float(A), ALU.mult))
                assert all((t * 1639 >> 16) == t // RING for t in range(ET))
                link(e.tensor_single_scalar(walk_m[:, :], walk_i[:, :], 1639, ALU.mult))
                link(e.tensor_single_scalar(walk_d[:, :], walk_m[:, :], 16, ALU.arith_shift_right))
                link(e.memset(k["walk_q"][:, :], 0))
                by_block = k["walk_q"][:, :].rearrange("p (b a) -> p b a", a=2 * GT)
                steps = lambda t: t[:, 0:STEPS].rearrange("p (b a) -> p b a", a=GT)
                link(e.scalar_tensor_tensor(walk_m[:, :], walk_d[:, :], -RING, walk_i[:, :], ALU.mult, ALU.add))
                link(e.tensor_single_scalar(k["walk_slot"][:, :], walk_m[:, :], A, ALU.mult))
                link(e.tensor_single_scalar(by_block[:, 0:SB, 0:GT], steps(walk_m), D, ALU.mult))
                link(e.tensor_single_scalar(by_block[:, 1:SB + 1, GT:2 * GT], steps(walk_i), HEADS, ALU.mult))
                for c in range(4):
                    link(e.tensor_scalar(pick[:, c, :], ps_e[:, :], step_tile[:, c:c + 1], None, ALU.is_equal))
                e.wait_ge(walk_pe, 3)
                for c in range(4):
                    w = min(P, ET - c * P)
                    link(e.tensor_copy(dT[0:w, c, :], ps_d[0:w, c * P:(c + 1) * P]))
                e.engine_nop().then_inc(walk, 1)
                e.wait_ge(walk_pe, 4)
                link(e.scalar_tensor_tensor(k["dstep"][:, :], nbase[:, :], -float(P), ps_k[:, :], ALU.mult, ALU.add))
                e.wait_ge(pe1, 1)
                e.tensor_copy(a[:, :, :], ps_w[0:64, 0:256].rearrange("p (a b) -> p a b", a=4)).then_inc(ev1, 1)
                e.wait_ge(pe2, 1)
                s = C * TP * C
                e.tensor_scalar_mul(wt[:, 0:2, :], ps_w[0:64, 256:384].rearrange("p (a b) -> p a b", a=2), s)
                e.tensor_scalar_mul(wt[:, 5, :], ps_w[0:64, 384:448], s)
                e.tensor_scalar_mul(wt[:, 3, :], ps_w[0:64, 448:512], s)
                e.tensor_scalar_mul(wt[:, 4, :], ps_w[0:64, 448:512], s).then_inc(ev2, 1)
                e.wait_ge(pe3, 1)
                e.tensor_copy(k["WH"][:, 0:64], ps_o[:, 0:64])
                e.tensor_scalar_mul(k["WH"][:, 64:128], ps_o[:, 0:64], -0.01)
                e.tensor_scalar_mul(k["WO"][:, 0:64], ps_o[:, 64:128], TP)
                e.tensor_scalar_mul(k["WO"][:, 64:128], ps_o[:, 128:192], SQ3 * TP)
                e.tensor_scalar_mul(k["WQ"][:, :], ps_o[0:64, 192:256], SQ3 * TP)
                e.tensor_scalar_mul(k["blockww"][0:64, 0:64], ps_o[0:64, 256:320], TP)
                e.tensor_scalar_mul(k["blockww"][64:128, 64:128], ps_o[64:128, 256:320], TP)
                e.wait_ge(w_in, 14 * 16)
                e.tensor_scalar_mul(k["LSC2"][0:64, :], k["LSC2"][0:64, :], C)
                e.tensor_scalar_mul(k["LSC2"][64:128, :], k["LSC2"][64:128, :], -C).then_inc(ev3, 1)

            @block.tensor
            def _(e):
                e.wait_ge(made, 7)
                e.wait_ge(chain, 5)
                e.matmul(ps_r[:, 0:ET], last_row[:, :], tile_f[:, :], start=True, stop=True).then_inc(walk_pe, 1)
                e.wait_ge(walk, 1)
                for c in range(4):
                    x = e.matmul(ps_e[:, c * P:(c + 1) * P], tbc[:, c, :], k["ident"][:, :], start=True, stop=True)
                x.then_inc(walk_pe, 1)
                for c in range(4):
                    w = min(P, ET - c * P)
                    x = e.transpose(ps_d[0:w, c * P:(c + 1) * P], k["dst_f"][:, c * P:c * P + w], k["ident"][:, :])
                x.then_inc(walk_pe, 1)
                e.wait_ge(walk, 2)
                for c in range(4):
                    w = min(P, ET - c * P)
                    x = e.matmul(ps_k[:, :], dT[0:w, c, :], pick[0:w, c, :], start=c == 0, stop=c == 3)
                x.then_inc(walk_pe, 1)
                e.wait_ge(w_in, 14 * 16)
                for i, (l, r) in enumerate((("t00", "ls0T"), ("t11", "ls1T"), ("t01", "ls0T"), ("t10", "ls1T"))):
                    x = e.matmul(ps_w[0:64, i * 64:i * 64 + 64], W[l], W[r], start=True, stop=True)
                x.then_inc(pe1, 1)
                e.wait_ge(ev1, 1)
                for i, l in enumerate(("lh0", "lh0", "lh1", "lh1")):
                    x = e.matmul(ps_w[0:64, 256 + i * 64:320 + i * 64], W[l], a[:, i, :], start=True, stop=True)
                x.then_inc(pe2, 1)
                e.wait_ge(ev2, 1)
                pair = lambda i: wt[:, i:i + 2, :].rearrange("p a b -> p (a b)")
                e.matmul(ps_o[:, 0:64], pair(0), k["ident"][0:64, 0:64], start=True, stop=True)
                e.matmul(ps_o[:, 64:128], pair(0), W["u00"], start=True, stop=False)
                e.matmul(ps_o[:, 64:128], pair(2), W["u11"], start=False, stop=True)
                e.matmul(ps_o[:, 128:192], pair(0), W["u01"], start=True, stop=False)
                e.matmul(ps_o[:, 128:192], pair(5), W["u10"], start=False, stop=True)
                e.matmul(ps_o[:, 192:256], pair(5), W["u11"], start=True, stop=True)
                e.matmul(ps_o[:, 256:320], pair(3), W["u10"], start=True, stop=True).then_inc(pe3, 1)


def moments(nc, k, tag):
    with ExitStack() as ctx:
        m = Mem(nc, ctx, tag)
        stats = m.sb("stats", [P, NT, 6])
        var = m.sb("var", [P, NT])
        root = m.sb("root", [P, NT])
        st, mv, ve, sq = m.sem("st"), m.sem("mv"), m.sem("ve"), m.sem("sq")
        with nc.Block() as block:
            @block.vector
            def _(e):
                def stat(i):
                    e.bn_stats(tile(stats, i), tile(k["X"], i)).then_inc(st, 1)
                rolled(e, NT, stat)

                def aggr(i):
                    wait(e, st, NT)
                    e.bn_aggr(tile(k["mv"], i), tile(stats, i)).then_inc(mv, 1)
                for i in range(NT):
                    aggr(i)
                e.wait_ge(mv, NT)
                e.tensor_scalar_add(var[:, :], k["mv"][:, :, 1], 1e-5).then_inc(ve, 1)
                e.wait_ge(sq, 1)
                e.reciprocal(k["rstd"][:, :], root[:, :]).then_inc(ve, 1)

            @block.scalar
            def _(e):
                e.wait_ge(ve, 1)
                e.activation(root[:, :], var[:, :], ACT.Sqrt).then_inc(sq, 1)


def nodes0(nc, d, k):
    with ExitStack() as ctx:
        m = Mem(nc, ctx, "nodes0")
        row = m.sb("row", [P, 4, T0W])
        tt = m.sb("tt", [P, 2, 384])
        ps_t = m.ps("ps_t", [P, 2, 512])
        ps_y = m.ps("ps_y", [P, 2, 512])
        normed, added, t_ps, t_sb, y_ps, y_sb = (m.sem(n) for n in ("normed", "added", "t_ps", "t_sb", "y_ps", "y_sb"))
        stored = [m.sem(f"stored{i}") for i in range(4)]
        table = d["tab0"].rearrange("(n p) c -> n p c", p=P)

        with nc.Block() as block:
            @block.vector
            def _(e):
                def body(i, j, it):
                    wait(e, stored[j], it * 16)
                    X = tile(k["X"], i)
                    mean = cols(k["mvf"], i * 2, 1)
                    rs = cols(k["rstd"], i, 1)
                    e.tensor_scalar(row[:, j, 0:64], X[:, 0:64], mean, rs, ALU.subtract, ALU.mult).then_inc(normed, 1)
                    e.tensor_scalar(row[:, j, 64:256].rearrange("p (m u) -> p u m", m=3),
                                    X[:, 64:256].rearrange("p (u m) -> p u m", m=3),
                                    mean, rs, ALU.subtract, ALU.mult).then_inc(normed, 1)
                    e.wait_ge(normed, i * 2 + 2)
                    e.tensor_tensor(X[:, 0:64], X[:, 0:64], row[:, j, 0:64], ALU.add)
                    e.tensor_tensor(X[:, 64:256].rearrange("p (u m) -> p u m", m=3),
                                    X[:, 64:256].rearrange("p (u m) -> p u m", m=3),
                                    row[:, j, 64:256].rearrange("p (m u) -> p u m", m=3), ALU.add).then_inc(added, 1)
                turns(body, bufs=4)(e)

            @block.tensor
            def _(e):
                def inputs(i, j):
                    e.wait_ge(normed, i * 2 + 2)
                    wait(e, t_sb, i - 1)
                    e.transpose(ps_t[:, j % 2, 0:128], row[:, j, 64:192], k["ident"][:, :])
                    e.transpose(ps_t[0:64, j % 2, 128:256], row[:, j, 192:256], k["ident"][:, :])
                    e.transpose(ps_t[0:64, j % 2, 256:384], row[:, j, 0:64], k["ident"][:, :]).then_inc(t_ps, 1)

                def body(i, j, it):
                    if not is_last(i):
                        inputs(i + 1, (j + 1) % 4)
                    e.wait_ge(t_sb, i + 1)
                    wait(e, y_sb, i - 1)
                    b = j % 2
                    e.matmul(ps_y[:, b, 0:128], tt[:, b, 0:128], k["blockww"][:, :], start=True, stop=True)
                    e.matmul(ps_y[:, b, 128:192], tt[0:64, b, 128:256], k["blockww"][0:64, 0:64], start=True, stop=True)
                    e.matmul(ps_y[:, b, 192:256], tt[0:64, b, 256:384], k["WQ"][:, :], start=True, stop=True).then_inc(y_ps, 1)
                inputs(0, 0)
                turns(body, bufs=4)(e)

            @block.scalar
            def _(e):
                def inputs(i, b):
                    e.wait_ge(t_ps, i + 1)
                    wait(e, y_ps, i - 1)
                    e.activation(tt[:, b, 0:128], ps_t[:, b, 0:128], ACT.Copy)
                    e.activation(tt[0:64, b, 128:384], ps_t[0:64, b, 128:384], ACT.Copy).then_inc(t_sb, 1)

                def body(i, j, it):
                    if not is_last(i):
                        inputs(i + 1, (j + 1) % 2)
                    e.wait_ge(y_ps, i + 1)
                    e.wait_ge(normed, i * 2 + 2)
                    e.activation(row[:, j, 256:512], ps_y[:, j % 2, 0:256], ACT.Copy).then_inc(y_sb, 1)
                inputs(0, 0)
                turns(body, bufs=4)(e)

            @block.sync
            def _(e):
                def body(i, j, it):
                    e.wait_ge(y_sb, i + 1)
                    e.wait_ge(normed, i * 2 + 2)
                    dst = table[i, :, :] if isinstance(i, int) else table[bass.ds(i, 1), :, :].rearrange("a p c -> (a p) c")
                    e.dma_start(dst, row[:, j, :]).then_inc(stored[j], 16)
                turns(body, bufs=4)(e)
                for j in range(4):
                    e.wait_ge(stored[j], 16 * len(range(j, NT, 4)))


def walk_values(nc, e, k, name, blk, blocks=1):
    top, n = {"walk_n": ((NT - 1) * A, GT), "walk_slot": ((RING - 1) * A, GT),
              "walk_q": ((QUN * GT - 1) * D, 2 * GT)}[name]
    at = cols(k[name][0:1, :], blk * n, n * blocks)
    v = nc.values_load_multi_w_load_instructions(
        at, engines=(e.engine,), min_val=0, max_val=top, skip_runtime_bounds_check_because=WALK)[1]
    if name == "walk_q":
        return v[:GT], [nc.s_assert_within(x, 0, (ET - 1) * HEADS, skip_runtime_bounds_check_because=WALK) for x in v[GT:]]
    return v


WALK = "the walk visits each edge tile and each node tile in order, in as many steps as it has"


def one_hots(e, k, hot, blk):
    return e.tensor_tensor(hot, k["iota"][:, 0:P].unsqueeze(1).to_broadcast([P, GT, P]),
                           cols(k["dstep"], blk * GT, GT).unsqueeze(2).to_broadcast([P, GT, P]), ALU.is_equal)


def gathers(e, scr, carried, staged, landed, table, buffer, stage, used, un=UN, after=lambda g, b: None):
    e.memset(scr[:, :], 0.0).then_inc(carried, 1)

    def body(it):
        for b in range(un):
            g = it * un + b
            for sem, count in used(g):
                wait(e, sem, count)
            e.wait_ge(staged, g + 1)
            e.wait_ge(carried, g + 1)
            e.tensor_tensor(scr[:, 0:1], scr[:, 1:2], scr[:, 1:2], ALU.add).then_inc(carried, 1)
            for j in range(GT):
                e.indirect_dma_start(out=buffer(b, j), out_offset=None, in_=table,
                                     in_offset=bass.IndirectOffsetOnAxis(ap=stage[:, b, j:j + 1], axis=0)
                                     ).then_inc(landed[b], 16)
            after(g, b)
    rolled(e, NG // un, body)


def stage_sources(e, k, stage, g, b, it, landed, staged):
    wait(e, landed[b], it * 16 * GT)
    e.activation(stage[:, b, :], cols(k["src_i"], g * GT, GT), ACT.Copy).then_inc(staged, 1)


def edges0(nc, d, k):
    with ExitStack() as ctx:
        m = Mem(nc, ctx, "edges0")
        G = m.sb("G", [P, UN, GT, T0W])
        stage = m.sb("stage", [P, UN, GT], I32)
        scr = m.sb("scr", [P, 2])
        ring = m.sb("ring", [P, RING, A])
        xm = m.sb("xm", [P, 2, GT, 3, 64])
        xs = m.sb("xs", [P, GT, 64])
        XT = m.sb("XT", [P, 2, GT * P])
        HT = m.sb("HT", [P, 2, GT * P])
        mx = m.sb("mx", [P, GT])
        nm = m.sb("nm", [P, GT])
        ex = m.sb("ex", [P, GT, 64])
        en, zs, z, rz, enr = (m.sb(n, [P, GT]) for n in ("en", "zs", "z", "rz", "enr"))
        rr = m.sb("rr", [P, GT, 3])
        o0 = m.sb("o0", [P, GT, 64])
        o1 = m.sb("o1", [P, GT, 3, 64])
        ye = m.sb("ye", [P, GT, 192])
        hot = m.sb("hot", [P, 2, GT, P])
        ps_x = m.ps("ps_x", [P, GT * P])
        ps_h = m.ps("ps_h", [P, GT * P])
        ps_p = m.ps("ps_p", [P, GT * P])
        ps_s = m.ps("ps_s", [P, 512])
        ps_a = [m.ps(f"ps_a{i}", [P, 512]) for i in range(GT)]
        S = m.sem
        landed = [S(f"landed{i}") for i in range(UN)]
        staged, xm_ok, xs_ok, xr_ok, xt_ps, xt_sb, h_ps, h_sb, p_ps, sc_ps = (S(n) for n in (
            "staged", "xm_ok", "xs_ok", "xr_ok", "xt_ps", "xt_sb", "h_ps", "h_sb", "p_ps", "sc_ps"))
        mx_ok, nm_ok, ex_ok, en_ok, z_ok, rz_ok, enr_ok, rr_ok, o0_ok, uv_ok, ud_ok, m0_ok, m1_ok = (S(n) for n in (
            "mx_ok", "nm_ok", "ex_ok", "en_ok", "z_ok", "rz_ok", "enr_ok", "rr_ok", "o0_ok", "uv_ok", "ud_ok", "m0_ok", "m1_ok"))
        hot_ok, sum_ps, acc_ok, scr_ok = (S(n) for n in ("hot_ok", "sum_ps", "acc_ok", "scr_ok"))
        acc = k["acc0"]
        four = lambda t: t[:, 0:GT * P].rearrange("p (t c) -> p t c", t=GT)

        with nc.Block() as block:
            @block.gpsimd
            def _(e):
                def direct(g, b):
                    e.wait_ge(xm_ok, g + 1)
                    wait(e, xr_ok, g)
                    e.tensor_tensor(xs[:, :, :], xm[:, b % 2, :, 0, :], xm[:, b % 2, :, 1, :], ALU.add).then_inc(xs_ok, 1)
                    e.wait_ge(xs_ok, g + 1)
                    e.tensor_tensor(G[:, b, :, 64:128], xs[:, :, :], xm[:, b % 2, :, 2, :], ALU.add).then_inc(xr_ok, 1)

                gathers(e, scr, scr_ok, staged, landed, d["tab0"], lambda b, j: G[:, b, j, :], stage,
                        lambda g: [(uv_ok, g - UN + 1), (o0_ok, g - UN + 1), (xt_ps, g - UN + 1)],
                        after=lambda g, b: None if isinstance(g, int) and g == 0 else direct(g - 1, (b - 1) % UN))
                direct(NG - 1, (NG - 1) % UN)

            @block.vector
            def _(e):
                e.memset(acc[:, :, :], 0.0).then_inc(acc_ok, 1)
                e.wait_ge(acc_ok, 1)

                def turn(g, b, it):
                    e.wait_ge(landed[b], (it + 1) * 16 * GT)
                    x1 = G[:, b, :, 64:256].rearrange("p t (m u) -> p t m u", m=3)
                    r = tiles(k["r"], g * GT, GT).unsqueeze(3).to_broadcast([P, GT, 3, 64])
                    wait(e, xr_ok, g - 1)
                    e.tensor_tensor(xm[:, b % 2, :, :, :], x1, r, ALU.mult).then_inc(xm_ok, 1)

                def largest(g):
                    e.wait_ge(sc_ps, g + 1)
                    wait(e, nm_ok, g)
                    sc = ps_s[:, 0:GT * 64].rearrange("p (t c) -> p t c", t=GT)
                    e.tensor_reduce(mx[:, :], sc, AX.X, ALU.max).then_inc(mx_ok, 1)
                    e.wait_ge(mx_ok, g + 1)
                    wait(e, en_ok, g)
                    wait(e, ex_ok, g)
                    e.tensor_scalar(nm[:, :], mx[:, :], -1.0, 0.0, ALU.mult, ALU.min).then_inc(nm_ok, 1)

                def weights(g, between):
                    e.wait_ge(en_ok, g + 1)
                    e.wait_ge(ex_ok, g + 1)
                    wait(e, rz_ok, g)
                    e.scalar_tensor_tensor(z[:, :], en[:, :], 192.0, zs[:, :], ALU.mult, ALU.add).then_inc(z_ok, 1)
                    between()
                    e.wait_ge(z_ok, g + 1)
                    wait(e, m0_ok, g)
                    e.reciprocal(rz[:, :], z[:, :]).then_inc(rz_ok, 1)
                    e.wait_ge(rz_ok, g + 1)
                    wait(e, uv_ok, g)
                    wait(e, m1_ok, g)
                    e.tensor_tensor(enr[:, :], en[:, :], rz[:, :], ALU.mult).then_inc(enr_ok, 1)
                    e.wait_ge(enr_ok, g + 1)
                    e.tensor_tensor(rr[:, :, :], tiles(k["r"], g * GT, GT),
                                    enr[:, :].unsqueeze(2).to_broadcast([P, GT, 3]), ALU.mult).then_inc(rr_ok, 1)

                def slot_of(g):
                    return (g % (RING // GT)) * GT

                def scalar_sum(g, b, i):
                    if i == 0:
                        e.wait_ge(p_ps, g + 1)
                        wait(e, m0_ok, g)
                    x = e.scalar_tensor_tensor(o0[:, i, :], G[:, b, i, 448:512], cols(k["s2"], g * GT + i, 1),
                                               four(ps_p)[:, i, 0:64], ALU.mult, ALU.add)
                    if i == GT - 1:
                        x.then_inc(o0_ok, 1)

                def scalar_part(g, i):
                    if i == 0:
                        e.wait_ge(o0_ok, g + 1)
                        e.wait_ge(rz_ok, g + 1)
                    x = e.scalar_tensor_tensor(tile(ring, slot_of(g) + i)[:, 0:64], o0[:, i, :], rz[:, i:i + 1], ex[:, i, :],
                                               ALU.mult, ALU.mult)
                    if i == GT - 1:
                        x.then_inc(m0_ok, 1)

                def turned(g):
                    n = GT - UA
                    e.wait_ge(rr_ok, g + 1)
                    wait(e, m1_ok, g)
                    e.tensor_tensor(o1[:, UA:GT, :, :], four(ps_p)[:, UA:GT, 64:128].unsqueeze(2).to_broadcast([P, n, 3, 64]),
                                    rr[:, UA:GT, :].unsqueeze(3).to_broadcast([P, n, 3, 64]), ALU.mult).then_inc(ud_ok, 1)

                def vector_part(g):
                    e.wait_ge(uv_ok, g + 1)
                    e.wait_ge(ud_ok, g + 1)
                    o = o1[:, :, :, :].rearrange("p t m u -> p t (m u)")
                    e.tensor_tensor(tiles(ring, slot_of(g), GT)[:, :, 64:256], ye[:, :, :], o, ALU.add).then_inc(m1_ok, 1)

                def hots(blk, b):
                    wait(e, sum_ps, (blk - 1) * GT)
                    one_hots(e, k, hot[:, b % 2, :, :], blk).then_inc(hot_ok, 1)

                def add(blk, j, n):
                    e.wait_ge(sum_ps, blk * GT + j + 1)
                    e.wait_ge(acc_ok, blk * GT + j + 1)
                    e.tensor_tensor(place(acc, n, D), place(acc, n, D), ps_a[j][:, 0:D], ALU.add).then_inc(acc_ok, 1)

                def body(it, last=False):
                    for b in range(UN):
                        g = it * UN + b
                        fixed = isinstance(g, int)
                        if b % 2 == 0 and not (fixed and g < 2):
                            to = walk_values(nc, e, k, "walk_n", g - 2, 2)
                        largest(g)
                        if not (last and b + 2 >= UN):
                            turn(g + 2, (b + 2) % UN, it + 1 if b + 2 >= UN else it)
                        if not (fixed and g == 0):
                            hots(g - 1, b - 1)
                        weights(g, lambda: None if fixed and g == 0 else vector_part(g - 1))
                        for j in range(GT):
                            scalar_sum(g, b, j)
                        turned(g)
                        for j in range(GT):
                            scalar_part(g, j)
                            if not (fixed and g < 2):
                                add(g - 2, j, to[b % 2 * GT + j])
                turn(0, 0, 0)
                turn(1, 1, 0)
                body(0)
                with e.Fori(1, NI - 1) as it:
                    body(it)
                body(NI - 1, last=True)
                hots(NG - 1, NG - 1)
                vector_part(NG - 1)
                for blk in range(NG - 2, SB):
                    to = walk_values(nc, e, k, "walk_n", blk)
                    for j in range(GT):
                        add(blk, j, to[j])
                    if blk + 2 < SB:
                        hots(blk + 2, blk + 2)
                e.wait_ge(acc_ok, SB * GT + 1)

            @block.tensor
            def _(e):
                def aggregate(blk, b, j, slot):
                    if j == 0:
                        e.wait_ge(hot_ok, blk + 1)
                        if not isinstance(blk, int) or blk < NG:
                            e.wait_ge(m1_ok, blk + 1)
                            e.wait_ge(m0_ok, blk + 1)
                    wait(e, acc_ok, (blk - 1) * GT + j + 2)
                    e.matmul(ps_a[j][:, 0:D], hot[:, b % 2, j, :], place(ring, slot, D), start=True, stop=True).then_inc(sum_ps, 1)

                def scored(g, b, between):
                    e.wait_ge(xr_ok, g + 1)
                    wait(e, xt_sb, g)
                    for t in range(GT):
                        x = e.transpose(ps_x[:, t * P:(t + 1) * P], G[:, b, t, 0:128], k["ident"][:, :])
                    x.then_inc(xt_ps, 1)
                    if not isinstance(g, int) or g > 0:
                        products(g - 1, (b - 1) % UN)
                    e.wait_ge(xt_sb, g + 1)
                    wait(e, h_sb, g)
                    e.matmul(ps_h[:, :], k["WH"][:, :], XT[:, b % 2, :], start=True, stop=True).then_inc(h_ps, 1)
                    between(0)
                    between(1)
                    e.wait_ge(h_sb, g + 1)
                    wait(e, mx_ok, g)
                    wait(e, ex_ok, g)
                    for t in range(GT):
                        x = e.matmul(ps_s[:, t * 64:(t + 1) * 64], HT[:, b % 2, t * P:(t + 1) * P],
                                     k["LSC2"][:, :], start=True, stop=True)
                    x.then_inc(sc_ps, 1)

                def products(g, b):
                    wait(e, ud_ok, g)
                    wait(e, uv_ok, g)
                    for t in range(GT):
                        x = e.matmul(ps_p[:, t * P:(t + 1) * P], XT[:, b % 2, t * P:(t + 1) * P], k["WO"][:, :],
                                     start=True, stop=True)
                    x.then_inc(p_ps, 1)

                def body(it, last=False):
                    for b in range(UN):
                        g = it * UN + b
                        first = isinstance(g, int) and g < 2
                        if not first:
                            slots = walk_values(nc, e, k, "walk_slot", g - 2)

                        def between(h):
                            if not first:
                                for j in (2 * h, 2 * h + 1):
                                    aggregate(g - 2, b, j, slots[j])
                        if last and b == UN - 1:
                            products(g, b)
                            between(0)
                            between(1)
                        else:
                            scored(g + 1, (b + 1) % UN, between)
                scored(0, 0, lambda h: None)
                body(0)
                with e.Fori(1, NI - 1) as it:
                    body(it)
                body(NI - 1, last=True)
                for blk in range(NG - 2, SB):
                    slots = walk_values(nc, e, k, "walk_slot", blk)
                    for j in range(GT):
                        aggregate(blk, blk % UN, j, slots[j])

            @block.scalar
            def _(e):
                def inputs(g, b):
                    e.wait_ge(xt_ps, g + 1)
                    wait(e, p_ps, g - 1)
                    wait(e, h_ps, g - 1)
                    e.activation(XT[:, b % 2, :], ps_x[:, :], ACT.Copy).then_inc(xt_sb, 1)

                def hidden(g, b):
                    e.wait_ge(h_ps, g + 1)
                    wait(e, sc_ps, g - 1)
                    e.activation(HT[:, b % 2, :], ps_h[:, :], ACT.Relu).then_inc(h_sb, 1)

                def exps(g):
                    e.wait_ge(nm_ok, g + 1)
                    wait(e, m0_ok, g)
                    wait(e, z_ok, g)
                    wait(e, enr_ok, g)
                    for t in range(GT):
                        x = e.activation(ex[:, t, :], ps_s[:, t * 64:(t + 1) * 64], ACT.Exp, bias=nm[:, t:t + 1],
                                         accum_out=zs[:, t:t + 1])
                    x.then_inc(ex_ok, 1)
                    e.activation(en[:, :], nm[:, :], ACT.Exp).then_inc(en_ok, 1)

                def vectors(g, b):
                    e.wait_ge(enr_ok, g + 1)
                    wait(e, m1_ok, g)
                    for t in range(GT):
                        e.activation(ye[:, t, :], G[:, b, t, 256:448], ACT.Identity, scale=enr[:, t:t + 1])
                    e.wait_ge(rr_ok, g + 1)
                    e.wait_ge(ud_ok, g + 1)
                    for t in range(UA):
                        for c in range(3):
                            x = e.activation(o1[:, t, c, :], four(ps_p)[:, t, 64:128], ACT.Identity, scale=rr[:, t, c:c + 1])
                    x.then_inc(uv_ok, 1)

                def body(it, last=False):
                    for b in range(UN):
                        g = it * UN + b
                        if not last:
                            stage_sources(e, k, stage, g + UN, b, it + 1, landed, staged)
                        end = last and b == UN - 1
                        if not end:
                            inputs(g + 1, (b + 1) % UN)
                        exps(g)
                        if not end:
                            hidden(g + 1, (b + 1) % UN)
                        vectors(g, b)
                for g in range(UN):
                    stage_sources(e, k, stage, g, g, 0, landed, staged)
                inputs(0, 0)
                hidden(0, 0)
                body(0)
                with e.Fori(1, NI - 1) as it:
                    body(it)
                body(NI - 1, last=True)


def lns(nc, d, k):
    EPS = 1e-8
    with ExitStack() as ctx:
        m = Mem(nc, ctx, "lns")
        w = m.sb("w", [P, 2, D])
        wa = m.sb("wa", [P, 2, D])
        ws = m.sb("ws", [P, 2, D], BF16)
        bias = m.sb("bias", [P, D])
        xn = m.sb("xn", [P, 2, D])
        at = m.sb("at", [P, 2, D])
        ab = m.sb("ab", [P, 2, D])
        wabs = m.sb("wabs", [P, 2, D])
        st = m.sb("st", [P, 2, D], BF16)
        sg = m.sb("sg", [P, 2, D])
        o = m.sb("o", [P, 2, D])
        o2 = m.sb("o2", [P, 2, D])
        ps_t = [m.ps(f"ps_t{i}", [P, 512]) for i in range(2)]
        ps_m = [m.ps(f"ps_m{i}", [P, 512]) for i in range(2)]
        ps_g = [m.ps(f"ps_g{i}", [P, 512]) for i in range(2)]
        S = m.sem
        ab_ok, wabs_ok = S("ab_ok"), S("wabs_ok")
        loaded, wa_ok, ws_ok, xn_ok, t_ps, at_ok, st_ok, y_ps, g_ps, sg_ok, o_ok, o2_ok, x_ok = (S(n) for n in (
            "loaded", "wa_ok", "ws_ok", "xn_ok", "t_ps", "at_ok", "st_ok", "y_ps", "g_ps", "sg_ok", "o_ok", "o2_ok", "x_ok"))
        with nc.Block() as block:
            @block.sync
            def _(e):
                e.dma_start(w[:, :, :], d["lnsT"].rearrange("(c p) n -> p c n", p=P)).then_inc(loaded, 16)
                e.dma_start(bias[:, :], d["lns_b"].to_broadcast([P, D])).then_inc(loaded, 16)

            @block.gpsimd
            def _(e):
                e.wait_ge(loaded, 32)
                e.wait_ge(wabs_ok, 1)
                e.tensor_scalar_add(wa[:, :, :], wabs[:, :, :], EPS).then_inc(wa_ok, 1)

            @block.vector
            def _(e):
                e.wait_ge(loaded, 32)

                def norm(i, j):
                    wait(e, t_ps, i - 1)
                    e.tensor_scalar(xn[:, j, :], tile(k["X"], i), cols(k["mvf"], i * 2, 1), cols(k["rstd"], i, 1),
                                    ALU.subtract, ALU.mult).then_inc(xn_ok, 1)

                def guard(i, j):
                    e.wait_ge(ab_ok, i + 1)
                    wait(e, y_ps, i - 1)
                    e.tensor_scalar_add(at[:, j, :], ab[:, j, :], EPS).then_inc(at_ok, 1)

                def body(i, j, it):
                    if not (isinstance(i, int) and i >= NT - 2):
                        norm(i + 2, j)
                    if not is_last(i):
                        guard(i + 1, 1 - j)
                    e.wait_ge(sg_ok, i + 1)
                    e.wait_ge(y_ps, i + 1)
                    wait(e, o2_ok, i - 1)
                    e.tensor_tensor(o[:, j, :], sg[:, j, :], ps_m[j][:, 0:D], ALU.mult).then_inc(o_ok, 1)
                    e.wait_ge(o_ok, i + 1)
                    wait(e, x_ok, i - 1)
                    e.tensor_tensor(o2[:, j, :], o[:, j, :], bias[:, :], ALU.add).then_inc(o2_ok, 1)
                    e.wait_ge(o2_ok, i + 1)
                    e.tensor_tensor(tile(k["X"], i), tile(k["X"], i), o2[:, j, :], ALU.add).then_inc(x_ok, 1)
                norm(0, 0)
                norm(1, 1)
                guard(0, 0)
                turns(body)(e)

            @block.tensor
            def _(e):
                e.wait_ge(wa_ok, 1)
                e.wait_ge(ws_ok, 1)

                def inputs(i, j):
                    e.wait_ge(xn_ok, i + 1)
                    wait(e, ab_ok, i - 1)
                    wait(e, st_ok, i - 1)
                    for c in range(2):
                        x = e.transpose(ps_t[j][:, c * P:(c + 1) * P], xn[:, j, c * P:(c + 1) * P], k["ident"][:, :])
                    x.then_inc(t_ps, 1)

                def body(i, j, it):
                    if not is_last(i):
                        inputs(i + 1, 1 - j)
                    e.wait_ge(st_ok, i + 1)
                    wait(e, sg_ok, i - 1)
                    for c in range(2):
                        x = e.matmul(ps_g[j][:, 0:D], st[:, j, c * P:(c + 1) * P], ws[:, c, :], start=c == 0, stop=c == 1)
                    x.then_inc(g_ps, 1)
                    e.wait_ge(at_ok, i + 1)
                    wait(e, o_ok, i - 1)
                    for c in range(2):
                        x = e.matmul(ps_m[j][:, 0:D], at[:, j, c * P:(c + 1) * P], wa[:, c, :], start=c == 0, stop=c == 1)
                    x.then_inc(y_ps, 1)
                inputs(0, 0)
                turns(body)(e)

            @block.scalar
            def _(e):
                e.wait_ge(loaded, 32)
                e.activation(wabs[:, :, :], w[:, :, :], ACT.Abs).then_inc(wabs_ok, 1)
                e.activation(ws[:, :, :], w[:, :, :], ACT.Sign).then_inc(ws_ok, 1)

                def inputs(i, j):
                    e.wait_ge(t_ps, i + 1)
                    wait(e, g_ps, i - 1)
                    e.activation(st[:, j, :], ps_t[j][:, 0:D], ACT.Sign).then_inc(st_ok, 1)
                    wait(e, at_ok, i - 1)
                    e.activation(ab[:, j, :], ps_t[j][:, 0:D], ACT.Abs).then_inc(ab_ok, 1)

                def body(i, j, it):
                    if not is_last(i):
                        inputs(i + 1, 1 - j)
                    e.wait_ge(g_ps, i + 1)
                    wait(e, o_ok, i - 1)
                    e.activation(sg[:, j, :], ps_g[j][:, 0:D], ACT.Sign).then_inc(sg_ok, 1)
                inputs(0, 0)
                turns(body)(e)


def qkv(nc, d, k):
    with ExitStack() as ctx:
        m = Mem(nc, ctx, "qkv")
        w = m.sb("w", [P, 2, 768])
        bias = m.sb("bias", [P, 768])
        xn = m.sb("xn", [P, 2, D])
        xt = m.sb("xt", [P, 2, D])
        row = m.sb("row", [P, 4, 2 * D])
        ps_t = [m.ps(f"ps_t{i}", [P, 512]) for i in range(2)]
        ps_y = [m.ps(f"ps_y{i}", [P, 1024]) for i in range(2)]
        S = m.sem
        loaded, xn_ok, t_ps, xt_ok, y_ps, row_ok, zero_ok = (S(n) for n in (
            "loaded", "xn_ok", "t_ps", "xt_ok", "y_ps", "row_ok", "zero_ok"))
        stored = [S(f"stored{i}") for i in range(4)]
        with nc.Block() as block:
            @block.sync
            def _(e):
                e.dma_start(w[:, :, :], d["wqkv"].rearrange("(c p) n -> p c n", p=P)).then_inc(loaded, 16)
                e.dma_start(bias[:, :], d["bqkv"].to_broadcast([P, 768])).then_inc(loaded, 16)

                def body(i, j, it):
                    e.wait_ge(row_ok, i + 1)
                    for n, name in enumerate(("qtab", "vtab")):
                        t = d[name].rearrange("(n p) c -> n p c", p=P)
                        dst = t[i, :, :] if isinstance(i, int) else t[bass.ds(i, 1), :, :].rearrange("a p c -> (a p) c")
                        e.dma_start(dst, row[:, j, n * D:(n + 1) * D]).then_inc(stored[j], 16)
                turns(body, bufs=4)(e)
                for j in range(4):
                    e.wait_ge(stored[j], 32 * len(range(j, NT, 4)))

            @block.gpsimd
            def _(e):
                e.memset(k["zeros"][:, :], 0.0).then_inc(zero_ok, 1)
                e.wait_ge(zero_ok, 1)
                e.dma_start(d["xg"].rearrange("(n p) c -> p n c", p=P),
                            k["zeros"][:, :].unsqueeze(1).to_broadcast([P, NX, D])).then_inc(k["zeroed"], 16)

            @block.vector
            def _(e):
                def norm(i, j):
                    wait(e, t_ps, i - 1)
                    e.tensor_scalar(xn[:, j, :], tile(k["X"], i), cols(k["mvf"], i * 2, 1), cols(k["rstd"], i, 1),
                                    ALU.subtract, ALU.mult).then_inc(xn_ok, 1)

                def body(i, j, it):
                    if not (isinstance(i, int) and i >= NT - 2):
                        norm(i + 2, j % 2)
                    e.wait_ge(y_ps, i + 1)
                    wait(e, stored[j], it * 32)
                    e.tensor_tensor(row[:, j, 0:D], ps_y[j % 2][:, 0:D], bias[:, 0:D], ALU.add)
                    e.tensor_tensor(tile(k["K"], i)[:, 0:D], ps_y[j % 2][:, D:2 * D], bias[:, D:2 * D], ALU.add)
                    e.tensor_tensor(row[:, j, D:2 * D], ps_y[j % 2][:, 512:768], bias[:, 512:768], ALU.add).then_inc(row_ok, 1)
                e.wait_ge(loaded, 32)
                norm(0, 0)
                norm(1, 1)
                turns(body, bufs=4)(e)

            @block.tensor
            def _(e):
                e.wait_ge(loaded, 32)

                def inputs(i, j):
                    e.wait_ge(xn_ok, i + 1)
                    wait(e, xt_ok, i - 1)
                    for c in range(2):
                        x = e.transpose(ps_t[j][:, c * P:(c + 1) * P], xn[:, j, c * P:(c + 1) * P], k["ident"][:, :])
                    x.then_inc(t_ps, 1)

                def body(i, j, it):
                    if not is_last(i):
                        inputs(i + 1, (j + 1) % 2)
                    e.wait_ge(xt_ok, i + 1)
                    wait(e, row_ok, i - 1)
                    for c in range(2):
                        e.matmul(ps_y[j % 2][:, 0:512], xt[:, j % 2, c * P:(c + 1) * P], w[:, c, 0:512], start=c == 0, stop=c == 1)
                    for c in range(2):
                        x = e.matmul(ps_y[j % 2][:, 512:768], xt[:, j % 2, c * P:(c + 1) * P], w[:, c, 512:768], start=c == 0, stop=c == 1)
                    x.then_inc(y_ps, 1)
                inputs(0, 0)
                turns(body, bufs=4)(e)

            @block.scalar
            def _(e):
                def body(i, j, it):
                    e.wait_ge(t_ps, i + 1)
                    wait(e, y_ps, i - 1)
                    e.activation(xt[:, j, :], ps_t[j][:, 0:D], ACT.Copy).then_inc(xt_ok, 1)
                turns(body)(e)


def scores(nc, d, k):
    with ExitStack() as ctx:
        m = Mem(nc, ctx, "scores")
        Q = m.sb("Q", [P, QUN * GT, D])
        sq = m.sb("sq", [P, QUN, GT], I32)
        scr = m.sb("scr", [P, 2])
        hot = m.sb("hot", [P, 2, GT, P])
        hotT = m.sb("hotT", [P, 2, GT * P])
        prod = m.sb("prod", [P, 2, GT, D])
        part = m.sb("part", [P, 2, GT * HEADS])
        ps_t = [m.ps(f"ps_t{i}", [P, 512]) for i in range(2)]
        ps_k = [m.ps(f"ps_k{i}", [P, 512]) for i in range(GT)]
        landed = [m.sem(f"landed{i}") for i in range(QUN)]
        staged, carried, hot_ok, t_ps, t_sb, k_ps, prod_ok, part_ok, s_ok = (m.sem(n) for n in (
            "staged", "carried", "hot_ok", "t_ps", "t_sb", "k_ps", "prod_ok", "part_ok", "s_ok"))
        assert QUN * GT - (NT - 1) >= (UN - 1) * GT

        def blocks(e, body):
            def some(it):
                for b in range(QUN):
                    body(it * QUN + b, b, it)
            rolled(e, NG // QUN, some)
            for blk in range(NG, SB):
                body(blk, blk % QUN, blk // QUN)

        with nc.Block() as block:
            @block.gpsimd
            def _(e):
                gathers(e, scr, carried, staged, landed, d["qtab"], lambda b, j: Q[:, b * GT + j, :], sq,
                        lambda g: [(prod_ok, (g - UN + 1) * GT)] if not isinstance(g, int) or g >= QUN else [], un=QUN)

            @block.vector
            def _(e):
                e.memset(k["S"][:, :], 0.0).then_inc(s_ok, 1)

                def hots(blk, i):
                    wait(e, t_ps, blk - 1)
                    one_hots(e, k, hot[:, i, :, :], blk).then_inc(hot_ok, 1)

                def add(blk, i, j, t):
                    e.wait_ge(part_ok, blk + 1)
                    e.wait_ge(s_ok, blk * GT + j + 1)
                    s = cols(k["S"], t, HEADS)
                    e.tensor_tensor(s, s, part[:, i, j * HEADS:(j + 1) * HEADS], ALU.add).then_inc(s_ok, 1)

                def body(blk, b, it):
                    first = isinstance(blk, int) and blk == 0
                    slots, before = walk_values(nc, e, k, "walk_q", blk)
                    if not isinstance(blk, int) or blk < NG:
                        e.wait_ge(landed[b], (it + 1) * 16 * GT)
                    for j in range(GT):
                        e.wait_ge(k_ps, blk * GT + j + 1)
                        wait(e, part_ok, blk - 1)
                        e.tensor_tensor(prod[:, b % 2, j, :], place(Q, slots[j], D), ps_k[j][:, 0:D], ALU.mult).then_inc(prod_ok, 1)
                        if not first:
                            add(blk - 1, (b - 1) % 2, j, before[j])
                    if not isinstance(blk, int) or blk + 2 < SB:
                        hots(blk + 2, b % 2)
                    e.wait_ge(prod_ok, (blk + 1) * GT)
                    wait(e, s_ok, (blk - 1) * GT + 1)
                    e.tensor_reduce(part[:, b % 2, :], prod[:, b % 2, :, :].rearrange("p t (h c) -> p (t h) c", c=HD),
                                    AX.X, ALU.add).then_inc(part_ok, 1)
                hots(0, 0)
                hots(1, 1)
                blocks(e, body)
                _, before = walk_values(nc, e, k, "walk_q", SB)
                for j in range(GT):
                    add(SB - 1, (SB - 1) % 2, j, before[j])
                e.wait_ge(s_ok, SB * GT + 1)

            @block.tensor
            def _(e):
                def transposes(blk, i):
                    e.wait_ge(hot_ok, blk + 1)
                    wait(e, t_sb, blk - 1)
                    for j in range(GT):
                        x = e.transpose(ps_t[i][:, j * P:(j + 1) * P], hot[:, i, j, :], k["ident"][:, :])
                    x.then_inc(t_ps, 1)

                def body(blk, b, it):
                    to = walk_values(nc, e, k, "walk_n", blk)
                    if not isinstance(blk, int) or blk + 1 < SB:
                        transposes(blk + 1, (b + 1) % 2)
                    for j in range(GT):
                        e.wait_ge(t_sb, blk + 1)
                        wait(e, prod_ok, (blk - 1) * GT + j + 1)
                        e.matmul(ps_k[j][:, 0:D], hotT[:, b % 2, j * P:(j + 1) * P], place(k["K"], to[j], D),
                                 start=True, stop=True).then_inc(k_ps, 1)
                transposes(0, 0)
                blocks(e, body)

            @block.scalar
            def _(e):
                def ahead(blk, b, it):
                    if not isinstance(blk, int) or blk + QA < NG:
                        stage_sources(e, k, sq, blk + QA, (b + QA) % QUN, it + (b + QA) // QUN, landed, staged)

                def body(blk, b, it):
                    ahead(blk, b, it)
                    e.wait_ge(t_ps, blk + 1)
                    wait(e, k_ps, (blk - 1) * GT)
                    e.activation(hotT[:, b % 2, :], ps_t[b % 2][:, :], ACT.Copy).then_inc(t_sb, 1)
                QA = UN
                for g in range(QA):
                    stage_sources(e, k, sq, g, g, 0, landed, staged)
                blocks(e, body)


CH = 16
CT = ET // CH
CE = CT * P


def softmax_shift(nc, d, k):
    B = 1.0e38
    with ExitStack() as ctx:
        m = Mem(nc, ctx, "shift")
        ST = m.sb("ST", [P, CE])
        DT = m.sb("DT", [P, CE + 2])
        pen = m.sb("pen", [P, CE + 1])
        eq = m.sb("eq", [P, CE + 1])
        F = m.sb("F", [P, CE])
        R = m.sb("R", [P, CE])
        down, up = m.sb("down", [P, P]), m.sb("up", [P, P])
        pi = m.sb("pi", [P, 4], I32)
        pf = m.sb("pf", [P, 2])
        hsel, csel = m.sb("hsel", [P, HEADS]), m.sb("csel", [P, CH])
        hselT = m.sb("hselT", [HEADS, P])
        ends = m.sb("ends", [P, 4])
        spread = m.sb("spread", [P, 4, CH])
        small = m.sb("small", [HEADS, 4, CH])
        carry = m.sb("carry", [HEADS, 2, CH + 1])
        pick = m.sb("pick", [P, 2, CH])
        init = m.sb("init", [P, 2])
        ps = [m.ps(f"ps{i}", [P, 512]) for i in range(2)]
        ps_e = m.ps("ps_e", [P, 512])
        tr, ev, sel, chain, side, pe = (m.sem(n) for n in ("tr", "ev", "sel", "chain", "side", "pe"))
        ex_ok, back, back_ev, made = (m.sem(n) for n in ("ex_ok", "back", "back_ev", "made"))
        S4 = k["S"][:, :].rearrange("p (c j h) -> p j c h", c=CH, h=HEADS)
        D4 = k["dst_f"][:, :].rearrange("p (c j) -> p j c", c=CH)
        D2, S2 = m.sb("D2", [P, CT, P]), m.sb("S2", [P, CT, P])
        by4 = lambda t: t[:, :, :].rearrange("p j (c h) -> p j c h", h=HEADS)
        ordered = m.sem("ordered")
        rounds = [(a, j0, min(4, CT - j0)) for a in range(2) for j0 in range(0, CT, 4)]
        half = len(rounds) // 2
        with nc.Block() as block:
            @block.tensor
            def _(e):
                e.wait_ge(ordered, 2)
                for n, (a, j0, w) in enumerate(rounds):
                    wait(e, ev, n - 1)
                    for j in range(w):
                        x = e.transpose(ps[n % 2][:, j * P:(j + 1) * P], (D2, S2)[a][:, j0 + j, :], k["ident"][:, :])
                    x.then_inc(tr, 1)
                e.wait_ge(ev, half)
                e.wait_ge(made, 4)
                e.matmul(ps_e[:, 0:1], down[:, :], DT[:, CE:CE + 1], start=True, stop=True)
                e.matmul(ps_e[:, 1:2], up[:, :], DT[:, 1:2], start=True, stop=True).then_inc(pe, 1)
                e.wait_ge(sel, 2)
                e.wait_ge(side, 1)
                e.transpose(ps_e[0:HEADS, 0:P], hsel[:, :], k["ident"][:, :]).then_inc(pe, 1)
                e.wait_ge(side, 2)
                e.wait_ge(chain, 1)
                e.matmul(ps_e[0:HEADS, 128:192], hsel[:, :], spread[:, :, :].rearrange("p a c -> p (a c)"),
                         start=True, stop=True).then_inc(pe, 1)
                e.wait_ge(side, 3)
                e.matmul(ps_e[:, 256:288], hselT[:, :], small[:, 0:2, :].rearrange("p a c -> p (a c)"), start=True, stop=True).then_inc(pe, 1)
                e.wait_ge(ex_ok, 1)
                for n, (a, j0, w) in enumerate(rounds[half:]):
                    wait(e, back_ev, n - 1)
                    for j in range(w):
                        x = e.transpose(ps[n % 2][:, j * P:(j + 1) * P], F[:, (j0 + j) * P:(j0 + j + 1) * P], k["ident"][:, :])
                    x.then_inc(back, 1)

            @block.gpsimd
            def _(e):
                e.memset(down[:, :], 0.0).then_inc(made, 1)
                e.memset(up[:, :], 0.0).then_inc(made, 1)
                e.wait_ge(made, 2)
                e.tensor_copy(down[:, HEADS:P], k["ident"][:, 0:P - HEADS]).then_inc(made, 1)
                e.tensor_copy(up[:, 0:P - HEADS], k["ident"][:, HEADS:P]).then_inc(made, 1)
                e.iota(pi[:, 0:1], pattern=[[1, 1]], base=0, channel_multiplier=1).then_inc(made, 1)

            @block.scalar
            def _(e):
                e.activation(by4(D2), D4.unsqueeze(3).to_broadcast([P, CT, CH, HEADS]), ACT.Copy).then_inc(ordered, 1)
                for n, (a, j0, w) in enumerate(rounds):
                    to = DT[:, 1 + j0 * P:1 + (j0 + w) * P] if a == 0 else ST[:, j0 * P:(j0 + w) * P]
                    e.wait_ge(tr, n + 1)
                    e.activation(to, ps[n % 2][:, 0:w * P], ACT.Copy).then_inc(ev, 1)
                e.wait_ge(chain, 2)
                e.activation(F[:, :], R[:, :], ACT.Exp, scale=1.0 / HD ** 0.5).then_inc(ex_ok, 1)
                for n, (a, j0, w) in enumerate(rounds[half:]):
                    e.wait_ge(back, n + 1)
                    e.activation(S4[:, j0:j0 + w, :, :],
                                 ps[n % 2][:, 0:w * P].rearrange("p (j c h) -> p j c h", j=w, h=HEADS), ACT.Copy).then_inc(back_ev, 1)

            @block.vector
            def _(e):
                n = [0]
                own = m.sem("own")

                def link(ins):
                    ins.then_inc(own, 1)
                    n[0] += 1
                    e.wait_ge(own, n[0])
                e.tensor_copy(by4(S2), S4).then_inc(ordered, 1)
                e.wait_ge(made, 5)
                link(e.tensor_single_scalar(pi[:, 1:2], pi[:, 0:1], HEADS - 1, ALU.bitwise_and))
                link(e.tensor_single_scalar(pi[:, 2:3], pi[:, 0:1], 3, ALU.arith_shift_right))
                link(e.tensor_copy(pf[:, :], pi[:, 1:3]))
                e.tensor_scalar(hsel[:, :], k["iota"][:, 0:HEADS], pf[:, 0:1], None, ALU.is_equal).then_inc(sel, 1)
                e.tensor_scalar(csel[:, :], k["iota"][:, 0:CH], pf[:, 1:2], None, ALU.is_equal).then_inc(sel, 1)
                e.wait_ge(sel, 2)
                e.wait_ge(pe, 1)
                link(e.tensor_tensor(DT[:, 0:1], ps_e[:, 0:1], csel[:, 0:1], ALU.subtract))
                link(e.tensor_tensor(DT[:, CE + 1:CE + 2], ps_e[:, 1:2], csel[:, CH - 1:CH], ALU.subtract))
                e.engine_nop().then_inc(side, 1)
                link(e.tensor_tensor(eq[:, :], DT[:, 0:CE + 1], DT[:, 1:CE + 2], ALU.is_equal))
                link(e.tensor_scalar(pen[:, :], eq[:, :], -1.0, B, ALU.add, ALU.mult))
                e.wait_ge(ev, len(rounds))
                e.tensor_reduce(ends[:, 1:2], pen[:, 0:CE], AX.X, ALU.min)
                e.tensor_reduce(ends[:, 3:4], pen[:, 1:CE + 1], AX.X, ALU.min)
                e.tensor_tensor_scan(F[:, :], pen[:, 0:CE], ST[:, :], -B, ALU.add, ALU.max)
                link(e.tensor_tensor_scan(R[:, ::-1], pen[:, CE:0:-1], ST[:, ::-1], -B, ALU.add, ALU.max))
                e.tensor_copy(ends[:, 0:1], F[:, CE - 1:CE])
                link(e.tensor_copy(ends[:, 2:3], R[:, 0:1]))
                e.tensor_tensor(spread[:, :, :], ends[:, :].unsqueeze(2).to_broadcast([P, 4, CH]),
                                csel[:, :].unsqueeze(1).to_broadcast([P, 4, CH]), ALU.mult).then_inc(chain, 1)
                e.wait_ge(pe, 2)
                e.tensor_copy(hselT[:, :], ps_e[0:HEADS, 0:P]).then_inc(side, 1)
                e.memset(carry[:, :, :], -B)
                e.wait_ge(pe, 3)
                link(e.tensor_copy(small[:, :, :], ps_e[0:HEADS, 128:192].rearrange("p (a c) -> p a c", a=4)))
                link(e.tensor_tensor_scan(carry[:, 0, 1:CH + 1], small[:, 1, :], small[:, 0, :], -B, ALU.add, ALU.max))
                link(e.tensor_tensor_scan(carry[:, 1, CH - 1::-1], small[:, 3, ::-1], small[:, 2, ::-1], -B, ALU.add, ALU.max))
                e.tensor_copy(small[:, 0, :], carry[:, 0, 0:CH])
                e.tensor_copy(small[:, 1, :], carry[:, 1, 1:CH + 1]).then_inc(side, 1)
                e.wait_ge(pe, 4)
                link(e.tensor_tensor(pick[:, :, :], ps_e[:, 256:288].rearrange("p (a c) -> p a c", a=2),
                                     csel[:, :].unsqueeze(1).to_broadcast([P, 2, CH]), ALU.mult))
                link(e.tensor_reduce(init[:, :], pick[:, :, :], AX.X, ALU.add))
                link(e.tensor_tensor_scan(F[:, :], pen[:, 0:CE], ST[:, :], init[:, 0:1], ALU.add, ALU.max))
                link(e.tensor_tensor_scan(R[:, ::-1], pen[:, CE:0:-1], ST[:, ::-1], init[:, 1:2], ALU.add, ALU.max))
                link(e.tensor_tensor(eq[:, 0:CE], F[:, :], R[:, :], ALU.max))
                e.tensor_tensor(R[:, :], ST[:, :], eq[:, 0:CE], ALU.subtract).then_inc(chain, 1)


def aggregate1(nc, d, k):
    with ExitStack() as ctx:
        m = Mem(nc, ctx, "agg1")
        V = m.sb("V", [P, UN, GT, D])
        stage = m.sb("stage", [P, UN, GT], I32)
        scr = m.sb("scr", [P, 2])
        ring = m.sb("ring", [P, RING, A])
        hot = m.sb("hot", [P, 2, GT, P])
        ps_a = [m.ps(f"ps_a{i}", [P, 512]) for i in range(4)]
        landed = [m.sem(f"landed{i}") for i in range(UN)]
        staged, carried, msg_ok, p_ok, hot_ok, sum_ps, acc_ok = (
            m.sem(n) for n in ("staged", "carried", "msg_ok", "p_ok", "hot_ok", "sum_ps", "acc_ok"))
        acc = k["acc1"]
        with nc.Block() as block:
            @block.gpsimd
            def _(e):
                gathers(e, scr, carried, staged, landed, d["vtab"], lambda b, j: V[:, b, j, :], stage,
                        lambda g: [(msg_ok, g - UN + 1)])

            @block.vector
            def _(e):
                e.memset(acc[:, :, :], 0.0).then_inc(acc_ok, 1)

                def hots(blk, b):
                    wait(e, sum_ps, blk * GT - GT)
                    one_hots(e, k, hot[:, b % 2, :, :], blk).then_inc(hot_ok, 1)

                def add(blk, j, n):
                    e.wait_ge(sum_ps, blk * GT + j + 1)
                    e.wait_ge(acc_ok, blk * GT + j + 1)
                    e.tensor_tensor(place(acc, n, A), place(acc, n, A), ps_a[j][:, 0:A], ALU.add).then_inc(acc_ok, 1)

                def body(it):
                    for b in range(UN):
                        g = it * UN + b
                        first = isinstance(g, int) and g == 0
                        if not first:
                            to = walk_values(nc, e, k, "walk_n", g - 1)
                        hots(g, b)
                        e.wait_ge(landed[b], (it + 1) * 16 * GT)
                        slot = (g % (RING // GT)) * GT
                        p = cols(k["S"], g * GT * HEADS, GT * HEADS).rearrange("p (t h) -> p t h", h=HEADS)
                        e.tensor_copy(tiles(ring, slot, GT)[:, :, D:A], p).then_inc(p_ok, 1)
                        e.tensor_tensor(tiles(ring, slot, GT)[:, :, 0:D].rearrange("p t (h c) -> p t h c", c=HD),
                                        V[:, b, :, :].rearrange("p t (h c) -> p t h c", c=HD),
                                        p.unsqueeze(3).to_broadcast([P, GT, HEADS, HD]), ALU.mult).then_inc(msg_ok, 1)
                        if not first:
                            for j in range(GT):
                                add(g - 1, j, to[j])
                rolled(e, NI, body)
                for blk in range(NG, SB + 1):
                    to = walk_values(nc, e, k, "walk_n", blk - 1)
                    if blk < SB:
                        hots(blk, blk)
                    for j in range(GT):
                        add(blk - 1, j, to[j])
                e.wait_ge(acc_ok, SB * GT + 1)

            @block.scalar
            def _(e):
                def body(it):
                    for b in range(UN):
                        stage_sources(e, k, stage, it * UN + b, b, it, landed, staged)
                rolled(e, NI, body)

            @block.tensor
            def _(e):
                def block_of(blk, b):
                    slots = walk_values(nc, e, k, "walk_slot", blk)
                    for j in range(GT):
                        e.wait_ge(hot_ok, blk + 1)
                        if j == 0 and not (isinstance(blk, int) and blk >= NG):
                            e.wait_ge(msg_ok, blk + 1)
                            e.wait_ge(p_ok, blk + 1)
                        wait(e, acc_ok, blk * GT + j - GT + 2)
                        e.matmul(ps_a[j][:, 0:A], hot[:, b % 2, j, :], place(ring, slots[j], A), start=True, stop=True).then_inc(sum_ps, 1)

                def body(it):
                    for b in range(UN):
                        block_of(it * UN + b, b)
                rolled(e, NI, body)
                for blk in range(NG, SB):
                    block_of(blk, blk)


def add_acc1(nc, k):
    with ExitStack() as ctx:
        m = Mem(nc, ctx, "add1")
        z, rz = m.sb("z", [P, NT, HEADS]), m.sb("rz", [P, NT, HEADS])
        s = m.sem("s")
        acc = k["acc1"]
        with nc.Block() as block:
            @block.vector
            def _(e):
                e.tensor_scalar_max(z[:, :, :], acc[:, :, D:D + HEADS], 1e-16).then_inc(s, 1)
                e.wait_ge(s, 1)
                e.reciprocal(rz[:, :, :], z[:, :, :]).then_inc(s, 1)
                e.wait_ge(s, 2)
                v = acc[:, :, 0:D].rearrange("p n (h c) -> p n h c", c=HD)
                e.tensor_tensor(v, v, rz[:, :, :].unsqueeze(3).to_broadcast([P, NT, HEADS, HD]), ALU.mult).then_inc(s, 1)
                e.wait_ge(s, 3)
                e.tensor_tensor(k["X"][:, :, :], k["X"][:, :, :], acc[:, :, 0:D], ALU.add).then_inc(s, 1)


def route(nc, d, k):
    with ExitStack() as ctx:
        m = Mem(nc, ctx, "route")
        gb = k["gb"]
        wr = m.sb("wr", [P, 2, NE])
        br = m.sb("br", [P, NE])
        xn = m.sb("xn", [P, 2, D])
        xt = m.sb("xt", [P, 2, D])
        lg = m.sb("lg", [P, NT, NE])
        top = m.sb("top", [P, NT, 8])
        idx = m.sb("idx", [P, NT, 8], U32)
        idf = m.sb("idf", [P, NT, 2])
        df, ed, ep = (m.sb(n, [P, NT]) for n in ("df", "ed", "ep"))
        w0, w1 = k["w"][:, 0:NT], k["w"][:, NT:2 * NT]
        one = k["one"]
        ps_t = [m.ps(f"ps_t{i}", [P, 512]) for i in range(2)]
        ps_l = [m.ps(f"ps_l{i}", [P, 512]) for i in range(2)]
        S = m.sem
        loaded, xn_ok, t_ps, xt_ok, xc_ok, l_ps, lg_ok, top_ok, idx_ok, own, df_ok, ed_ok = (S(n) for n in (
            "loaded", "xn_ok", "t_ps", "xt_ok", "xc_ok", "l_ps", "lg_ok", "top_ok", "idx_ok", "own", "df_ok", "ed_ok"))
        with nc.Block() as block:
            @block.sync
            def _(e):
                e.dma_start(gb[:, 0, :], d["gamma"]).then_inc(loaded, 16)
                e.dma_start(gb[:, 1, :], d["beta"]).then_inc(loaded, 16)
                e.dma_start(wr[:, :, :], d["Wr"].rearrange("(c p) n -> p c n", p=P)).then_inc(loaded, 16)
                e.dma_start(br[:, :], d["br"].to_broadcast([P, NE])).then_inc(loaded, 16)
                e.dma_start(k["b1b2"][:, :], d["b1b2"].to_broadcast([P, NE * (HID + D)])).then_inc(k["w_in"], 16)
                e.dma_start(k["W1"][:, :, :, :], d["W1"].rearrange("x (c p) h -> p x c h", p=P)).then_inc(k["w_in"], 16)
                e.dma_start(k["W2"][:, :, :, :], d["W2"].rearrange("x (c p) h -> p x c h", p=P)).then_inc(k["w_in"], 16)

            @block.vector
            def _(e):
                def norm(i, j):
                    wait(e, t_ps, i - 1)
                    wait(e, xc_ok, i - 1)
                    e.tensor_scalar(xn[:, j, :], tile(k["X"], i), cols(k["mvf"], i * 2, 1), cols(k["rstd"], i, 1),
                                    ALU.subtract, ALU.mult).then_inc(xn_ok, 1)

                def body(i, j, it):
                    if not (isinstance(i, int) and i >= NT - 2):
                        norm(i + 2, j)
                    e.wait_ge(t_ps, i + 1)
                    wait(e, l_ps, i - 1)
                    for c in range(2):
                        e.tensor_scalar(xt[:, j, c * P:(c + 1) * P], ps_t[j][:, c * P:(c + 1) * P], gb[:, 0, c:c + 1],
                                        gb[:, 1, c:c + 1], ALU.mult, ALU.add).then_inc(xt_ok, 1)
                    e.wait_ge(l_ps, i + 1)
                    e.tensor_tensor(tile(lg, i), ps_l[j][:, 0:NE], br[:, :], ALU.add).then_inc(lg_ok, 1)
                e.wait_ge(loaded, 64)
                norm(0, 0)
                norm(1, 1)
                turns(body)(e)
                n = [0]

                def link(ins):
                    ins.then_inc(own, 1)
                    n[0] += 1
                    e.wait_ge(own, n[0])
                e.wait_ge(lg_ok, NT)
                for i in range(NT):
                    e.max(top[:, i, :], lg[:, i, :]).then_inc(top_ok, 1)
                for i in range(NT):
                    e.wait_ge(top_ok, i + 1)
                    e.max_index(idx[:, i, :], top[:, i, :], lg[:, i, :]).then_inc(idx_ok, 1)
                e.wait_ge(idx_ok, NT)
                link(e.tensor_copy(idf[:, :, :], idx[:, :, 0:2]))
                e.tensor_tensor(df[:, :], top[:, :, 1], top[:, :, 0], ALU.subtract).then_inc(df_ok, 1)
                e.wait_ge(ed_ok, 1)
                link(e.tensor_scalar_add(ep[:, :], ed[:, :], 1.0))
                link(e.reciprocal(w0, ep[:, :]))
                link(e.tensor_tensor(w1, ed[:, :], w0, ALU.mult))
                for r in range(2):
                    link(e.tensor_tensor(one[:, r, :, :], k["iota"][:, 0:NE].unsqueeze(1).to_broadcast([P, NT, NE]),
                                         idf[:, :, r].unsqueeze(2).to_broadcast([P, NT, NE]), ALU.is_equal))

            @block.tensor
            def _(e):
                e.wait_ge(loaded, 64)

                def inputs(i, j):
                    e.wait_ge(xn_ok, i + 1)
                    wait(e, xt_ok, 2 * i - 2)
                    for c in range(2):
                        x = e.transpose(ps_t[j][:, c * P:(c + 1) * P], xn[:, j, c * P:(c + 1) * P], k["ident"][:, :])
                    x.then_inc(t_ps, 1)

                def body(i, j, it):
                    if not is_last(i):
                        inputs(i + 1, 1 - j)
                    e.wait_ge(xt_ok, 2 * i + 2)
                    wait(e, lg_ok, i - 1)
                    for c in range(2):
                        x = e.matmul(ps_l[j][:, 0:NE], xt[:, j, c * P:(c + 1) * P], wr[:, c, :], start=c == 0, stop=c == 1)
                    x.then_inc(l_ps, 1)
                inputs(0, 0)
                turns(body)(e)

            @block.scalar
            def _(e):
                def body(i, j, it):
                    e.wait_ge(xn_ok, i + 1)
                    e.activation(tile(k["XN"], i), xn[:, j, :], ACT.Copy).then_inc(xc_ok, 1)
                turns(body)(e)
                e.wait_ge(df_ok, 1)
                e.activation(ed[:, :], df[:, :], ACT.Exp).then_inc(ed_ok, 1)


HC = HID // P
NX = 2 * NT + NE - 1
NXT = 64


def dispatch(nc, d, k):
    R = 2 * NT
    with ExitStack() as ctx:
        m = Mem(nc, ctx, "disp")
        tri = m.sb("tri", [P, P])
        ones = m.sb("ones", [P, P])
        tot = m.sb("tot", [P, NE, R])
        inc = m.sb("inc", [P, NE, R])
        keep = m.sb("keep", [P, NE, R])
        off = m.sb("off", [P, R, NE])
        cnt, tf, end, base = (m.sb(n, [P, NE]) for n in ("cnt", "tf", "end", "base"))
        ci, ti = m.sb("ci", [P, NE], I32), m.sb("ti", [P, NE], I32)
        slot_f = m.sb("slot_f", [P, R])
        end2 = m.sb("end2", [1, NE])
        full = m.sb("full", [1, NXT, NE])
        tx, tx7 = m.sb("tx", [1, NXT]), m.sb("tx7", [1, NXT])
        ps = [m.ps(f"ps{i}", [P, 512]) for i in range(2)]
        made, own, counted, slots_ok, sent = (m.sem(n) for n in ("made", "own", "counted", "slots_ok", "sent"))
        one = k["one"][:, :, :, :].rearrange("p r n x -> p (r n) x")
        with nc.Block() as block:
            @block.gpsimd
            def _(e):
                e.memset(tri[:, :], 1.0).then_inc(made, 1)
                e.memset(ones[:, :], 1.0).then_inc(made, 1)
                e.wait_ge(made, 2)
                e.affine_select(out=tri[:, :], in_=tri[:, :], compare_op=ALU.is_gt, fill=0.0, base=0,
                                pattern=[[1, P]], channel_multiplier=-1).then_inc(made, 1)
                e.wait_ge(slots_ok, 1)
                e.wait_ge(k["zeroed"], 16)
                for c in range(R):
                    e.indirect_dma_start(out=d["xg"], in_=k["XN"][:, c % NT, :], in_offset=None,
                                         out_offset=bass.IndirectOffsetOnAxis(ap=k["slot"][:, c:c + 1], axis=0)).then_inc(sent, 16)
                e.wait_ge(sent, 16 * R)

            @block.tensor
            def _(e):
                e.wait_ge(made, 3)
                e.matmul(ps[0][:, 0:R * NE], tri[:, :], one.rearrange("p c x -> p (c x)"), start=True, stop=True)
                e.matmul(ps[1][:, 0:R * NE], ones[:, :], one.rearrange("p c x -> p (c x)"), start=True, stop=True).then_inc(counted, 1)

            @block.vector
            def _(e):
                n = [0]

                def link(ins):
                    ins.then_inc(own, 1)
                    n[0] += 1
                    e.wait_ge(own, n[0])
                link(e.memset(keep[:, :, :], 1.0))
                link(e.memset(keep[:, :, 0:1], 0.0))
                e.wait_ge(counted, 1)
                link(e.tensor_copy(tot[:, :, :], ps[1][:, 0:R * NE].rearrange("p (c x) -> p x c", x=NE)))
                flat = lambda t: t[:, :, :].rearrange("p x c -> p (x c)")
                link(e.tensor_tensor_scan(flat(inc), flat(keep), flat(tot), 0.0, ALU.mult, ALU.add))
                link(e.tensor_scalar_add(cnt[:, :], inc[:, :, R - 1], float(P - 1)))
                link(e.tensor_copy(ci[:, :], cnt[:, :]))
                link(e.tensor_single_scalar(ti[:, :], ci[:, :], 7, ALU.arith_shift_right))
                link(e.tensor_copy(tf[:, :], ti[:, :]))
                link(e.tensor_tensor_scan(end[:, :], ones[:, 0:NE], tf[:, :], 0.0, ALU.mult, ALU.add))
                link(e.tensor_tensor(base[:, :], end[:, :], tf[:, :], ALU.subtract))
                link(e.tensor_tensor(inc[:, :, :], inc[:, :, :], tot[:, :, :], ALU.subtract))
                link(e.scalar_tensor_tensor(inc[:, :, :], base[:, :].unsqueeze(2).to_broadcast([P, NE, R]), float(P), inc[:, :, :],
                                            ALU.mult, ALU.add))
                link(e.tensor_tensor(off[:, :, :], ps[0][:, 0:R * NE].rearrange("p (c x) -> p c x", x=NE),
                                     inc[:, :, :].rearrange("p x c -> p c x"), ALU.add))
                link(e.tensor_tensor(off[:, :, :], off[:, :, :], one, ALU.mult))
                link(e.tensor_reduce(slot_f[:, :], off[:, :, :], AX.X, ALU.add))
                e.tensor_copy(k["slot"][:, :], slot_f[:, :]).then_inc(slots_ok, 1)
                link(e.tensor_scalar_add(end2[:, :], end[0:1, :], 2.0))
                link(e.tensor_tensor(full[:, :, :], end2[:, :].unsqueeze(1).to_broadcast([1, NXT, NE]),
                                     k["iota"][0:1, 0:NXT].unsqueeze(2).to_broadcast([1, NXT, NE]), ALU.is_le))
                link(e.tensor_reduce(tx[:, :], full[:, :, :], AX.X, ALU.add))
                link(e.tensor_scalar_min(tx7[:, :], tx[:, :], float(NE - 1)))
                link(e.tensor_single_scalar(k["at_w"][:, :], tx7[:, :], float(2 * HID), ALU.mult))
                link(e.tensor_single_scalar(k["at_b"][:, :], tx7[:, :], float(HID + D), ALU.mult))


def experts(nc, d, k):
    with ExitStack() as ctx:
        m = Mem(nc, ctx, "experts")
        xg, xt, y = m.sb("xg", [P, 2, D]), m.sb("xt", [P, 2, D]), m.sb("y", [P, 2, D])
        hb, H, HT = m.sb("hb", [P, 2, HID]), m.sb("H", [P, 2, HID]), m.sb("HT", [P, 2, HID])
        ps_t, ps_h, ps_r, ps_y = ([m.ps(f"{n}{i}", [P, 512]) for i in range(2)] for n in ("ps_t", "ps_h", "ps_r", "ps_y"))
        t_ps, xt_ok, h_ps, hb_ok, g_ok, r_ps, ht_ok, y_ps, y_ok = (m.sem(n) for n in (
            "t_ps", "xt_ok", "h_ps", "hb_ok", "g_ok", "r_ps", "ht_ok", "y_ps", "y_ok"))
        loaded = [m.sem(f"loaded{i}") for i in range(2)]
        stored = [m.sem(f"stored{i}") for i in range(2)]
        W1 = k["W1"][:, :, :, :].rearrange("p x c h -> p (x c h)")
        W2 = k["W2"][:, :, :, :].rearrange("p x c h -> p (x c h)")
        gb = k["gb"]
        fixed = lambda i: isinstance(i, int)
        dram = lambda t, i: (t[i, :, :] if fixed(i) else t[bass.ds(i, 1), :, :].rearrange("a p c -> (a p) c"))

        def expert_values(e, tab, at, n, top):
            return nc.values_load_multi_w_load_instructions(
                cols(k[tab][0:1, :], at, n), engines=(e.engine,), min_val=0, max_val=top,
                skip_runtime_bounds_check_because="an expert's number times its weights, from a minimum with the last one")[1]
        with nc.Block() as block:
            @block.sync
            def _(e):
                t = d["xg"].rearrange("(n p) c -> n p c", p=P)

                def body(i, j, it):
                    wait(e, t_ps, i - 1)
                    e.dma_start(xg[:, j, :], dram(t, i)).then_inc(loaded[j], 16)
                turns(body, NX, first=2)(e)

            @block.gpsimd
            def _(e):
                t = d["yg"].rearrange("(n p) c -> n p c", p=P)

                def body(i, j, it):
                    e.wait_ge(y_ok, i + 1)
                    e.dma_start(dram(t, i), y[:, j, :]).then_inc(stored[j], 16)
                turns(body, NX, first=2)(e)
                e.wait_ge(stored[0], 16 * (NX - NX // 2))
                e.wait_ge(stored[1], 16 * (NX // 2))

            @block.tensor
            def _(e):
                e.wait_ge(k["w_in"], 48)
                v = {}

                def inputs(i, j, it):
                    e.wait_ge(loaded[j], 16 * (it + 1))
                    wait(e, xt_ok, i - 1)
                    for c in range(2):
                        x = e.transpose(ps_t[j][:, c * P:(c + 1) * P], xg[:, j, c * P:(c + 1) * P], k["ident"][:, :])
                    x.then_inc(t_ps, 1)

                def up(i, j, at):
                    e.wait_ge(xt_ok, i + 1)
                    wait(e, hb_ok, i - 1)
                    for c in range(2):
                        x = e.matmul(ps_h[j][:, :], xt[:, j, c * P:(c + 1) * P], cols(W1, at + c * HID, HID), start=c == 0, stop=c == 1)
                    x.then_inc(h_ps, 1)

                def turn(i, j):
                    e.wait_ge(g_ok, i + 1)
                    wait(e, ht_ok, i - 1)
                    for c in range(HC):
                        x = e.transpose(ps_r[j][:, c * P:(c + 1) * P], H[:, j, c * P:(c + 1) * P], k["ident"][:, :])
                    x.then_inc(r_ps, 1)

                def down(i, j, at):
                    e.wait_ge(ht_ok, i + 1)
                    wait(e, y_ok, i - 1)
                    for c in range(HC):
                        x = e.matmul(ps_y[j][:, 0:D], HT[:, j, c * P:(c + 1) * P], cols(W2, at + c * D, D), start=c == 0, stop=c == HC - 1)
                    x.then_inc(y_ps, 1)

                def body(i, j, it):
                    if j == 0:
                        v["w"] = expert_values(e, "at_w", i, 4, (NE - 1) * 2 * HID)
                    if not (fixed(i) and i == NX - 1):
                        inputs(i + 1, 1 - j, it + j)
                    up(i, j, v["w"][2 + j])
                    if not (fixed(i) and i < 2):
                        down(i - 2, j, v["w"][j])
                    if not (fixed(i) and i < 1):
                        turn(i - 1, 1 - j)
                inputs(0, 0, 0)
                turns(body, NX, first=2)(e)
                last = NX - 1
                down(last - 1, 1, v["w"][1])
                turn(last, 0)
                down(last, 0, v["w"][2])

            @block.vector
            def _(e):
                def norm(i, j):
                    e.wait_ge(t_ps, i + 1)
                    wait(e, h_ps, i - 1)
                    for c in range(2):
                        x = e.tensor_scalar(xt[:, j, c * P:(c + 1) * P], ps_t[j][:, c * P:(c + 1) * P], gb[:, 0, c:c + 1],
                                            gb[:, 1, c:c + 1], ALU.mult, ALU.add)
                    x.then_inc(xt_ok, 1)
                def out(i, j, it, at):
                    e.wait_ge(y_ps, i + 1)
                    wait(e, stored[j], 16 * it)
                    e.tensor_tensor(y[:, j, :], ps_y[j][:, 0:D], cols(k["b1b2"], at + HID, D), ALU.add).then_inc(y_ok, 1)
                v = {}

                def body(i, j, it):
                    if j == 0:
                        v["b"] = expert_values(e, "at_b", i, 4, (NE - 1) * (HID + D))
                    if not (fixed(i) and i == NX - 1):
                        norm(i + 1, 1 - j)
                    e.wait_ge(h_ps, i + 1)
                    wait(e, g_ok, i - 1)
                    e.tensor_tensor(hb[:, j, :], ps_h[j][:, :], cols(k["b1b2"], v["b"][2 + j], HID), ALU.add).then_inc(hb_ok, 1)
                    if not (fixed(i) and i < 2):
                        out(i - 2, j, it - 1, v["b"][j])
                e.wait_ge(k["w_in"], 48)
                norm(0, 0)
                turns(body, NX, first=2)(e)
                last = NX - 1
                out(last - 1, 1, (last - 1) // 2, v["b"][1])
                out(last, 0, last // 2, v["b"][2])

            @block.scalar
            def _(e):
                def turned(i, j):
                    e.wait_ge(r_ps, i + 1)
                    wait(e, y_ps, i - 1)
                    e.activation(HT[:, j, :], ps_r[j][:, :], ACT.Copy).then_inc(ht_ok, 1)

                def body(i, j, it):
                    e.wait_ge(hb_ok, i + 1)
                    wait(e, r_ps, i - 1)
                    e.activation(H[:, j, :], hb[:, j, :], ACT.Gelu).then_inc(g_ok, 1)
                    if not (fixed(i) and i < 1):
                        turned(i - 1, 1 - j)
                turns(body, NX, first=2)(e)
                turned(NX - 1, 0)


def combine(nc, d, k):
    R, NBUF = 2 * NT, 8
    with ExitStack() as ctx:
        m = Mem(nc, ctx, "comb")
        Y = m.sb("Y", [P, NBUF, D])
        landed = [m.sem(f"landed{i}") for i in range(NBUF)]
        added = m.sem("added")
        with nc.Block() as block:
            @block.gpsimd
            def _(e):
                for c in range(R):
                    wait(e, added, c - NBUF + 1)
                    e.indirect_dma_start(out=Y[:, c % NBUF, :], out_offset=None, in_=d["yg"],
                                         in_offset=bass.IndirectOffsetOnAxis(ap=k["slot"][:, c:c + 1], axis=0)
                                         ).then_inc(landed[c % NBUF], 16)

            @block.vector
            def _(e):
                for c in range(R):
                    e.wait_ge(landed[c % NBUF], 16 * (c // NBUF + 1))
                    wait(e, added, c - NT + 1)
                    X = k["X"][:, c % NT, :]
                    e.scalar_tensor_tensor(X, Y[:, c % NBUF, :], k["w"][:, c:c + 1], X, ALU.mult, ALU.add).then_inc(added, 1)


def write_x(nc, d, k):
    with ExitStack() as ctx:
        done = Mem(nc, ctx, "out").sem("done")
        block = ctx.enter_context(nc.Block())

        @block.sync
        def _(e):
            full = NODES // P
            e.dma_start(d["out"][0:full * P, :].rearrange("(n p) c -> p n c", p=P), k["X"][:, 0:full, :]).then_inc(done, 16)
            e.dma_start(d["out"][full * P:NODES, :], k["X"][0:NODES - full * P, full, :]).then_inc(done, 16)
            e.wait_ge(done, 32)


def add_acc0(nc, k):
    with ExitStack() as ctx:
        s = Mem(nc, ctx, "add0").sem("s")
        block = ctx.enter_context(nc.Block())

        @block.vector
        def _(e):
            X, acc = k["X"], k["acc0"]
            e.tensor_tensor(X[:, :, 0:64], X[:, :, 0:64], acc[:, :, 0:64], ALU.add)
            for m in range(3):
                e.tensor_tensor(X[:, :, 64 + m:256:3], X[:, :, 64 + m:256:3], acc[:, :, 64 + 64 * m:128 + 64 * m], ALU.add)
            e.engine_nop().then_inc(s, 1)


def build(nc, d, stop=99):
    with ExitStack() as ctx:
        m = Mem(nc, ctx, "k")
        k = {}
        for name, shape, dt in (("X", [P, NT, D], F32), ("iota", [P, 512], F32), ("ident", [P, P], F32),
                                ("dst_f", [P, ET], F32), ("src_i", [P, ET], I32), ("dst_i", [P, ET], I32),
                                ("walk_n", [1, 512], I32), ("walk_slot", [1, 512], I32), ("walk_q", [1, (SB + 1) * 2 * GT], I32),
                                ("dstep", [P, 512], F32),
                                 ("mv", [P, NT, 2], F32), ("rstd", [P, NT], F32)):
            k[name] = m.sb(name, shape, dt)
        k["mvf"] = k["mv"][:, :, :].rearrange("p n a -> p (n a)")
        with ExitStack() as c0:
            m0 = Mem(nc, c0, "l0")
            for name, shape in (("r", [P, ET, 3]), ("s2", [P, ET]), ("WH", [P, 128]), ("WO", [P, 128]), ("WQ", [64, 64]),
                                ("LSC2", [P, 64]), ("blockww", [P, P]), ("attr", [P, ET, 3])):
                k[name] = m0.sb(name, shape)
            edges_in(nc, d, k)
            setup(nc, d, k)
            moments(nc, k, "mom0")
            nodes0(nc, d, k)
            if stop > 0:
                k["acc0"] = m0.sb("acc0", [P, NT, A])
                edges0(nc, d, k)
                add_acc0(nc, k)
        if stop > 1:
            moments(nc, k, "mom1")
            lns(nc, d, k)
        if stop > 2:
            k["w_in"], k["zeroed"] = m.sem("w_in"), m.sem("zeroed")
            k["zeros"] = m.sb("zeros", [P, D])
            moments(nc, k, "mom2")
            with ExitStack() as c1:
                m1 = Mem(nc, c1, "l1")
                k["S"] = m1.sb("S", [P, ET * HEADS])
                with ExitStack() as c2:
                    k["K"] = Mem(nc, c2, "l1k").sb("K", [P, NT, A])
                    qkv(nc, d, k)
                    scores(nc, d, k)
                softmax_shift(nc, d, k)
                k["acc1"] = m1.sb("acc1", [P, NT, A])
                aggregate1(nc, d, k)
                add_acc1(nc, k)
        if stop > 3:
            moments(nc, k, "mom3")
            k["W1"] = m.sb("W1", [P, NE, 2, HID])
            k["W2"] = m.sb("W2", [P, NE, HC, D])
            k["b1b2"] = m.sb("b1b2", [P, NE * (HID + D)])
            k["gb"] = m.sb("gb", [P, 2, 2])
            k["w"] = m.sb("w", [P, 2 * NT])
            k["slot"] = m.sb("slot", [P, 2 * NT], I32)
            k["at_w"], k["at_b"] = m.sb("at_w", [1, NXT], I32), m.sb("at_b", [1, NXT], I32)
            with ExitStack() as c2:
                m2 = Mem(nc, c2, "nodes")
                k["XN"] = m2.sb("XN", [P, NT, D])
                k["one"] = m2.sb("one", [P, 2, NT, NE])
                route(nc, d, k)
                dispatch(nc, d, k)
            experts(nc, d, k)
            combine(nc, d, k)
        write_x(nc, d, k)


def kernel(**a):
    import numpy as np
    import concourse.bacc as bacc
    from concourse.bass_utils import run_bass_kernel_spmd

    nc = bacc.Bacc("TRN2", target_bir_lowering=False, num_devices=1)
    f = {n: np.ascontiguousarray(v) for n, v in a.items()}
    g = lambda n: f["L0_gnn_" + n]
    pad = EPAD - EDGES
    src = np.pad(f["src"], (0, pad))
    dst = np.pad(f["dst"], (0, pad), constant_values=NPAD - 1)
    attr = np.pad(f["edge_attr_3"], ((0, pad), (0, 0)))
    arrays = {
        "x": np.pad(f["x"], ((0, NPAD - NODES), (0, 0))),
        "src_pt": src.reshape(ET, P).T, "dst_pt": dst.reshape(ET, P).T,
        "dst_flat": np.pad(dst, (0, P), constant_values=NPAD - 1)[None],
        "attr_pt": attr.reshape(ET, P, 3).transpose(1, 0, 2),
        "ls0T": g("lin_src_w0").T, "ls1T": g("lin_src_w1").T,
        "t00": g("tp1_w00"), "t11": g("tp1_w11"), "t01": g("tp1_w01"), "t10": g("tp1_w10"),
        "lh0": g("lin_hidden_w0"), "lh1": g("lin_hidden_w1"),
        "u00": g("tp2_w00"), "u11": g("tp2_w11"), "u01": g("tp2_w01"), "u10": g("tp2_w10"),
        "lsc": g("lin_scalar_w"),
        "lnsT": f["L0_ffn_weight"].T, "lns_b": f["L0_ffn_bias"].reshape(1, D),
        "wqkv": np.concatenate([f["L1_gnn_Wq"], f["L1_gnn_Wk"], f["L1_gnn_Wv"]], 1),
        "bqkv": np.concatenate([f["L1_gnn_bq"], f["L1_gnn_bk"], f["L1_gnn_bv"]])[None],
        "gamma": f["L1_ffn_gamma"].reshape(2, P).T, "beta": f["L1_ffn_beta"].reshape(2, P).T,
        "Wr": f["L1_ffn_Wr"], "br": f["L1_ffn_br"][None],
        "W1": f["L1_ffn_W1"], "b1b2": np.concatenate([f["L1_ffn_b1"], f["L1_ffn_b2"]], 1).reshape(1, -1),
        "W2": f["L1_ffn_W2"],
    }
    arrays = {n: np.ascontiguousarray(v) for n, v in arrays.items()}
    d = {n: nc.dram_tensor("in_" + n, v.shape, mybir.dt.from_np(v.dtype), kind="ExternalInput").ap()
         for n, v in arrays.items()}
    d["sorted"] = nc.dram_tensor("sorted", (EPAD, 8), I32, kind="Internal").ap()
    d["tab0"] = nc.dram_tensor("tab0", (NPAD, T0W), F32, kind="Internal").ap()
    for n in ("qtab", "vtab"):
        d[n] = nc.dram_tensor(n, (NPAD, D), F32, kind="Internal").ap()
    for n in ("xg", "yg"):
        d[n] = nc.dram_tensor(n, (NX * P, D), F32, kind="Internal").ap()
    d["out"] = nc.dram_tensor("out_x", (NODES, D), F32, kind="ExternalOutput").ap()
    build(nc, d, **OPTIONS)
    r = run_bass_kernel_spmd(nc, [{"in_" + n: v for n, v in arrays.items()}], core_ids=[0])
    return r.results[0]["out_x"]


OPTIONS = {}
```
